# Optimizing a Trainium2 kernel written in Bass

```python
import numpy as np
import jax
import jax.numpy as jnp

def _softmax(x, axis=-1):
    return jax.nn.softmax(x, axis=axis)

def _gelu(x):
    return jax.nn.gelu(x, approximate=True)

def _silu(x):
    return jax.nn.silu(x)

def _sigmoid(x):
    return jax.nn.sigmoid(x)

def _layernorm(x, axis=-1, eps=1e-05):
    m = jnp.mean(x, axis=axis, keepdims=True)
    v = jnp.var(x, axis=axis, keepdims=True)
    return (x - m) / jnp.sqrt(v + eps)

def _scatter_add(tgt, idx, src, axis=0):
    return tgt.at[idx].add(src)

def _segment_sum(src, seg, n):
    return jax.ops.segment_sum(src, seg, n)
kernel_name = 'mk_vit_tower_cls_d1_tok_img256_r4_7a7680'

def setup_inputs(seed: int=0):
    np.random.seed(seed)
    _w = jnp.asarray

    def _rec_inputs():
        import jax
        import jax.numpy as jnp
        _rk = jax.random.key(seed)
        x = 7.22013e-05 + 1.00017 * jax.random.normal(jax.random.fold_in(_rk, 1), (8, 64, 64, 64), jnp.float32)
        cls_tok = 0.02 * jax.random.normal(jax.random.fold_in(_rk, 5), (1, 1, 64), jnp.float32)
        return (x, cls_tok)
    x, cls_tok = _rec_inputs()

    def _L0_tok_setup():
        import jax, jax.numpy as jnp
        import numpy as np
        K = 3
        PAD = (K - 1) // 2
        BN_EPS = 1e-05

        def _unfold(x):
            b, c, h, w = x.shape
            xp = jnp.pad(x, ((0, 0), (0, 0), (PAD, PAD), (PAD, PAD)))
            shifts = [xp[:, :, i:i + h, j:j + w] for i in range(K) for j in range(K)]
            return jnp.stack(shifts, axis=2)
        key = jax.random.key(seed)
        ks = jax.random.split(key, 4)
        b, c, h, w = (8, 64, 64, 64)
        cr = c // 4
        x = jax.random.normal(ks[0], (b, c, h, w), dtype=jnp.float32)
        conv1_w = jax.random.normal(ks[1], (cr, c), dtype=jnp.float32) * (1.0 / np.sqrt(c))
        conv1_b = jnp.zeros((cr,), dtype=jnp.float32)
        bn_gamma = jnp.ones((cr,), dtype=jnp.float32)
        bn_beta = jnp.zeros((cr,), dtype=jnp.float32)
        bn_mean = jnp.zeros((cr,), dtype=jnp.float32)
        bn_var = jnp.ones((cr,), dtype=jnp.float32)
        conv2_w = jax.random.normal(ks[2], (K * K, cr), dtype=jnp.float32) * (1.0 / np.sqrt(cr))
        conv2_b = jnp.zeros((K * K,), dtype=jnp.float32)
        return {'x': x, 'conv1_w': conv1_w, 'conv1_b': conv1_b, 'bn_gamma': bn_gamma, 'bn_beta': bn_beta, 'bn_mean': bn_mean, 'bn_var': bn_var, 'conv2_w': conv2_w, 'conv2_b': conv2_b}
    _L0_tok_all = _L0_tok_setup()
    _L0_tok_in = {k: v for k, v in _L0_tok_all.items() if k in ('conv1_w', 'conv1_b', 'bn_gamma', 'bn_beta', 'bn_mean', 'bn_var', 'conv2_w', 'conv2_b')}
    del _L0_tok_all

    def _L0_attn_setup():
        import jax, jax.numpy as jnp
        import numpy as np
        GAMMA = 0.96875
        SCALE_BASE = 512.0

        def xpos_rope(x, downscale=False):
            B, S, D = x.shape
            half = D // 2
            inv_freq = 1.0 / 10000.0 ** (jnp.arange(0, D, 2, dtype=jnp.float32) / D)
            pos = jnp.arange(S, dtype=jnp.float32)
            ang = pos[:, None] * inv_freq[None, :]
            sin, cos = (jnp.sin(ang), jnp.cos(ang))
            base = (jnp.arange(0, D, 2, dtype=jnp.float32) + 0.4 * D) / (1.4 * D)
            scale = base[None, :] ** (pos[:, None] / SCALE_BASE)
            if downscale:
                scale = 1.0 / scale
            x1 = x[..., 0::2]
            x2 = x[..., 1::2]
            r1 = (x1 * cos - x2 * sin) * scale
            r2 = (x1 * sin + x2 * cos) * scale
            out = jnp.stack([r1, r2], axis=-1).reshape(B, S, D)
            return out

        def get_D(gamma, seq_len):
            n = jnp.arange(seq_len, dtype=jnp.float32)
            diff = n[:, None] - n[None, :]
            mask = diff >= 0
            D = jnp.where(mask, gamma ** jnp.where(mask, diff, 0.0), 0.0)
            return D

        def _reference_tuple_inner(x, W_Q, W_K, W_V):
            S = x.shape[1]
            D = get_D(GAMMA, S)
            Q = xpos_rope(x @ W_Q, downscale=False)
            K = xpos_rope(x @ W_K, downscale=True)
            V = x @ W_V
            ret = jnp.einsum('bnd,bmd->bnm', Q, K) * D[None, :, :]
            out = jnp.einsum('bnm,bmv->bnv', ret, V)
            return (out, ret)
        key = jax.random.key(seed)
        k1, k2, k3, k4 = jax.random.split(key, 4)
        B, S, d_model, d_k, d_v = (8, 1024, 64, 64, 64)
        x = jax.random.normal(k1, (B, S, d_model), dtype=jnp.float32)
        W_Q = jax.random.normal(k2, (d_model, d_k), dtype=jnp.float32) / d_model
        W_K = jax.random.normal(k3, (d_model, d_k), dtype=jnp.float32) / d_model
        W_V = jax.random.normal(k4, (d_model, d_v), dtype=jnp.float32) / d_model
        return {'x': x, 'W_Q': W_Q, 'W_K': W_K, 'W_V': W_V}
    _L0_attn_all = _L0_attn_setup()
    _L0_attn_in = {k: v for k, v in _L0_attn_all.items() if k in ('W_Q', 'W_K', 'W_V')}
    del _L0_attn_all

    def _L0_ffn_setup():
        import jax, jax.numpy as jnp
        import numpy as np
        B, S, D = (8, 1024, 64)
        H = 4 * D
        CAPACITY = 0.5
        key = jax.random.key(seed)
        ks = jax.random.split(key, 6)
        x = jax.random.normal(ks[0], (B, S, D), dtype=jnp.float32)
        attention_mask = jnp.zeros((B, 1, 1, S), dtype=jnp.float32)
        wr = jax.random.normal(ks[1], (D, 1), dtype=jnp.float32) * 0.02
        br = jnp.zeros((1,), dtype=jnp.float32)
        w1 = jax.random.normal(ks[2], (D, H), dtype=jnp.float32) * 0.02
        b1 = jnp.zeros((H,), dtype=jnp.float32)
        w2 = jax.random.normal(ks[3], (H, D), dtype=jnp.float32) * 0.02
        b2 = jnp.zeros((D,), dtype=jnp.float32)
        return {'x': x, 'attention_mask': attention_mask, 'wr': wr, 'br': br, 'w1': w1, 'b1': b1, 'w2': w2, 'b2': b2}
    _L0_ffn_all = _L0_ffn_setup()
    _L0_ffn_in = {k: v for k, v in _L0_ffn_all.items() if k in ('attention_mask', 'wr', 'br', 'w1', 'b1', 'w2', 'b2')}
    del _L0_ffn_all
    return {'x': x, 'cls_tok': cls_tok, 'L0_tok_conv1_w': _L0_tok_in['conv1_w'], 'L0_tok_conv1_b': _L0_tok_in['conv1_b'], 'L0_tok_bn_gamma': _L0_tok_in['bn_gamma'], 'L0_tok_bn_beta': _L0_tok_in['bn_beta'], 'L0_tok_bn_mean': _L0_tok_in['bn_mean'], 'L0_tok_bn_var': _L0_tok_in['bn_var'], 'L0_tok_conv2_w': _L0_tok_in['conv2_w'], 'L0_tok_conv2_b': _L0_tok_in['conv2_b'], 'L0_attn_W_Q': _L0_attn_in['W_Q'], 'L0_attn_W_K': _L0_attn_in['W_K'], 'L0_attn_W_V': _L0_attn_in['W_V'], 'L0_ffn_attention_mask': _L0_ffn_in['attention_mask'], 'L0_ffn_wr': _L0_ffn_in['wr'], 'L0_ffn_br': _L0_ffn_in['br'], 'L0_ffn_w1': _L0_ffn_in['w1'], 'L0_ffn_b1': _L0_ffn_in['b1'], 'L0_ffn_w2': _L0_ffn_in['w2'], 'L0_ffn_b2': _L0_ffn_in['b2']}

def reference(x, cls_tok, L0_tok_conv1_w, L0_tok_conv1_b, L0_tok_bn_gamma, L0_tok_bn_beta, L0_tok_bn_mean, L0_tok_bn_var, L0_tok_conv2_w, L0_tok_conv2_b, L0_attn_W_Q, L0_attn_W_K, L0_attn_W_V, L0_ffn_attention_mask, L0_ffn_wr, L0_ffn_br, L0_ffn_w1, L0_ffn_b1, L0_ffn_w2, L0_ffn_b2):
    import jax
    import jax.numpy as jnp

    def _L0_tok_ref(x, conv1_w, conv1_b, bn_gamma, bn_beta, bn_mean, bn_var, conv2_w, conv2_b):
        import jax, jax.numpy as jnp
        import numpy as np
        K = 3
        PAD = (K - 1) // 2
        BN_EPS = 1e-05

        def _unfold(x):
            b, c, h, w = x.shape
            xp = jnp.pad(x, ((0, 0), (0, 0), (PAD, PAD), (PAD, PAD)))
            shifts = [xp[:, :, i:i + h, j:j + w] for i in range(K) for j in range(K)]
            return jnp.stack(shifts, axis=2)
        b, c, h, w = x.shape
        y = jnp.einsum('oc,bchw->bohw', conv1_w, x) + conv1_b[None, :, None, None]
        y = (y - bn_mean[None, :, None, None]) * (bn_gamma[None, :, None, None] * jax.lax.rsqrt(bn_var + BN_EPS)[None, :, None, None]) + bn_beta[None, :, None, None]
        y = jax.nn.relu(y)
        wdyn = jnp.einsum('ok,bkhw->bohw', conv2_w, y) + conv2_b[None, :, None, None]
        patches = _unfold(x)
        out = jnp.einsum('bckhw,bkhw->bchw', patches, wdyn)
        return out.reshape(b, h * w, c)

    def _L0_attn_ref(x, W_Q, W_K, W_V):
        import jax, jax.numpy as jnp
        import numpy as np
        GAMMA = 0.96875
        SCALE_BASE = 512.0

        def xpos_rope(x, downscale=False):
            B, S, D = x.shape
            half = D // 2
            inv_freq = 1.0 / 10000.0 ** (jnp.arange(0, D, 2, dtype=jnp.float32) / D)
            pos = jnp.arange(S, dtype=jnp.float32)
            ang = pos[:, None] * inv_freq[None, :]
            sin, cos = (jnp.sin(ang), jnp.cos(ang))
            base = (jnp.arange(0, D, 2, dtype=jnp.float32) + 0.4 * D) / (1.4 * D)
            scale = base[None, :] ** (pos[:, None] / SCALE_BASE)
            if downscale:
                scale = 1.0 / scale
            x1 = x[..., 0::2]
            x2 = x[..., 1::2]
            r1 = (x1 * cos - x2 * sin) * scale
            r2 = (x1 * sin + x2 * cos) * scale
            out = jnp.stack([r1, r2], axis=-1).reshape(B, S, D)
            return out

        def get_D(gamma, seq_len):
            n = jnp.arange(seq_len, dtype=jnp.float32)
            diff = n[:, None] - n[None, :]
            mask = diff >= 0
            D = jnp.where(mask, gamma ** jnp.where(mask, diff, 0.0), 0.0)
            return D

        def _reference_tuple_inner(x, W_Q, W_K, W_V):
            S = x.shape[1]
            D = get_D(GAMMA, S)
            Q = xpos_rope(x @ W_Q, downscale=False)
            K = xpos_rope(x @ W_K, downscale=True)
            V = x @ W_V
            ret = jnp.einsum('bnd,bmd->bnm', Q, K) * D[None, :, :]
            out = jnp.einsum('bnm,bmv->bnv', ret, V)
            return (out, ret)
        return _reference_tuple_inner(x, W_Q, W_K, W_V)[0]

    def _L0_ffn_ref(x, attention_mask, wr, br, w1, b1, w2, b2):
        import jax, jax.numpy as jnp
        import numpy as np
        B, S, D = (8, 1024, 64)
        H = 4 * D
        CAPACITY = 0.5
        b, s, d = x.shape
        weights = (jnp.einsum('bsd,do->bso', x, wr) + br)[..., 0]
        k = max(1, int(CAPACITY * s))
        kk = k - 1 if k > 1 else 1
        _, idx = jax.lax.top_k(weights, k)
        sel_idx = idx[:, :kk]
        sel = jnp.take_along_axis(x, sel_idx[:, :, None], axis=1)
        h = jax.nn.gelu(jnp.einsum('bkd,dh->bkh', sel, w1) + b1)
        y = jnp.einsum('bkh,hd->bkd', h, w2) + b2
        w_sel = jnp.take_along_axis(weights, sel_idx, axis=1)
        y = y * w_sel[..., None]
        batch_idx = jnp.arange(b)[:, None]
        processed = jnp.zeros_like(x).at[batch_idx, sel_idx].set(y)
        return processed + x
    h = _L0_tok_ref(x, L0_tok_conv1_w, L0_tok_conv1_b, L0_tok_bn_gamma, L0_tok_bn_beta, L0_tok_bn_mean, L0_tok_bn_var, L0_tok_conv2_w, L0_tok_conv2_b)
    h = jnp.concatenate([jnp.broadcast_to(cls_tok, (h.shape[0], 1, h.shape[2])), h], axis=1)
    h = h + _L0_attn_ref(_layernorm(h, axis=-1), L0_attn_W_Q, L0_attn_W_K, L0_attn_W_V)
    h = h + _L0_ffn_ref(_layernorm(h, axis=-1), L0_ffn_attention_mask, L0_ffn_wr, L0_ffn_br, L0_ffn_w1, L0_ffn_b1, L0_ffn_w2, L0_ffn_b2)
    return h

_drawn_inputs = setup_inputs


def setup_inputs(seed=0):
    import zlib

    import numpy as np

    out = dict(_drawn_inputs(seed))
    spreads = {'L0_tok_conv1_b': (0.0, 0.1),
     'L0_tok_bn_gamma': (1.0, 0.2),
     'L0_tok_bn_beta': (0.0, 0.1),
     'L0_tok_bn_mean': (0.0, 0.1),
     'L0_tok_bn_var': (1.0, 0.2),
     'L0_tok_conv2_b': (0.0, 0.1),
     'L0_ffn_b1': (0.0, 0.8),
     'L0_ffn_b2': (0.0, 0.8)}
    factors = {'cls_tok': 8.0, 'L0_ffn_wr': 8.0, 'L0_ffn_w1': 8.0, 'L0_ffn_w2': 8.0}
    for name, (base, spread) in spreads.items():
        noise = np.random.default_rng([zlib.crc32(name.encode()), seed]).standard_normal(out[name].shape)
        drawn = base * np.exp(spread * noise) if base else spread * noise
        out[name] = jnp.asarray(drawn.astype(out[name].dtype))
    for name, factor in factors.items():
        out[name] = (out[name] * factor).astype(out[name].dtype)
    return out
```

```python
from contextlib import ExitStack

import concourse.bass as bass
import numpy as np
from concourse import mybir

B, C, H, W = 8, 64, 64, 64
NPAIR = B // 2
CR = C // 4
TAPS = 9
SEQ = C * H + 1
D = W
CH = C * H // 128
HID = 4 * D
GAMMA = 0.96875
SCALE_BASE = 512.0
EPS = 1e-5
TOPK = max(1, int(0.5 * SEQ)) - 1

HS, WS = 5, 16
WB = W // WS
NG = -(-H // HS)
PR, PC = HS + 2, WS + 2
YROW = CR + 1
ROWS_PER_CONV = 512 // W
NCONV = H // ROWS_PER_CONV
NSLOT = CH // 2
NFILL = CH // 4
NQ = CH // 4 * 2
COLS = CH + 1
VRING, QRING, PRING = 4, 3, 8

CONST = {}


def _layout():
    at = 0
    for name, n in (("ident", 128), ("cmask", 128), ("tri", 128), ("ones", 128), ("ymask", 64),
                    ("tmask", HS * WS), ("sel", 3 * PR * PC), ("spread", 128), ("valid", 2 * COLS),
                    ("onerow", 1)):
        CONST[name] = (at, at + n)
        at += n
    return at


NCONST = _layout()


def small_constants():
    c = np.zeros((128, NCONST), np.float32)

    def put(name, rows, a):
        s, e = CONST[name]
        c[:rows, s:e] = a.reshape(rows, e - s)

    i = np.arange(128)
    put("ident", 128, np.eye(128))
    put("cmask", 128, (i[:, None] <= i[None, :]) * GAMMA ** -128.0)
    put("tri", 128, (i[:, None] < i[None, :]) * 1.0)
    put("ones", 128, np.ones((128, 128)))
    ym = np.zeros((128, W))
    for u in range(2):
        for rw in range(3):
            r0 = 64 * u + rw * YROW
            ym[r0:r0 + YROW] = (np.arange(W) % WS % 3 == rw)
    put("ymask", 128, ym)
    tm = np.zeros((PR * PC, HS, WS))
    sel = np.zeros((27, 3, PR * PC))
    for r in range(PR):
        for s in range(PC):
            for h in range(HS):
                for w in range(WS):
                    tm[r * PC + s, h, w] = 0 <= r - h <= 2 and 0 <= s - w <= 2
            for rh in range(3):
                for rw in range(3):
                    sel[rw * TAPS + (r - rh) % 3 * 3 + (s - rw) % 3, rh, r * PC + s] = 1
    put("tmask", PR * PC, tm)
    put("sel", 27, sel)
    sp = np.zeros((CR, 128))
    one = np.zeros((128, 1))
    for u in range(2):
        for rw in range(3):
            for k in range(CR):
                sp[k, 64 * u + rw * YROW + k] = 1
            one[64 * u + rw * YROW + CR] = 1
    put("spread", CR, sp)
    put("onerow", 128, one)
    v = np.ones((128, 2, COLS))
    v[1:, :, 0] = 0
    put("valid", 128, v)
    return c


def position_tables():
    f = np.float32
    inv_freq = (f(1.0) / np.power(f(10000.0), np.arange(0, D, 2, dtype=f) / f(D))).astype(f)
    pos = (1 + np.arange(CH * 128)).astype(f)
    ang = (pos[:, None] * inv_freq[None, :]).astype(f).astype(np.float64)
    base = ((np.arange(0, D, 2, dtype=f) + f(0.4 * D)) / f(1.4 * D)).astype(np.float64)
    scale = base[None, :] ** (pos[:, None].astype(np.float64) / SCALE_BASE)
    step = (np.arange(CH * 128) % 128 + 1.0)[:, None]
    q = scale * GAMMA ** (step + 128)
    k = 1.0 / scale * GAMMA ** -step
    out = []
    for trig in (np.cos(ang), np.sin(ang)):
        t = np.stack([trig * q, trig * k], axis=1)
        out.append(t.reshape(CH, 128, 64).transpose(1, 0, 2))
    return np.ascontiguousarray(np.stack(out), dtype=np.float32)


def vit_tower(nc, x, cls_tok, conv1_w, conv1_b, bn_gamma, bn_beta, bn_mean, bn_var, conv2_w, conv2_b,
              W_Q, W_K, W_V, wr, br, w1, b1, w2, b2, consts, tables, out):
    fp32, i32, u32 = mybir.dt.float32, mybir.dt.int32, mybir.dt.uint32
    ALU, ACT, AX = mybir.AluOpType, mybir.ActivationFunctionType, mybir.AxisListType

    with ExitStack() as ctx:
        def sb(name, shape, dt=fp32):
            return ctx.enter_context(nc.sbuf_tensor(name, shape, dt))

        def sem(name):
            return ctx.enter_context(nc.semaphore(name))

        h_dram = nc.dram_tensor("h_scratch", [B, C * H * W], fp32, kind="Internal").ap()

        cst = sb("cst", [128, NCONST])

        def const(name, rows=128):
            s, e = CONST[name]
            return cst[0:rows, s:e]

        cos_t = sb("cos_t", [128, CH, 64])
        sin_t = sb("sin_t", [128, CH, 64])
        wqkv = sb("wqkv", [128, 3, D])
        wqk_bd = sb("wqk_bd", [128, 2, 2, 2, 32])
        wv_bd = sb("wv_bd", [128, 2, D])
        wrt = sb("wrt", [128, 1])
        wr_bd = sb("wr_bd", [128, 2])
        w1t = sb("w1t", [128, HID])
        w2t = sb("w2t", [128, 2, D])
        b1t = sb("b1t", [128, 2])
        b2t = sb("b2t", [128, D])
        brt = sb("brt", [128, 1])
        bn5 = sb("bn5", [CR, 5])
        c1w = sb("c1w", [CR, C])
        c2bd = sb("c2bd", [27, 128])
        bnp = sb("bnp", [128, 5])
        bns = sb("bns", [128, 4])
        w1_conv = sb("w1_conv", [128, 128])
        gen_w = sb("gen_w", [128, 3, PR * PC])
        half = sb("half", [128, CH])

        xblk = sb("xblk", [128, WB, H + 2, PC])
        scores = sb("scores", [128, 2, 512])
        y_raw = scores
        y3 = sb("y3", [128, H, W])
        patch = sb("patch", [128, 2, WB, 128])
        taps = sb("taps", [128, 2, 2, HS, W])
        strip = sb("strip", [128, 4, HS, W])

        X = sb("X", [128, 2, CH, D])
        xn = sb("xn", [128, CH, 2, D])
        base = sb("base", [128, 2, CH, D])
        yraw = sb("yraw", [128, 2, CH, D])
        xT = sb("xT", [128, CH, 128])
        sq = sb("sq", [128, CH, D])
        st = sb("st", [128, 5, CH])
        terms = sb("terms", [128, 4, 512])
        t1, t2 = terms[:, 0:2, :], terms[:, 2:4, :]
        qk = sb("qk", [128, 2, 512])
        V = sb("V", [128, VRING, 2, 128])
        QKT = sb("QKT", [128, QRING, 2, 2, 128])
        RT = scores[:, :, :].rearrange("p r (u c n) -> p r u c n", u=2, c=2)
        P = sb("P", [128, PRING, 2, D])
        P0 = sb("P0", [128, D])
        hid = terms[:, :, :].rearrange("p (k m) n -> p k m n", m=2)

        cl = sb("cl", [1, 832])
        crow, cxn, ctmp, cqkv, ck, ch2, cxn2, cy, cbase, czz = (cl[:, a:b] for a, b in (
            (0, 64), (64, 128), (128, 192), (192, 384), (384, 448), (448, 512), (512, 576), (576, 640),
            (640, 704), (704, 832)))
        cst1 = sb("cst1", [1, 8])
        ccol = sb("ccol", [128, 4])
        w_cls = sb("w_cls", [1, 1])

        wt = sb("wt", [128, 2, COLS])
        key = sb("key", [128, 2, 2, COLS], i32)
        hi = sb("hi", [128, 2, COLS])
        lo = sb("lo", [128, 2, COLS])
        cmp = sb("cmp", [128, 2, COLS])
        cmp2 = sb("cmp2", [128, 2, COLS])
        part = sb("part", [128, 2])
        cand = sb("cand", [128, 2])
        dlt = sb("dlt", [128, 2])
        need = sb("need", [128, 2])
        wsel = sb("wsel", [128, 2, COLS])
        rank = sb("rank", [128, 2, COLS])

        pa = ctx.enter_context(nc.psum_tensor("pa", [128, 2, 512], fp32))
        pv = ctx.enter_context(nc.psum_tensor("pv", [128, 512], fp32))
        pt = ctx.enter_context(nc.psum_tensor("pt", [128, 512], fp32))
        ps = ctx.enter_context(nc.psum_tensor("ps", [128, 4, 512], fp32))
        p_patch = (pv, pt)

        s_load, s_tab, s_x, s_xl, s_out = sem("weights_loaded"), sem("tables_loaded"), sem("image_loaded"), sem("tokens_loaded"), sem("stored")
        s_strip = [sem(f"strip_stored{n}") for n in range(4)]
        s_setup = sem("setup_step")
        s_pad, s_blk = sem("image_padding_zero"), sem("image_cut")
        s_memz = sem("weights_zeroed")
        s_conv, s_yraw, s_y3 = sem("conv1_done"), sem("relu_done"), sem("y3_ready")
        s_pt, s_patch = sem("patch_transposed"), sem("patch_ready")
        s_gen, s_taps = sem("taps_made"), sem("taps_masked")
        s_app, s_strd = sem("involution_done"), sem("strip_ready")
        s_sum, s_mean, s_cent, s_sq, s_ss, s_var, s_rstd, s_norm = (sem("ln_" + n) for n in (
            "sum", "mean", "centred", "squared", "square_sum", "variance", "rstd", "normed"))
        s_base = sem("base_ready")
        s_xt, s_xte = sem("tokens_transposed"), sem("xT_ready")
        s_qkv, s_rot, s_qk, s_v = sem("qkv_done"), sem("rotated"), sem("qk_ready"), sem("v_ready")
        s_tr, s_qkt, s_u, s_state = sem("qk_transposed"), sem("qkt_ready"), sem("kv_done"), sem("state_ready")
        s_sc, s_ret, s_o, s_h2 = sem("scores_done"), sem("ret_ready"), sem("retention_done"), sem("h2_ready")
        s_w, s_wt = sem("router_done"), sem("router_read")
        s_cmp, s_cnt, s_chain = sem("count_asked"), sem("count_done"), sem("router_step")
        s_hid, s_gelu, s_y, s_yev = sem("hidden_done"), sem("gelu_done"), sem("ffn_done"), sem("ffn_read")
        s_yb, s_mul, s_fin, s_cls = sem("ffn_biased"), sem("ffn_weighted"), sem("result_ready"), sem("cls_result_ready")

        counting = [s_x, s_xl, s_out, *s_strip, s_blk, s_conv, s_yraw, s_y3, s_pt, s_patch, s_gen, s_taps, s_app,
                    s_strd, s_sum, s_mean, s_cent, s_sq, s_ss, s_var, s_rstd, s_norm, s_base, s_xt, s_xte, s_qkv,
                    s_rot, s_qk, s_v, s_tr, s_qkt, s_u, s_state, s_sc, s_ret, s_o, s_h2, s_w, s_wt, s_cmp, s_cnt,
                    s_chain, s_hid, s_gelu, s_y, s_yev, s_yb, s_mul, s_fin, s_cls]

        def wait(eng, s, j, per_pair, n):
            reg, add = j
            n += add * per_pair
            if isinstance(reg, int):
                if reg * per_pair + n > 0:
                    eng.wait_ge(s, 1 + reg * per_pair + n)
            else:
                eng.wait_ge(s, reg * per_pair + (1 + max(n, 0)))

        def pair(j):
            return j[0] + j[1]

        def rows(g):
            return min(HS, H - HS * g)

        N_SETUP_LOADS = 16 * 34
        NREQ = 2 * 16 + 2
        NCHAIN = 119
        block = ctx.enter_context(nc.Block())

        def walk(eng, first, retention, involution, ffn):
            first()
            with eng.Fori(0, NPAIR - 1) as i:
                retention((i, 0))
                involution((i, 1))
                ffn((i, 0), True)
            retention((NPAIR - 1, 0))
            ffn((NPAIR - 1, 0), False)

        @block.sync
        def _(sp):
            loads = [0]

            def load(dst, src):
                loads[0] += 1
                sp.dma_start(dst, src).then_inc(s_load, 16)

            def load_image(j, parts=(0, 1)):
                wait(sp, s_ss, (j[0], j[1] - 1), 4, 2)
                for half_image in parts:
                    wait(sp, s_blk, j, 2, half_image)
                    src = x[bass.ds(pair(j) * 2, 2), :, H // 2 * half_image:H // 2 * (half_image + 1), :]
                    sp.dma_start(sq[:, :, :], src.rearrange("b c h w -> (b c) h w")).then_inc(s_x, 16)

            def store_strips(j):
                for g in range(NG):
                    nh = rows(g)
                    wait(sp, s_strd, j, NG, g + 1)
                    dst = h_dram[bass.ds(pair(j) * 2, 2), :].rearrange("b (c n) -> (b c) n", c=C)
                    sp.dma_start(dst[:, g * HS * W:(g * HS + nh) * W],
                                 strip[:, g % 4, 0:nh, :].rearrange("p h w -> p (h w)")).then_inc(s_strip[g % 4], 16)

            def load_tokens(j):
                for n in range(4):
                    per = 16 * len(range(n, NG, 4))
                    wait(sp, s_strip[n], j, per, per)
                wait(sp, s_base, j, 2, 0)
                for u in range(2):
                    src = h_dram[bass.ds(pair(j) * 2 + u, 1), :].rearrange("a (c l d) -> l (a c) d", l=128, d=D)
                    for c0 in range(0, CH, CH // 2):
                        sp.dma_start(X[:, u, c0:c0 + CH // 2, :], src[:, c0:c0 + CH // 2, :]).then_inc(s_xl, 16)

            def store_result(j):
                for u in range(2):
                    wait(sp, s_fin, j, 2, u + 1)
                    dst = out[bass.ds(pair(j) * 2 + u, 1), 1:SEQ, :].rearrange("a (c l) d -> l (a c) d", l=128)
                    sp.dma_start(dst, yraw[:, u, :, :]).then_inc(s_out, 16)

            load(cst[:, :], consts)
            load_image((0, 0), (0,))
            for n, a in enumerate((conv1_b, bn_mean, bn_gamma, bn_beta, bn_var)):
                load(bn5[:, n:n + 1], a.rearrange("(p a) -> p a", a=1))
            load(c1w[:, :], conv1_w)
            sp.wait_ge(s_memz, 1)
            for u in range(2):
                for rw in range(3):
                    r, c0 = slice(rw * TAPS, (rw + 1) * TAPS), 64 * u + rw * YROW
                    load(c2bd[r, c0:c0 + CR], conv2_w)
                    load(c2bd[r, c0 + CR:c0 + YROW], conv2_b.rearrange("(p a) -> p a", a=1))
            for u in range(2):
                hs = slice(64 * u, 64 * u + 64)
                for n, a in enumerate((W_Q, W_K, W_V)):
                    load(wqkv[hs, n, :], a)
                load(wrt[hs, :], wr)
                load(w1t[hs, :], w1)
            load(w2t[:, :, :], w2.rearrange("(m p) d -> p m d", m=2))
            with nc.allow_non_contiguous_dma("256 biases, once"):
                load(b1t[:, :], b1.rearrange("(m p) -> p m", m=2))
            load(b2t[:, :], b2.partition_broadcast(128))
            load(brt[:, :], br.partition_broadcast(128))
            load(crow, cls_tok[0, :, :])
            assert 16 * loads[0] == N_SETUP_LOADS
            load_image((0, 0), (1,))
            for n, tab in enumerate((cos_t, sin_t)):
                sp.dma_start(tab[:, :, :], tables[n, :, :, :]).then_inc(s_tab, 16)

            def first():
                store_strips((0, 0))
                load_tokens((0, 0))

            def ffn(j, more):
                if more:
                    load_tokens((j[0], j[1] + 1))
                store_result(j)

            def retention(j):
                if not isinstance(j[0], int):
                    load_image((j[0], j[1] + 1))

            walk(sp, first, retention, store_strips, ffn)
            wait(sp, s_out, (0, NPAIR), 64, 0)

        @block.gpsimd
        def _(pool):
            def y3_masks(j):
                for n in range(NCONV):
                    wait(pool, s_yraw, j, NCONV, n + 1)
                    r0 = n * ROWS_PER_CONV
                    nc.gpsimd.tensor_tensor(
                        y3[:, r0:r0 + ROWS_PER_CONV, :],
                        y_raw[:, n % 2, :].rearrange("p (h w) -> p h w", w=W),
                        const("ymask").unsqueeze(1).broadcast_to([128, ROWS_PER_CONV, W]),
                        ALU.mult).then_inc(s_y3, 1)

            def centre(j, kind, u):
                wait(pool, s_mean, j, 4, 2 * kind + u + 1)
                wait(pool, s_xt, j, 2 * NFILL, NFILL * kind)
                nc.gpsimd.tensor_tensor(xn[:, :, u, :], X[:, u, :, :],
                                        st[:, 1, :].unsqueeze(2).broadcast_to([128, CH, D]),
                                        ALU.subtract).then_inc(s_cent, 1)

            def normalise(j, kind, u):
                n = 2 * kind + u + 1
                wait(pool, s_var, j, 4, n)
                nc.gpsimd.tensor_tensor(st[:, 4, :], st[:, 3, :], half[:, :], ALU.pow).then_inc(s_rstd, 1)
                wait(pool, s_rstd, j, 4, n)
                nc.gpsimd.tensor_tensor(xn[:, :, u, :], xn[:, :, u, :],
                                        st[:, 4, :].unsqueeze(2).broadcast_to([128, CH, D]),
                                        ALU.mult).then_inc(s_norm, 1)

            def layer_norm(j, kind):
                for u in range(2):
                    centre(j, kind, u)
                    normalise(j, kind, u)

            for s in counting:
                pool.sem_inc(s, 1)
            nc.gpsimd.memset(xblk[:, :, :, :], 0.0).then_inc(s_pad, 1)
            nc.gpsimd.memset(c2bd[:, :], 0.0).then_inc(s_memz, 1)
            nc.gpsimd.memset(half[:, :], -0.5).then_inc(s_memz, 1)
            pool.wait_ge(s_memz, 2)
            pool.wait_ge(s_setup, 2)
            nc.gpsimd.tensor_tensor(bns[:, 1:2], bns[:, 0:1], half[:, 0:1], ALU.pow).then_inc(s_setup, 1)
            for n in (13, 27):
                pool.wait_ge(s_setup, n)
                nc.gpsimd.tensor_tensor(cst1[:, 3:4], cst1[:, 2:3], half[0:1, 0:1], ALU.pow).then_inc(s_setup, 1)

            def first():
                y3_masks((0, 0))
                layer_norm((0, 0), 0)

            def retention(j):
                for t in range(NSLOT):
                    wait(pool, s_rot, j, NSLOT, t + 1)
                    wait(pool, s_u, j, NSLOT, t - 1)
                    o, a, b = (v[:, t % 2, :].rearrange("p (f e n) -> p f e n", e=2, n=32) for v in (qk, t1, t2))
                    nc.gpsimd.tensor_tensor(o[:, :, 0, :], a[:, :, 0, :], b[:, :, 0, :], ALU.subtract)
                    nc.gpsimd.tensor_tensor(o[:, :, 1, :], a[:, :, 1, :], b[:, :, 1, :], ALU.add).then_inc(s_qk, 1)
                if isinstance(j[0], int) and j[0] == NPAIR - 1:
                    norm2(j)

            def norm2(j):
                layer_norm(j, 1)
                for u in range(2):
                    wait(pool, s_norm, j, 4, 2 + u + 1)
                    wait(pool, s_fin, j, 2, 0)
                    nc.gpsimd.tensor_tensor(base[:, u, :, :], X[:, u, :, :], xn[:, :, u, :],
                                            ALU.add).then_inc(s_base, 1)

            def involution(j):
                y3_masks(j)
                norm2((j[0], j[1] - 1))

            def ffn(j, more):
                if more:
                    layer_norm((j[0], j[1] + 1), 0)
                for u in range(2):
                    wait(pool, s_yev, j, NQ, NQ)
                    nc.gpsimd.tensor_tensor(yraw[:, u, :, :], yraw[:, u, :, :],
                                            b2t[:, :].unsqueeze(1).broadcast_to([128, CH, D]),
                                            ALU.add).then_inc(s_yb, 1)

            walk(pool, first, retention, involution, ffn)

        @block.scalar
        def _(act):
            def cut_image(j, n, b):
                if b == 0:
                    wait(act, s_app, j, NG, 0)
                    wait(act, s_x, j, 32, 16 * (n + 1))
                r0 = 1 + H // 2 * n
                first_col, last_col = max(WS * b - 1, 0), min(WS * b + WS + 1, W)
                d0 = first_col - (WS * b - 1)
                last = nc.scalar.activation(xblk[:, b, r0:r0 + H // 2, d0:d0 + last_col - first_col],
                                            sq[:, :, first_col:last_col], ACT.Copy)
                if b == WB - 1:
                    last.then_inc(s_blk, 1)

            def relus(j):
                for n in range(NCONV):
                    wait(act, s_conv, j, NCONV, n + 1)
                    wait(act, s_y3, j, NCONV, n - 1)
                    nc.scalar.activation(y_raw[:, n % 2, :], pa[:, n % 2, :], ACT.Relu,
                                         bias=bns[:, 3:4], scale=bns[:, 2:3]).then_inc(s_yraw, 1)

            def involution(j, norm2=True):
                relus(j)
                for g in range(NG + 1):
                    if norm2 and g in (3, 7):
                        square((j[0], j[1] - 1), 1, g // 7)
                    if g < NG:
                        K = (rows(g) + 2) * PC
                        wait(act, s_pt, j, NG, g + 1)
                        wait(act, s_app, j, NG, g - 1)
                        nc.scalar.activation(patch[0:K, g % 2, :, :].rearrange("p b c -> p (b c)"),
                                             p_patch[g % 2][0:K, :], ACT.Copy).then_inc(s_patch, 1)
                    if g >= 1:
                        q = g - 1
                        nh = rows(q)
                        wait(act, s_app, j, NG, q + 1)
                        wait(act, s_strip[q % 4], j, 16 * len(range(q % 4, NG, 4)), 16 * (q // 4))
                        nc.scalar.activation(strip[:, q % 4, 0:nh, :].rearrange("p h w -> p (h w)"),
                                             ps[:, 2 + q % 2, 0:nh * W], ACT.Copy).then_inc(s_strd, 1)

            def square(j, kind, u):
                wait(act, s_cent, j, 4, 2 * kind + u + 1)
                wait(act, s_blk, j, 2, 2 + 2 * kind * (not isinstance(j[0], int)))
                wait(act, s_ss, j, 4, 2 * kind + u)
                nc.scalar.activation(sq[:, :, :], xn[:, :, u, :], ACT.Square).then_inc(s_sq, 1)

            def read_transposes(j, kind):
                for n in range(NFILL):
                    wait(act, s_xt, j, 2 * NFILL, NFILL * kind + n + 1)
                    nc.scalar.activation(xT[:, 4 * n:4 * n + 4, :].rearrange("p c l -> p (c l)"),
                                         pa[:, n % 2, :], ACT.Copy).then_inc(s_xte, 1)

            def retention(j):
                read_transposes(j, 0)
                for k in range(NSLOT + 1):
                    if not isinstance(j[0], int) and k % 8 >= 2 and k % 8 < 2 + WB:
                        cut_image((j[0], j[1] + 1), k // 8, k % 8 - 2)
                    if k < NSLOT:
                        wait(act, s_qkv, j, NSLOT, k + 1)
                        wait(act, s_o, j, NSLOT, k - VRING + 1)
                        nc.scalar.activation(V[:, k % VRING, :, :].rearrange("p c d -> p (c d)"),
                                             pv[:, 0:256], ACT.Copy).then_inc(s_v, 1)
                    if k >= 1:
                        t = k - 1
                        wait(act, s_tr, j, NSLOT, t + 1)
                        wait(act, s_o, j, NSLOT, t - QRING + 1)
                        nc.scalar.activation(QKT[:, t % QRING, :, :, :].rearrange("p c a l -> p (c a l)"),
                                             pt[:, :], ACT.Copy).then_inc(s_qkt, 1)
                if isinstance(j[0], int) and j[0] == NPAIR - 1:
                    for u in range(2):
                        square(j, 1, u)

            def ffn(j, more):
                read_transposes(j, 1)
                for k in range(NQ + 1):
                    if k < NQ:
                        for m in range(2):
                            wait(act, s_hid, j, 2 * NQ, 2 * k + m + 1)
                            wait(act, s_y, j, NQ, k - 1)
                            nc.scalar.activation(hid[:, k % 2, m, :], ps[:, 2 * (k % 2) + m, :],
                                                 ACT.Gelu_apprx_tanh, bias=b1t[:, m:m + 1]).then_inc(s_gelu, 1)
                    if k >= 1:
                        q = k - 1
                        cg, u = q // 2, q % 2
                        wait(act, s_y, j, NQ, q + 1)
                        wait(act, s_out, j, 64, 0)
                        nc.scalar.activation(yraw[:, u, 4 * cg:4 * cg + 4, :].rearrange("p c d -> p (c d)"),
                                             pa[:, q % 2, 0:256], ACT.Copy).then_inc(s_yev, 1)
                    if more and k in (10, 13):
                        square((j[0], j[1] + 1), 0, 0 if k == 10 else 1)
                wait(act, s_cls, j, 1, 1)
                for u in range(2):
                    act.dma_start(out[bass.ds(pair(j) * 2 + u, 1), 0, :], czz[:, D * u:D * u + D]).then_inc(s_out, 16)

            act.wait_ge(s_pad, 1)
            for n in range(2):
                for b in range(WB):
                    cut_image((0, 0), n, b)
            act.wait_ge(s_load, N_SETUP_LOADS)
            act.wait_ge(s_setup, 32)
            for m in range(2):
                last = nc.scalar.activation(ccol[:, 2 + m:3 + m], pa[:, 0, 4 + m:5 + m],
                                            ACT.Gelu_apprx_tanh, bias=b1t[:, m:m + 1])
            last.then_inc(s_setup, 1)

            def first():
                involution((0, 0), norm2=False)
                for u in range(2):
                    square((0, 0), 0, u)

            walk(act, first, retention, involution, ffn)

        @block.vector
        def _(dve):
            def ln_mean(j, kind, u):
                n = 2 * kind + u
                if kind == 0:
                    wait(dve, s_xl, j, 64, 64)
                else:
                    wait(dve, s_h2, j, NSLOT, NSLOT)
                wait(dve, s_cent, j, 4, n)
                nc.vector.tensor_reduce(st[:, 0, :], X[:, u, :, :], AX.X, ALU.add).then_inc(s_sum, 1)
                wait(dve, s_sum, j, 4, n + 1)
                nc.vector.tensor_scalar(st[:, 1, :], st[:, 0, :], 1.0 / D, None, ALU.mult).then_inc(s_mean, 1)

            def ln_var(j, kind, u):
                n = 2 * kind + u
                wait(dve, s_sq, j, 4, n + 1)
                nc.vector.tensor_reduce(st[:, 2, :], sq[:, :, :], AX.X, ALU.add).then_inc(s_ss, 1)
                wait(dve, s_ss, j, 4, n + 1)
                wait(dve, s_rstd, j, 4, n)
                nc.vector.tensor_scalar(st[:, 3, :], st[:, 2, :], 1.0 / D, EPS, ALU.mult, ALU.add).then_inc(s_var, 1)

            def layer_norm(j, kind):
                for u in range(2):
                    ln_mean(j, kind, u)
                    ln_var(j, kind, u)

            def mask_taps(j, g, u):
                nh = rows(g)
                K = (nh + 2) * PC
                wait(dve, s_gen, j, 2 * NG, 2 * g + u + 1)
                wait(dve, s_app, j, NG, g - 1)
                shape = [K, nh, WB, WS]
                nc.vector.tensor_tensor(
                    taps[0:K, g % 2, u, 0:nh, :].rearrange("p h (b w) -> p h b w", w=WS),
                    ps[0:K, u, 0:nh * W].rearrange("p (h b w) -> p h b w", b=WB, w=WS),
                    const("tmask", K).rearrange("p (h w) -> p h w", w=WS)[:, 0:nh, :].unsqueeze(2).broadcast_to(shape),
                    ALU.mult).then_inc(s_taps, 1)

            def involution(j):
                for g in range(NG):
                    for u in range(2):
                        mask_taps(j, g, u)

            def after(n):
                dve.wait_ge(s_setup, n)

            dve.wait_ge(s_load, N_SETUP_LOADS)
            dve.wait_ge(s_memz, 2)
            nc.vector.memset(w1_conv[:, :], 0.0).then_inc(s_memz, 1)
            nc.vector.memset(wqk_bd[:, :, :, :, :], 0.0).then_inc(s_memz, 1)
            nc.vector.memset(wv_bd[:, :, :], 0.0).then_inc(s_memz, 1)
            nc.vector.memset(wr_bd[:, :], 0.0).then_inc(s_memz, 1)
            nc.vector.memset(wt[:, :, :], 0.0).then_inc(s_memz, 1)
            nc.vector.memset(P[:, :, :, :], 0.0).then_inc(s_memz, 1)
            dve.wait_ge(s_memz, 8)
            after(1)
            nc.vector.tensor_copy(bnp[:, :], pa[:, 0, 0:5])
            nc.vector.tensor_scalar(bns[:, 0:1], pa[:, 0, 4:5], EPS, None, ALU.add)
            for u in range(2):
                hs = slice(64 * u, 64 * u + 64)
                nc.vector.tensor_copy(w1_conv[hs, 64 * u:64 * u + 64], pa[hs, 1, 64 * u:64 * u + 64])
                for a in range(2):
                    nc.vector.tensor_copy(wqk_bd[hs, a, u, :, :],
                                          wqkv[hs, a, :].rearrange("p (j e) -> p e j", e=2))
                nc.vector.tensor_copy(wv_bd[hs, u, :], wqkv[hs, 2, :])
                nc.vector.tensor_copy(wr_bd[hs, u:u + 1], wrt[hs, :])
            nc.vector.tensor_copy(gen_w[:, :, :].rearrange("p r n -> p (r n)"), pv[:, 0:3 * PR * PC]).then_inc(s_setup, 1)
            chain = [(bns[:, 2:3], bnp[:, 2:3], bns[:, 1:2], ALU.mult),
                     (bns[:, 0:1], bnp[:, 0:1], bnp[:, 1:2], ALU.subtract),
                     (bns[:, 0:1], bns[:, 0:1], bns[:, 2:3], ALU.mult),
                     (bns[:, 0:1], bns[:, 0:1], bnp[:, 3:4], ALU.add),
                     (bns[:, 3:4], bns[:, 0:1], const("onerow"), ALU.add)]
            for n, (o, a, b, op) in enumerate(chain):
                after(3 + n)
                nc.vector.tensor_tensor(o, a, b, op).then_inc(s_setup, 1)

            def cls_norm(n, src, dst):
                after(n)
                nc.vector.tensor_reduce(cst1[:, 0:1], src, AX.X, ALU.add).then_inc(s_setup, 1)
                after(n + 1)
                nc.vector.tensor_scalar(cst1[:, 1:2], cst1[:, 0:1], 1.0 / D, None, ALU.mult).then_inc(s_setup, 1)
                after(n + 2)
                nc.vector.tensor_scalar(dst, src, cst1[:, 1:2], None, ALU.subtract).then_inc(s_setup, 1)
                after(n + 3)
                nc.vector.scalar_tensor_tensor(ctmp, dst, 1.0, dst, ALU.mult, ALU.mult,
                                               accum_out=cst1[:, 0:1]).then_inc(s_setup, 1)
                after(n + 4)
                nc.vector.tensor_scalar(cst1[:, 2:3], cst1[:, 0:1], 1.0 / D, EPS, ALU.mult, ALU.add).then_inc(s_setup, 1)
                after(n + 6)
                nc.vector.tensor_scalar(dst, dst, cst1[:, 3:4], None, ALU.mult).then_inc(s_setup, 1)

            cls_norm(8, crow, cxn)
            after(16)
            nc.vector.tensor_copy(ccol[0:64, 0:1], pa[0:64, 0, 0:1]).then_inc(s_setup, 1)
            after(18)
            nc.vector.tensor_copy(cqkv, pa[0:1, 0, 0:192])
            nc.vector.tensor_copy(ck.rearrange("p (e j) -> p e j", e=2),
                                  pa[0:1, 0, 64:128].rearrange("p (j e) -> p e j", e=2)).then_inc(s_setup, 1)
            after(19)
            nc.vector.scalar_tensor_tensor(ctmp, cqkv[:, 0:64], 1.0, cqkv[:, 64:128], ALU.mult, ALU.mult,
                                           accum_out=cst1[:, 4:5]).then_inc(s_setup, 1)
            after(21)
            nc.vector.tensor_scalar(P0[:, :], pa[:, 1, 0:64], GAMMA ** -128.0, None, ALU.mult)
            nc.vector.scalar_tensor_tensor(ch2, cqkv[:, 128:192], cst1[:, 4:5], crow,
                                           ALU.mult, ALU.add).then_inc(s_setup, 1)
            cls_norm(22, ch2, cxn2)
            after(30)
            nc.vector.tensor_copy(ccol[0:64, 1:2], pa[0:64, 0, 0:1])
            nc.vector.tensor_tensor(cbase, ch2, cxn2, ALU.add).then_inc(s_setup, 1)
            after(34)
            nc.vector.tensor_tensor(cy, pa[0:1, 0, 64:128], b2t[0:1, :], ALU.add)
            nc.vector.tensor_tensor(w_cls[:, :], pa[0:1, 1, 64:65], brt[0:1, :], ALU.add).then_inc(s_setup, 1)
            after(35)
            nc.vector.tensor_copy(wt[0:1, :, 0:1].rearrange("p u c -> p (u c)"),
                                  w_cls[:, :].broadcast_to([1, 2])).then_inc(s_setup, 1)
            after(36)

            def first():
                involution((0, 0))
                layer_norm((0, 0), 0)

            def rotate(j, t):
                ring = t % 2
                wait(dve, s_qkv, j, NSLOT, t + 1)
                wait(dve, s_qk, j, NSLOT, t - 1)
                ch = slice(2 * t, 2 * t + 2)

                def halves(a, e):
                    return a.rearrange("p (f u e n) -> p f u e n", f=4, u=2, e=2)[:, :, :, e, :]

                def table(a, n):
                    return a[:, ch, :].rearrange("p c (f n) -> p (c f) n", f=2).unsqueeze(2).broadcast_to([128, 4, n, 32])

                nc.vector.tensor_tensor(t1[:, ring, :].rearrange("p (f g n) -> p f g n", f=4, g=4),
                                        pa[:, ring, :].rearrange("p (f g n) -> p f g n", f=4, g=4),
                                        table(cos_t, 4), ALU.mult)
                nc.vector.tensor_tensor(halves(t2[:, ring, :], 0), halves(pa[:, ring, :], 1),
                                        table(sin_t, 2), ALU.mult)
                nc.vector.tensor_tensor(halves(t2[:, ring, :], 1), halves(pa[:, ring, :], 0),
                                        table(sin_t, 2), ALU.mult).then_inc(s_rot, 1)

            def states(j, t):
                wait(dve, s_u, j, NSLOT, t + 1)
                wait(dve, s_o, j, NSLOT, t - 3)
                for c in range(2):
                    ch = 2 * t + c
                    wait(dve, s_state, j, CH + 1, ch + 1)
                    for u in range(2):
                        r = slice(64 * u, 64 * u + 64)
                        last = nc.vector.scalar_tensor_tensor(P[r, ch % PRING, u, :], P[r, (ch - 1) % PRING, u, :],
                                                              GAMMA ** 128.0, ps[r, 3, 64 * c:64 * c + 64],
                                                              ALU.mult, ALU.add)
                    last.then_inc(s_state, 1)

            def mask_scores(j, t):
                wait(dve, s_sc, j, NSLOT, t + 1)
                wait(dve, s_o, j, NSLOT, t - 1)
                nc.vector.tensor_tensor(RT[:, t % 2, :, :, :],
                                        ps[:, 0:2, 0:256].rearrange("p u (c n) -> p u c n", c=2),
                                        const("cmask").unsqueeze(1).unsqueeze(1).broadcast_to([128, 2, 2, 128]),
                                        ALU.mult).then_inc(s_ret, 1)

            def add_residual(j, t):
                wait(dve, s_o, j, NSLOT, t + 1)
                xs = X[:, :, 2 * t:2 * t + 2, :]
                nc.vector.tensor_tensor(xs, ps[:, 2, 0:256].rearrange("p (c u d) -> p u c d", u=2, c=2), xs,
                                        ALU.add).then_inc(s_h2, 1)

            def retention(j):
                wait(dve, s_o, j, NSLOT, 0)
                for u in range(2):
                    r = slice(64 * u, 64 * u + 64)
                    last = nc.vector.tensor_copy(P[r, PRING - 1, u, :], P0[r, :])
                last.then_inc(s_state, 1)
                for k in range(NSLOT + 3):
                    if k < NSLOT:
                        rotate(j, k)
                    if 0 <= k - 1 < NSLOT:
                        states(j, k - 1)
                    if 0 <= k - 2 < NSLOT:
                        mask_scores(j, k - 2)
                    if 0 <= k - 3 < NSLOT:
                        add_residual(j, k - 3)
                if isinstance(j[0], int) and j[0] == NPAIR - 1:
                    layer_norm(j, 1)

            def involution_and_norm2(j):
                jn = (j[0], j[1] - 1)
                parts = {1: [(ln_mean, 0)], 5: [(ln_var, 0), (ln_mean, 1)], 9: [(ln_var, 1)]}
                for g in range(NG):
                    for u in range(2):
                        mask_taps(j, g, u)
                    for part_of, u in parts.get(g, []):
                        part_of(jn, 1, u)

            def ffn(j, more):
                n = [0]

                def link(ins):
                    n[0] += 1
                    ins.then_inc(s_chain, 1)
                    wait(dve, s_chain, j, NCHAIN, n[0])

                asked = [0]

                def total(op, vals, thr, dst):
                    link(nc.vector.tensor_tensor(dst[:, :, :], vals[:, :, :],
                                                 thr[:, :].unsqueeze(2).broadcast_to([128, 2, COLS]), op))
                    nc.vector.tensor_reduce(part[:, :], dst[:, :, :], AX.X, ALU.add).then_inc(s_cmp, 1)
                    asked[0] += 1

                def counted():
                    wait(dve, s_cnt, j, NREQ, asked[0])
                    return pt[:, 2 * (asked[0] % 2):2 * (asked[0] % 2) + 2]

                def search(vals):
                    for bit in range(15, -1, -1):
                        total(ALU.is_ge, vals, cand, cmp)
                        it = asked[0]
                        if more and it in (12, 16):
                            ln_mean((j[0], j[1] + 1), 0, it // 16)
                        if more and it in (24, 28):
                            ln_var((j[0], j[1] + 1), 0, it // 28)
                        got = counted()
                        link(nc.vector.tensor_scalar(dlt[:, :], got, float(TOPK), float(2 ** bit), ALU.is_ge, ALU.mult))
                        link(nc.vector.scalar_tensor_tensor(cand[:, :], dlt[:, :], -float(2 ** (bit - 1)) if bit else -1.0,
                                                            cand[:, :], ALU.add, ALU.add))

                wait(dve, s_w, j, 1, 1)
                link(nc.vector.tensor_scalar(wt[:, :, 1:COLS], pv[:, 0:2 * CH].rearrange("p (c u) -> p u c", u=2),
                                             brt[:, 0:1], None, ALU.add))
                bits = wt[:, :, :].bitcast(i32)
                k0, k1 = key[:, 0, :, :], key[:, 1, :, :]
                link(nc.vector.tensor_scalar(k0, bits, 31, -2 ** 31, ALU.arith_shift_right, ALU.bitwise_or))
                link(nc.vector.tensor_tensor(k1, k0, bits, ALU.bitwise_xor))
                link(nc.vector.tensor_scalar(k0.bitcast(u32), k1.bitcast(u32), 16, None, ALU.logical_shift_right))
                link(nc.vector.tensor_scalar(k1, k1, 65535, None, ALU.bitwise_and))
                valid = const("valid").rearrange("p (u c) -> p u c", u=2)
                link(nc.vector.scalar_tensor_tensor(hi[:, :, :], k0, 1.0, valid, ALU.add, ALU.mult))
                link(nc.vector.memset(cand[:, :], 32769.0))
                search(hi)
                bc = cand[:, :].unsqueeze(2).broadcast_to([128, 2, COLS])
                link(nc.vector.tensor_tensor(cmp[:, :, :], hi[:, :, :], bc, ALU.is_equal))
                link(nc.vector.tensor_tensor(cmp2[:, :, :], hi[:, :, :], bc, ALU.is_gt))
                link(nc.vector.scalar_tensor_tensor(lo[:, :, :], k1, 1.0, cmp[:, :, :], ALU.add, ALU.mult))
                link(nc.vector.scalar_tensor_tensor(lo[:, :, :], cmp2[:, :, :], 70000.0, lo[:, :, :], ALU.mult, ALU.add))
                link(nc.vector.memset(cand[:, :], 32769.0))
                search(lo)
                total(ALU.is_gt, lo, cand, cmp)
                got = counted()
                link(nc.vector.tensor_scalar(need[:, :], got, -1.0, float(TOPK), ALU.mult, ALU.add))
                nc.vector.tensor_tensor(cmp2[:, :, :], lo[:, :, :], bc, ALU.is_equal).then_inc(s_cmp, 1)
                asked[0] += 1
                wait(dve, s_cnt, j, NREQ, asked[0])
                inside, totals = pt[:, 64:64 + 2 * COLS], pt[:, 192:192 + 2 * COLS]
                for u in range(2):
                    link(nc.vector.tensor_tensor_scan(rank[:, u, :], const("ones")[:, 0:COLS],
                                                      totals[:, u * COLS:(u + 1) * COLS], 0.0, ALU.mult, ALU.add))
                flat = rank[:, :, :].rearrange("p u c -> p (u c)")
                link(nc.vector.tensor_tensor(flat, flat, totals, ALU.subtract))
                link(nc.vector.tensor_tensor(flat, flat, inside, ALU.add))
                link(nc.vector.tensor_tensor(rank[:, :, :], rank[:, :, :],
                                             need[:, :].unsqueeze(2).broadcast_to([128, 2, COLS]), ALU.is_lt))
                link(nc.vector.tensor_tensor(rank[:, :, :], rank[:, :, :], cmp2[:, :, :], ALU.mult))
                link(nc.vector.tensor_tensor(rank[:, :, :], rank[:, :, :], cmp[:, :, :], ALU.add))
                wait(dve, s_out, j, 64, 0)
                link(nc.vector.tensor_tensor(wsel[:, :, :], rank[:, :, :], wt[:, :, :], ALU.mult))
                cz = czz.rearrange("p (u d) -> p u d", u=2)
                link(nc.vector.tensor_tensor(cz, cy.unsqueeze(1).broadcast_to([1, 2, D]),
                                             wsel[0:1, :, 0:1].broadcast_to([1, 2, D]), ALU.mult))
                nc.vector.tensor_tensor(cz, cz, cbase.unsqueeze(1).broadcast_to([1, 2, D]), ALU.add).then_inc(s_cls, 1)
                for u in range(2):
                    wait(dve, s_yb, j, 2, u + 1)
                    nc.vector.tensor_tensor(yraw[:, u, :, :], yraw[:, u, :, :],
                                            wsel[:, u, 1:COLS].unsqueeze(2).broadcast_to([128, CH, D]),
                                            ALU.mult).then_inc(s_mul, 1)
                    wait(dve, s_mul, j, 2, u + 1)
                    wait(dve, s_base, j, 2, u + 1)
                    nc.vector.tensor_tensor(yraw[:, u, :, :], yraw[:, u, :, :], base[:, u, :, :],
                                            ALU.add).then_inc(s_fin, 1)
                assert n[0] == NCHAIN and asked[0] == NREQ, (n[0], asked[0])

            walk(dve, first, retention, involution_and_norm2, ffn)


        @block.tensor
        def _(pe):
            mm = nc.tensor.matmul

            def involution(j):
                wait(pe, s_h2, j, NSLOT, 0)
                wait(pe, s_qkt, j, NSLOT, 0)
                wait(pe, s_v, j, NSLOT, 0)
                wait(pe, s_state, j, CH + 1, 0)
                wait(pe, s_blk, j, 2, 2)
                for n in range(NCONV):
                    wait(pe, s_yraw, j, NCONV, n - 1)
                    r0 = 1 + n * ROWS_PER_CONV
                    mm(pa[:, n % 2, :].rearrange("p (h b w) -> p b h w", b=WB, w=WS), w1_conv[:, :],
                       xblk[:, :, r0:r0 + ROWS_PER_CONV, 1:WS + 1], start=True, stop=True).then_inc(s_conv, 1)
                for k in range(NG + 1):
                    if k < NG:
                        g, nh = k, rows(k)
                        K = (nh + 2) * PC
                        wait(pe, s_patch, j, NG, g - 1)
                        for b in range(WB):
                            last = nc.tensor.transpose(p_patch[g % 2][0:K, 128 * b:128 * b + 128],
                                                       xblk[:, b, HS * g:HS * g + nh + 2, :].rearrange("p r s -> p (r s)"),
                                                       const("ident"))
                        last.then_inc(s_pt, 1)
                        wait(pe, s_y3, j, NCONV, (HS * g + nh - 1) // ROWS_PER_CONV + 1)
                        for u in range(2):
                            wait(pe, s_taps, j, 2 * NG, 2 * (g - 1) + u + 1)
                            r = slice(64 * u, 64 * u + 3 * YROW)
                            dst = ps[0:K, u, 0:nh * W].rearrange("p (h w) -> p h w", w=W)
                            for rh in range(3):
                                last = mm(dst[:, rh:nh:3, :], gen_w[r, rh, 0:K],
                                          y3[r, HS * g + rh:HS * g + nh:3, :], start=True, stop=True)
                            last.then_inc(s_gen, 1)
                    if k >= 1:
                        g, nh = k - 1, rows(k - 1)
                        K = (nh + 2) * PC
                        wait(pe, s_patch, j, NG, g + 1)
                        wait(pe, s_taps, j, 2 * NG, 2 * g + 2)
                        wait(pe, s_strd, j, NG, g - 1)
                        for b in range(WB):
                            for u in range(2):
                                dst = ps[64 * u:64 * u + 64, 2 + g % 2, 0:nh * W].rearrange("p (h w) -> p h w", w=W)
                                last = mm(dst[:, :, WS * b:WS * b + WS], patch[0:K, g % 2, b, 64 * u:64 * u + 64],
                                          taps[0:K, g % 2, u, 0:nh, WS * b:WS * b + WS], start=True, stop=True)
                        last.then_inc(s_app, 1)

            def transposes(j, kind):
                for u in range(2):
                    wait(pe, s_norm, j, 4, 2 * kind + u + 1)
                for n in range(NFILL):
                    if n >= 2:
                        wait(pe, s_xte, j, 2 * NFILL, NFILL * kind + n - 1)
                    for c in range(4):
                        last = nc.tensor.transpose(pa[:, n % 2, 128 * c:128 * c + 128], xn[:, 4 * n + c, :, :].rearrange("p u d -> p (u d)"),
                                                   const("ident"))
                    last.then_inc(s_xt, 1)

            def retention(j):
                wait(pe, s_gelu, j, 2 * NQ, 0)
                wait(pe, s_yev, j, NQ, 0)
                wait(pe, s_cls, j, 1, 0)
                wait(pe, s_strd, j, NG, NG)
                wait(pe, s_taps, j, 2 * NG, 2 * NG)
                wait(pe, s_patch, j, NG, NG)
                wait(pe, s_yraw, j, NCONV, NCONV)
                transposes(j, 0)
                wait(pe, s_xte, j, 2 * NFILL, NFILL)
                for k in range(NSLOT + 3):
                    if k < NSLOT:
                        t = k
                        wait(pe, s_rot, j, NSLOT, t - 1)
                        wait(pe, s_v, j, NSLOT, t)
                        for c in range(2):
                            lhsT = xT[:, 2 * t + c, :]
                            mm(pa[:, t % 2, 256 * c:256 * c + 256], lhsT,
                               wqk_bd[:, :, :, :, :].rearrange("p a u e j -> p (a u e j)"), start=True, stop=True)
                            last = mm(pv[:, 128 * c:128 * c + 128], lhsT,
                                      wv_bd[:, :, :].rearrange("p u d -> p (u d)"), start=True, stop=True)
                        last.then_inc(s_qkv, 1)
                    if 0 <= k - 1 < NSLOT:
                        t = k - 1
                        wait(pe, s_qk, j, NSLOT, t + 1)
                        wait(pe, s_qkt, j, NSLOT, t)
                        src = qk[:, t % 2, :].rearrange("p (c a n) -> p c a n", c=2, a=2)
                        for c in range(2):
                            for a in range(2):
                                last = nc.tensor.transpose(pt[:, 128 * (2 * c + a):128 * (2 * c + a) + 128],
                                                           src[:, c, a, :], const("ident"))
                        last.then_inc(s_tr, 1)
                        wait(pe, s_v, j, NSLOT, t + 1)
                        wait(pe, s_state, j, CH + 1, 2 * t + 1)
                        for c in range(2):
                            for u in range(2):
                                last = mm(ps[64 * u:64 * u + 64, 3, 64 * c:64 * c + 64],
                                          src[:, c, 1, 64 * u:64 * u + 64],
                                          V[:, t % VRING, c, 64 * u:64 * u + 64], start=True, stop=True)
                        last.then_inc(s_u, 1)
                    if 0 <= k - 2 < NSLOT:
                        t = k - 2
                        wait(pe, s_qkt, j, NSLOT, t + 1)
                        wait(pe, s_ret, j, NSLOT, t)
                        for c in range(2):
                            for u in range(2):
                                r = slice(64 * u, 64 * u + 64)
                                last = mm(ps[:, u, 128 * c:128 * c + 128], QKT[r, t % QRING, c, 1, :],
                                          QKT[r, t % QRING, c, 0, :], start=True, stop=True)
                        last.then_inc(s_sc, 1)
                    if 0 <= k - 3 < NSLOT:
                        t = k - 3
                        wait(pe, s_ret, j, NSLOT, t + 1)
                        wait(pe, s_state, j, CH + 1, 2 * t + 2)
                        wait(pe, s_h2, j, NSLOT, t)
                        for c in range(2):
                            mm(ps[:, 2, 128 * c:128 * c + 128], QKT[:, t % QRING, c, 0, :],
                               P[:, (2 * t + c - 1) % PRING, :, :].rearrange("p u d -> p (u d)"),
                               start=True, stop=False)
                            for u in range(2):
                                last = mm(ps[:, 2, 128 * c + 64 * u:128 * c + 64 * u + 64], RT[:, t % 2, u, c, :],
                                          V[:, t % VRING, c, 64 * u:64 * u + 64], start=False, stop=(u == 1))
                        last.then_inc(s_o, 1)

            def ffn(j, more):
                wait(pe, s_h2, j, NSLOT, NSLOT)
                wait(pe, s_state, j, CH + 1, CH + 1)
                wait(pe, s_qkt, j, NSLOT, NSLOT)
                if more:
                    nx = (j[0], j[1] + 1)
                    wait(pe, s_strd, nx, NG, NG)
                    wait(pe, s_taps, nx, 2 * NG, 2 * NG)
                    wait(pe, s_yraw, nx, NCONV, NCONV)
                    wait(pe, s_patch, nx, NG, NG)
                transposes(j, 1)
                wait(pe, s_xte, j, 2 * NFILL, 2 * NFILL)
                for ch in range(CH):
                    last = mm(pv[:, 2 * ch:2 * ch + 2], xT[:, ch, :], wr_bd[:, :], start=True, stop=True)
                last.then_inc(s_w, 1)

                def count(n):
                    wait(pe, s_cmp, j, NREQ, n + 1)
                    if n < NREQ - 1:
                        c0 = 2 * ((n + 1) % 2)
                        mm(pt[:, c0:c0 + 2], const("ones"), part[:, :], start=True, stop=True).then_inc(s_cnt, 1)
                    else:
                        tie = cmp2[:, :, :].rearrange("p u c -> p (u c)")
                        mm(pt[:, 64:64 + 2 * COLS], const("tri"), tie, start=True, stop=True)
                        mm(pt[:, 192:192 + 2 * COLS], const("ones"), tie, start=True, stop=True).then_inc(s_cnt, 1)

                for k in range(NQ + 1):
                    if k < NQ:
                        cg, u = k // 2, k % 2
                        r = slice(64 * u, 64 * u + 64)
                        for m in range(2):
                            wait(pe, s_gelu, j, 2 * NQ, 2 * (k - 2) + m + 1)
                            mm(ps[:, 2 * (k % 2) + m, :], w1t[r, 128 * m:128 * m + 128],
                               xT[r, 4 * cg:4 * cg + 4, :].rearrange("p c l -> p (c l)"),
                               start=True, stop=True).then_inc(s_hid, 1)
                            count(2 * k + m)
                    if k >= 1:
                        q = k - 1
                        wait(pe, s_gelu, j, 2 * NQ, 2 * q + 2)
                        wait(pe, s_yev, j, NQ, q - 1)
                        for c in range(4):
                            for m in range(2):
                                last = mm(pa[:, q % 2, 64 * c:64 * c + 64], hid[:, q % 2, m, 128 * c:128 * c + 128],
                                          w2t[:, m, :], start=(m == 0), stop=(m == 1))
                        last.then_inc(s_y, 1)
                for n in range(2 * NQ, NREQ):
                    count(n)

            pe.wait_ge(s_load, N_SETUP_LOADS)
            mm(pa[:, 0, 0:5], const("spread", CR), bn5[:, :], start=True, stop=True)
            for u in range(2):
                mm(pa[64 * u:64 * u + 64, 1, 64 * u:64 * u + 64], c1w[:, :], const("spread", CR)[:, 0:64],
                   start=True, stop=True)
            for rh in range(3):
                n = PR * PC
                last = mm(pv[:, n * rh:n * rh + n], c2bd[:, :], const("sel", 27)[:, n * rh:n * rh + n],
                          start=True, stop=True)
            last.then_inc(s_setup, 1)
            pe.wait_ge(s_setup, 15)
            nc.tensor.transpose(pa[0:64, 0, 0:1], cxn, const("ident", 1)[:, 0:1]).then_inc(s_setup, 1)
            pe.wait_ge(s_setup, 17)
            mm(pa[0:1, 0, 0:192], ccol[0:64, 0:1], wqkv[0:64, :, :].rearrange("p a d -> p (a d)"),
               start=True, stop=True).then_inc(s_setup, 1)
            pe.wait_ge(s_setup, 20)
            for u in range(2):
                last = mm(pa[64 * u:64 * u + 64, 1, 0:64], ck, cqkv[:, 128:192], start=True, stop=True)
            last.then_inc(s_setup, 1)
            pe.wait_ge(s_setup, 29)
            nc.tensor.transpose(pa[0:64, 0, 0:1], cxn2, const("ident", 1)[:, 0:1]).then_inc(s_setup, 1)
            pe.wait_ge(s_setup, 31)
            for m in range(2):
                mm(pa[:, 0, 4 + m:5 + m], w1t[0:64, 128 * m:128 * m + 128], ccol[0:64, 1:2], start=True, stop=True)
            mm(pa[0:1, 1, 64:65], ccol[0:64, 1:2], wrt[0:64, :], start=True, stop=True).then_inc(s_setup, 1)
            pe.wait_ge(s_setup, 33)
            for m in range(2):
                last = mm(pa[0:1, 0, 64:128], ccol[:, 2 + m:3 + m], w2t[:, m, :], start=(m == 0), stop=(m == 1))
            last.then_inc(s_setup, 1)
            pe.wait_ge(s_setup, 36)
            pe.wait_ge(s_memz, 8)
            pe.wait_ge(s_tab, 32)

            def first():
                involution((0, 0))

            walk(pe, first, retention, involution, ffn)


_INS = ['x', 'cls_tok', 'L0_tok_conv1_w', 'L0_tok_conv1_b', 'L0_tok_bn_gamma', 'L0_tok_bn_beta', 'L0_tok_bn_mean',
        'L0_tok_bn_var', 'L0_tok_conv2_w', 'L0_tok_conv2_b', 'L0_attn_W_Q', 'L0_attn_W_K', 'L0_attn_W_V',
        'L0_ffn_wr', 'L0_ffn_br', 'L0_ffn_w1', 'L0_ffn_b1', 'L0_ffn_w2', 'L0_ffn_b2']


def kernel(**inputs):
    import numpy as _np
    import concourse.bacc as _bacc
    from concourse import mybir as _mybir
    from concourse.bass_utils import run_bass_kernel_spmd as _run

    nc = _bacc.Bacc("TRN2", target_bir_lowering=False, num_devices=1)
    arrays, args = {}, []
    feeds = [(name, _np.ascontiguousarray(inputs[name])) for name in _INS]
    feeds += [("small_constants", small_constants()), ("position_tables", position_tables())]
    for name, a in feeds:
        arrays[f"in_{name}_dram"] = a
        args.append(nc.dram_tensor(f"in_{name}_dram", a.shape, _mybir.dt.from_np(a.dtype), kind="ExternalInput").ap())
    args.append(nc.dram_tensor("out_0_dram", (B, SEQ, D), _mybir.dt.float32, kind="ExternalOutput").ap())
    vit_tower(nc, *args)
    r = _run(nc, [arrays], core_ids=[0])
    return r.results[0]["out_0_dram"]
```

```python
from contextlib import ExitStack

import concourse.bass as bass
import numpy as np
from concourse import mybir

B, C, H, W = 8, 64, 64, 64
NPAIR = B // 2
CR = C // 4
TAPS = 9
SEQ = C * H + 1
D = W
CH = C * H // 128
HID = 4 * D
GAMMA = 0.96875
SCALE_BASE = 512.0
EPS = 1e-5
TOPK = max(1, int(0.5 * SEQ)) - 1

HS, WS = 5, 16
WB = W // WS
NG = -(-H // HS)
PR, PC = HS + 2, WS + 2
YROW = CR + 1
ROWS_PER_CONV = 512 // W
NCONV = H // ROWS_PER_CONV
NSLOT = CH // 2
NFILL = CH // 4
NQ = CH // 2
NB = HID // 64
LQ, CQ = 4, CH // 4
LR, CP = 8, CH // 8
COLS = CH + 1
VRING, QRING, PRING = 4, 3, 8

CONST = {}


def _layout():
    at = 0
    for name, n in (("ident", 128), ("cmask", 128), ("tri", 128), ("ones", 128), ("ymask", 64),
                    ("tmask", HS * WS), ("sel", 3 * PR * PC), ("blocks", 128),
                    ("rep", 27), ("spread", 128), ("valid", 2 * COLS),
                    ("onerow", 1)):
        CONST[name] = (at, at + n)
        at += n
    return at


NCONST = _layout()


def small_constants():
    c = np.zeros((128, NCONST), np.float32)

    def put(name, rows, a):
        s, e = CONST[name]
        c[:rows, s:e] = a.reshape(rows, e - s)

    i = np.arange(128)
    put("ident", 128, np.eye(128))
    put("cmask", 128, (i[:, None] <= i[None, :]) * GAMMA ** -128.0)
    put("tri", 128, (i[:, None] < i[None, :]) * 1.0)
    put("ones", 128, np.ones((128, 128)))
    ym = np.zeros((128, W))
    for u in range(2):
        for rw in range(3):
            r0 = 64 * u + rw * YROW
            ym[r0:r0 + YROW] = (np.arange(W) % WS % 3 == rw)
    put("ymask", 128, ym)
    tm = np.zeros((PR * PC, HS, WS))
    sel = np.zeros((27, 3, PR * PC))
    for r in range(PR):
        for s in range(PC):
            for h in range(HS):
                for w in range(WS):
                    tm[r * PC + s, h, w] = 0 <= r - h <= 2 and 0 <= s - w <= 2
            for rh in range(3):
                for rw in range(3):
                    sel[rw * TAPS + (r - rh) % 3 * 3 + (s - rw) % 3, rh, r * PC + s] = 1
    put("tmask", PR * PC, tm)
    put("sel", 27, sel)
    bl = np.zeros((27, 128))
    for rw in range(3):
        for u in range(2):
            bl[rw * TAPS:(rw + 1) * TAPS, 64 * u + rw * YROW:64 * u + (rw + 1) * YROW] = 1
    put("blocks", 27, bl)
    put("rep", TAPS, np.tile(np.eye(TAPS), 3))
    sp = np.zeros((CR, 128))
    one = np.zeros((128, 1))
    for u in range(2):
        for rw in range(3):
            for k in range(CR):
                sp[k, 64 * u + rw * YROW + k] = 1
            one[64 * u + rw * YROW + CR] = 1
    put("spread", CR, sp)
    put("onerow", 128, one)
    v = np.ones((128, 2, COLS))
    v[1:, :, 0] = 0
    put("valid", 128, v)
    return c


def position_tables():
    f = np.float32
    inv_freq = (f(1.0) / np.power(f(10000.0), np.arange(0, D, 2, dtype=f) / f(D))).astype(f)
    pos = (1 + np.arange(CH * 128)).astype(f)
    ang = (pos[:, None] * inv_freq[None, :]).astype(f).astype(np.float64)
    base = ((np.arange(0, D, 2, dtype=f) + f(0.4 * D)) / f(1.4 * D)).astype(np.float64)
    scale = base[None, :] ** (pos[:, None].astype(np.float64) / SCALE_BASE)
    step = (np.arange(CH * 128) % 128 + 1.0)[:, None]
    q = scale * GAMMA ** (step + 128)
    k = 1.0 / scale * GAMMA ** -step
    out = []
    for trig in (np.cos(ang), np.sin(ang)):
        t = np.stack([trig * q, trig * k], axis=1)
        out.append(t.reshape(CH, 128, 64).transpose(1, 0, 2))
    return np.ascontiguousarray(np.stack(out), dtype=np.float32)


def vit_tower(nc, x, cls_tok, conv1_w, conv1_b, bn_gamma, bn_beta, bn_mean, bn_var, conv2_w, conv2_b,
              W_Q, W_K, W_V, wr, br, w1, b1, w2, b2, consts, tables, out):
    bf16 = mybir.dt.bfloat16
    fp32, i32, u32 = mybir.dt.float32, mybir.dt.int32, mybir.dt.uint32
    ALU, ACT, AX = mybir.AluOpType, mybir.ActivationFunctionType, mybir.AxisListType

    with ExitStack() as ctx:
        def sb(name, shape, dt=fp32):
            return ctx.enter_context(nc.sbuf_tensor(name, shape, dt))

        def sem(name):
            return ctx.enter_context(nc.semaphore(name))

        h_dram = nc.dram_tensor("h_scratch", [B, C * H * W], fp32, kind="Internal").ap()

        cst = sb("cst", [128, NCONST])

        def const(name, rows=128):
            s, e = CONST[name]
            return cst[0:rows, s:e]

        cos_t = sb("cos_t", [128, CH, 64])
        sin_t = sb("sin_t", [128, CH, 64])
        wqkv = sb("wqkv", [128, 3, D])
        wqk_bd = sb("wqk_bd", [128, 2, 2, 2, 32])
        wv_bd = sb("wv_bd", [128, 2, D])
        wrt = sb("wrt", [D, 1])
        wr_b = sb("wr_b", [128, D])
        w1_bd = sb("w1_bd", [128, NB, 2, 64])
        w2_bd = sb("w2_bd", [128, NB, 2, D])
        b1t = sb("b1t", [128, NB])
        b2t = sb("b2t", [128, D])
        brt = sb("brt", [128, 1])
        bn5 = sb("bn5", [CR, 5])
        c1w = sb("c1w", [CR, C])
        c2t = sb("c2t", [TAPS, YROW])
        c2rep = sb("c2rep", [TAPS, 128])
        c2bd = sb("c2bd", [27, 128])
        bnp = sb("bnp", [128, 5])
        bns = sb("bns", [128, 4])
        w1_conv = sb("w1_conv", [128, 128])
        gen_w = sb("gen_w", [128, 2, 3, PR * PC])
        ones_b = sb("ones_b", [128, 128], bf16)
        tri_b = sb("tri_b", [128, 128], bf16)
        half = sb("half", [128, 2 * CQ])

        xblk = sb("xblk", [128, WB, H + 2, PC])
        scores = sb("scores", [128, 2, 512])
        y_raw = scores
        y3 = sb("y3", [128, H, W])
        patch = sb("patch", [128, 2, WB, 128])
        taps = sb("taps", [128, 2, 2, HS, W])
        strip = sb("strip", [128, 4, HS, W])

        X = sb("X", [128, 2, CH, D])
        xn = sb("xn", [128, CH, 2, D])
        base = sb("base", [128, 2, CH, D])
        yraw = sb("yraw", [128, 2, CH, D])
        xT = sb("xT", [128, CH, 128])
        sq = sb("sq", [128, CH, D])
        st = sb("st", [128, LQ, 5, 2 * CQ])

        def quarter(a, q):
            return a[:, CQ * q:CQ * q + CQ, :, :].rearrange("p c u d -> p u c d") if a is xn \
                else a[:, :, CQ * q:CQ * q + CQ, :]

        def piece(a, r):
            return a[:, :, CP * r:CP * r + CP, :]

        def squares(kind, q):
            if kind:
                return quarter(yraw, q)
            return sq[:, 2 * CQ * (q % 2):2 * CQ * (q % 2) + 2 * CQ, :].rearrange("p (u c) d -> p u c d", u=2)

        def stat(q, n):
            return st[:, q, n, :].rearrange("p (u c) -> p u c", u=2)

        def each_feature(a):
            return a.unsqueeze(3).broadcast_to([128, 2, CQ, D])
        terms = sb("terms", [128, 4, 512])
        t1, t2 = terms[:, 0:2, :], terms[:, 2:4, :]
        qk = sb("qk", [128, 2, 512])
        V = sb("V", [128, VRING, 2, 128])
        QKT = sb("QKT", [128, QRING, 2, 2, 128])
        RT = scores[:, :, :].rearrange("p r (u c n) -> p r u c n", u=2, c=2)
        P = sb("P", [128, PRING, 2, D])
        P0 = sb("P0", [128, D])
        hid = terms[:, :, :].rearrange("p (k m) (b n) -> p k (m b) n", m=2, b=2)

        cl = sb("cl", [1, 832])
        crow, cxn, ctmp, cqkv, ck, ch2, cxn2, cy, cbase, czz = (cl[:, a:b] for a, b in (
            (0, 64), (64, 128), (128, 192), (192, 384), (384, 448), (448, 512), (512, 576), (576, 640),
            (640, 704), (704, 832)))
        cst1 = sb("cst1", [1, 8])
        ccol = sb("ccol", [128, 2 + NB])
        w_cls = sb("w_cls", [1, 1])

        wt = sb("wt", [128, 2, COLS])
        key = sb("key", [128, 2, 2, COLS], i32)
        hi = sb("hi", [128, 2, COLS])
        lo = sb("lo", [128, 2, COLS])
        cmp = sb("cmp", [128, 2, COLS])
        tie = sb("tie", [128, 2, COLS], bf16)
        part = sb("part", [128, 2], bf16)
        cand = sb("cand", [128, 2])
        dlt = sb("dlt", [128, 2])
        need = sb("need", [128, 2])
        wsel = sb("wsel", [128, 2, COLS])
        rank = sb("rank", [128, 2, COLS])
        cmp2 = rank

        pa = ctx.enter_context(nc.psum_tensor("pa", [128, 2, 512], fp32))
        pv = ctx.enter_context(nc.psum_tensor("pv", [128, 512], fp32))
        pt = ctx.enter_context(nc.psum_tensor("pt", [128, 512], fp32))
        ps = ctx.enter_context(nc.psum_tensor("ps", [128, 4, 512], fp32))
        p_patch = (pv, pt)

        s_load, s_cload, s_tab = sem("weights_loaded"), sem("conv_weights_loaded"), sem("tables_loaded")
        s_x, s_out = sem("image_loaded"), sem("stored")
        s_xl = [sem(f"tokens_loaded{q}") for q in range(LQ)]
        s_strip = [sem(f"strip_stored{n}") for n in range(4)]
        s_setup = sem("setup_step")
        s_pad, s_blk = sem("image_padding_zero"), sem("image_cut")
        s_memz, s_zero = sem("weights_zeroed"), sem("tiles_zeroed")
        s_conv, s_yraw = sem("conv1_done"), sem("relu_done")
        s_y3 = sem("y3_ready")
        s_pt, s_patch = sem("patch_transposed"), sem("patch_ready")
        s_gen, s_taps = sem("taps_made"), sem("taps_masked")
        s_app, s_strd = sem("involution_done"), sem("strip_ready")
        s_sum, s_mean, s_cent, s_sq, s_ss, s_var, s_rstd, s_norm = (sem("ln_" + n) for n in (
            "sum", "mean", "centred", "squared", "square_sum", "variance", "rstd", "normed"))
        s_base = sem("base_ready")
        s_xt, s_xte = sem("tokens_transposed"), sem("xT_ready")
        s_qkv, s_rot, s_qk, s_v = sem("qkv_done"), sem("rotated"), sem("qk_ready"), sem("v_ready")
        s_tr, s_qkt, s_u, s_state = sem("qk_transposed"), sem("qkt_ready"), sem("kv_done"), sem("state_ready")
        s_sc, s_ret, s_o, s_h2 = sem("scores_done"), sem("ret_ready"), sem("retention_done"), sem("h2_ready")
        s_prod, s_w = sem("router_products"), sem("router_sums")
        s_cmp, s_cnt, s_chain = sem("count_asked"), sem("count_done"), sem("router_step")
        s_hid, s_gelu, s_y, s_yev = sem("hidden_done"), sem("gelu_done"), sem("ffn_done"), sem("ffn_read")
        s_yb, s_mul, s_fin, s_cls = sem("ffn_biased"), sem("ffn_weighted"), sem("result_ready"), sem("cls_result_ready")

        counting = [s_x, *s_xl, s_out, *s_strip, s_blk, s_conv, s_yraw, s_y3, s_pt, s_patch, s_gen, s_taps, s_app,
                    s_strd, s_sum, s_mean, s_cent, s_sq, s_ss, s_var, s_rstd, s_norm, s_base, s_xt, s_xte, s_qkv,
                    s_rot, s_qk, s_v, s_tr, s_qkt, s_u, s_state, s_sc, s_ret, s_o, s_h2, s_prod, s_w, s_cmp, s_cnt,
                    s_chain, s_hid, s_gelu, s_y, s_yev, s_yb, s_mul, s_fin, s_cls]

        def at(j, per_pair, n):
            reg, add = j
            return reg * per_pair + (1 + max(n + add * per_pair, 0)) if not isinstance(reg, int) \
                else 1 + max((reg + add) * per_pair + n, 0)

        def is_last(j):
            return isinstance(j[0], int) and j[0] == NPAIR - 1

        def counts(j, n):
            bank = pa[:, 0, :] if n < NEARLY and not isinstance(j[0], int) else pt
            return bank[:, 2 * (n % 2):2 * (n % 2) + 2]

        def pair(j):
            return j[0] + j[1]

        def rows(g):
            return min(HS, H - HS * g)

        N_SETUP_LOADS = 16 * 17
        N_CONV_LOADS = 16 * 9
        NREQ = 2 * 16 + 2
        FIRST_ASKING = NG - 8
        NEARLY = 8
        NCHAIN = 119
        NORMS = 2 * LQ
        NSTORED = 16 * (2 * LQ + 2)
        block = ctx.enter_context(nc.Block())

        def walk(eng, first, retention, involution, ffn):
            first()
            with eng.Fori(0, NPAIR - 1) as i:
                retention((i, 0))
                involution((i, 1))
                ffn((i, 0), True)
            retention((NPAIR - 1, 0))
            ffn((NPAIR - 1, 0), False)

        @block.sync
        def _(sp):
            loads = [0]

            def load(dst, src):
                loads[0] += 1
                sp.dma_start(dst, src).then_inc(s_load, 16)

            def load_image(j, buffers=(sq, sq)):
                sp.wait_ge(s_ss, at((j[0], j[1] - 1), NORMS, LQ))
                for n, dst in enumerate(buffers):
                    if dst is sq:
                        sp.wait_ge(s_blk, at(j, 2, n))
                    src = x[bass.ds(pair(j) * 2, 2), :, H // 2 * n:H // 2 * (n + 1), :]
                    sp.dma_start(dst[:, :, :], src.rearrange("b c h w -> (b c) h w")).then_inc(s_x, 16)

            def store_strips(j):
                for g in range(NG):
                    nh = rows(g)
                    sp.wait_ge(s_strd, at(j, NG, g + 1))
                    dst = h_dram[bass.ds(pair(j) * 2, 2), :].rearrange("b (c n) -> (b c) n", c=C)
                    sp.dma_start(dst[:, g * HS * W:(g * HS + nh) * W],
                                 strip[:, g % 4, 0:nh, :].rearrange("p h w -> p (h w)")).then_inc(s_strip[g % 4], 16)

            def load_tokens(j):
                for n in range(4):
                    per = 16 * len(range(n, NG, 4))
                    sp.wait_ge(s_strip[n], at(j, per, per))
                sp.wait_ge(s_base, at(j, LQ, 0))
                for q in range(LQ):
                    cs = slice(CQ * q, CQ * q + CQ)
                    for u in range(2):
                        src = h_dram[bass.ds(pair(j) * 2 + u, 1), :].rearrange("a (c l d) -> l (a c) d", l=128, d=D)
                        sp.dma_start(X[:, u, cs, :], src[:, cs, :]).then_inc(s_xl[q], 16)

            def store_result(j):
                for q in range(LQ):
                    sp.wait_ge(s_fin, at(j, LR, LR // LQ * (q + 1)))
                    cs = slice(CQ * q, CQ * q + CQ)
                    for u in range(2):
                        dst = out[bass.ds(pair(j) * 2 + u, 1), 1:SEQ, :].rearrange("a (c l) d -> l (a c) d", l=128)
                        sp.dma_start(dst[:, cs, :], yraw[:, u, cs, :]).then_inc(s_out, 16)

            load_image((0, 0), (sq, yraw[:, 0, :, :]))
            sp.wait_ge(s_memz, 4)
            for u in range(2):
                hs = slice(64 * u, 64 * u + 64)
                for n, a in enumerate((W_Q, W_K, W_V)):
                    load(wqkv[hs, n, :], a)
                load(w1_bd[hs, :, u, :], w1.rearrange("d (b h) -> d b h", h=64))
                load(w2_bd[hs, :, u, :], w2.rearrange("(b h) d -> h b d", h=64))
                with nc.allow_non_contiguous_dma("256 biases, once"):
                    load(b1t[hs, :], b1.rearrange("(b h) -> h b", h=64))
            load(wrt[:, :], wr)
            load(wr_b[:, :], wr.rearrange("d a -> (a d)").partition_broadcast(128))
            load(b2t[:, :], b2.partition_broadcast(128))
            load(brt[:, :], br.partition_broadcast(128))
            load(crow, cls_tok[0, :, :])
            assert 16 * loads[0] == N_SETUP_LOADS
            for n, tab in enumerate((cos_t, sin_t)):
                sp.dma_start(tab[:, :, :], tables[n, :, :, :]).then_inc(s_tab, 16)

            def first():
                store_strips((0, 0))
                load_tokens((0, 0))

            def ffn(j, more):
                if more:
                    load_tokens((j[0], j[1] + 1))
                store_result(j)

            def retention(j):
                if not isinstance(j[0], int):
                    load_image((j[0], j[1] + 1))

            walk(sp, first, retention, store_strips, ffn)
            sp.wait_ge(s_out, at((0, NPAIR), NSTORED, 0))

        @block.gpsimd
        def _(pool):
            def centre(j, kind, q):
                m = LQ * kind + q
                pool.wait_ge(s_mean, at(j, NORMS, m + 1))
                pool.wait_ge(s_xt, at(j, 2 * NFILL, NFILL * (kind - 1) + NFILL // LQ * (q + 1)))
                if kind == 0:
                    pool.wait_ge(s_w, at(j, LQ, 0))
                nc.gpsimd.tensor_tensor(quarter(xn, q), quarter(X, q), each_feature(stat(q, 1)),
                                        ALU.subtract).then_inc(s_cent, 1)

            def root(j, kind, q):
                pool.wait_ge(s_var, at(j, NORMS, LQ * kind + q + 1))
                nc.gpsimd.tensor_tensor(st[:, q, 4, :], st[:, q, 3, :], half[:, 0:2 * CQ], ALU.pow).then_inc(s_rstd, 1)

            def normalise(j, kind, q):
                pool.wait_ge(s_rstd, at(j, NORMS, LQ * kind + q + 1))
                nc.gpsimd.tensor_tensor(quarter(xn, q), quarter(xn, q), each_feature(stat(q, 4)),
                                        ALU.mult).then_inc(s_norm, 1)

            def bases(j):
                for q in range(LQ):
                    pool.wait_ge(s_norm, at(j, NORMS, LQ + q + 1))
                    pool.wait_ge(s_fin, at(j, LR, 0))
                    nc.gpsimd.tensor_tensor(quarter(base, q), quarter(X, q), quarter(xn, q),
                                            ALU.add).then_inc(s_base, 1)

            def bias(j, r):
                pool.wait_ge(s_yev, at(j, NQ, NQ // LR * (r + 1)))
                nc.gpsimd.tensor_tensor(piece(yraw, r), piece(yraw, r),
                                        b2t[:, :].unsqueeze(1).unsqueeze(1).broadcast_to([128, 2, CP, D]),
                                        ALU.add).then_inc(s_yb, 1)

            for s in counting:
                pool.sem_inc(s, 1)
            nc.gpsimd.memset(xblk[:, :, :, :], 0.0).then_inc(s_pad, 1)
            nc.gpsimd.memset(w1_bd[:, :, :, :], 0.0).then_inc(s_memz, 1)
            nc.gpsimd.memset(w2_bd[:, :, :, :], 0.0).then_inc(s_memz, 1)
            nc.gpsimd.memset(half[:, :], -0.5).then_inc(s_memz, 1)
            nc.gpsimd.memset(c2rep[:, :], 0.0).then_inc(s_memz, 1)
            pool.wait_ge(s_memz, 4)
            pool.wait_ge(s_setup, 5)
            nc.gpsimd.tensor_tensor(bns[:, 1:2], bns[:, 0:1], half[:, 0:1], ALU.pow).then_inc(s_setup, 1)

            def first():
                for n in (16, 30):
                    pool.wait_ge(s_setup, n)
                    nc.gpsimd.tensor_tensor(cst1[:, 3:4], cst1[:, 2:3], half[0:1, 0:1], ALU.pow).then_inc(s_setup, 1)
                centre((0, 0), 0, 0)
                centre((0, 0), 0, 1)
                for q in range(LQ):
                    root((0, 0), 0, q)

            def retention(j):
                for t in range(NSLOT):
                    pool.wait_ge(s_rot, at(j, NSLOT, t + 1))
                    pool.wait_ge(s_u, at(j, NSLOT, t - 1))
                    o, a, b = (v[:, t % 2, :].rearrange("p (f e n) -> p f e n", e=2, n=32) for v in (qk, t1, t2))
                    nc.gpsimd.tensor_tensor(o[:, :, 0, :], a[:, :, 0, :], b[:, :, 0, :], ALU.subtract)
                    nc.gpsimd.tensor_tensor(o[:, :, 1, :], a[:, :, 1, :], b[:, :, 1, :], ALU.add).then_inc(s_qk, 1)
                    if t >= 7 and t % 4 == 3:
                        centre(j, 1, t // 4 - 1)
                    if t == 10 or t == 14:
                        root(j, 1, t // 4 - 2)
                    if t == 12:
                        normalise(j, 1, 0)
                normalise(j, 1, 1)
                root(j, 1, 2)
                normalise(j, 1, 2)
                if is_last(j):
                    root(j, 1, 3)
                    bases(j)

            def involution(j):
                jn = (j[0], j[1] - 1)
                centre(jn, 1, 3)
                root(jn, 1, 3)
                normalise(jn, 1, 3)
                bases(jn)

            def ffn(j, more):
                nx = (j[0], j[1] + 1)
                if more:
                    for q in (0, 1, 2):
                        centre(nx, 0, q)
                    root(nx, 0, 0)
                    normalise(nx, 0, 0)
                    centre(nx, 0, 3)
                    for q in (1, 2, 3):
                        root(nx, 0, q)
                        normalise(nx, 0, q)
                for r in range(LR):
                    bias(j, r)

            walk(pool, first, retention, involution, ffn)

        @block.scalar
        def _(act):
            def cut_image(j, n, b):
                if b == 0:
                    act.wait_ge(s_app, at(j, NG, 0))
                    act.wait_ge(s_x, at(j, 32, 32 if isinstance(j[0], int) else 16 * (n + 1)))
                r0 = 1 + H // 2 * n
                first_col, last_col = max(WS * b - 1, 0), min(WS * b + WS + 1, W)
                d0 = first_col - (WS * b - 1)
                src = yraw[:, 0, :, :] if n == 1 and isinstance(j[0], int) else sq
                last = nc.scalar.activation(xblk[:, b, r0:r0 + H // 2, d0:d0 + last_col - first_col],
                                            src[:, :, first_col:last_col], ACT.Copy)
                if b == WB - 1:
                    last.then_inc(s_blk, 1)

            def relus(j):
                for n in range(NCONV):
                    act.wait_ge(s_conv, at(j, NCONV, n + 1))
                    act.wait_ge(s_y3, at(j, NCONV, n - 1))
                    if n < 2 and not isinstance(j[0], int):
                        act.wait_ge(s_o, at((j[0], j[1] - 1), NSLOT, NSLOT - 1 + n))
                    nc.scalar.activation(y_raw[:, n % 2, :], pa[:, n % 2, :], ACT.Relu,
                                         bias=bns[:, 3:4], scale=bns[:, 2:3]).then_inc(s_yraw, 1)

            def involution(j, norm2=True):
                relus(j)
                for g in range(NG + 1):
                    if norm2 and g == 0:
                        square((j[0], j[1] - 1), 1, 3)
                    if g < NG:
                        K = (rows(g) + 2) * PC
                        act.wait_ge(s_pt, at(j, NG, g + 1))
                        act.wait_ge(s_app, at(j, NG, g - 1))
                        nc.scalar.activation(patch[0:K, g % 2, :, :].rearrange("p b c -> p (b c)"),
                                             p_patch[g % 2][0:K, :], ACT.Copy).then_inc(s_patch, 1)
                        if norm2 and g >= NG - NFILL:
                            read_fill((j[0], j[1] - 1), 1, g - NG + NFILL, pa[:, 1, :])
                    if g >= 1:
                        q = g - 1
                        nh = rows(q)
                        act.wait_ge(s_app, at(j, NG, q + 1))
                        act.wait_ge(s_strip[q % 4], at(j, 16 * len(range(q % 4, NG, 4)), 16 * (q // 4)))
                        nc.scalar.activation(strip[:, q % 4, 0:nh, :].rearrange("p h w -> p (h w)"),
                                             ps[:, 2 + q % 2, 0:nh * W], ACT.Copy).then_inc(s_strd, 1)

            def square(j, kind, q):
                m = LQ * kind + q
                act.wait_ge(s_cent, at(j, NORMS, m + 1))
                if kind:
                    act.wait_ge(s_out, at(j, NSTORED, 0))
                else:
                    act.wait_ge(s_blk, at(j, 2, 2))
                    act.wait_ge(s_ss, at(j, NORMS, m - 1))
                nc.scalar.activation(squares(kind, q), quarter(xn, q), ACT.Square).then_inc(s_sq, 1)

            def read_fill(j, kind, n, bank):
                act.wait_ge(s_xt, at(j, 2 * NFILL, NFILL * kind + n + 1))
                if kind:
                    act.wait_ge(s_qkv, at(j, NSLOT, NSLOT))
                else:
                    act.wait_ge(s_hid, at((j[0], j[1] - 1), NB * NQ, NB * (2 * n + 2)))
                src = pa[:, n % 2, :] if bank is None else bank
                nc.scalar.activation(xT[:, 4 * n:4 * n + 4, :].rearrange("p c l -> p (c l)"),
                                     src, ACT.Copy).then_inc(s_xte, 1)

            def retention(j):
                for k in range(NSLOT + 1):
                    if not isinstance(j[0], int) and k % 8 >= 2 and k % 8 < 2 + WB:
                        cut_image((j[0], j[1] + 1), k // 8, k % 8 - 2)
                    if k < NSLOT:
                        act.wait_ge(s_qkv, at(j, NSLOT, k + 1))
                        act.wait_ge(s_o, at(j, NSLOT, k - VRING + 1))
                        nc.scalar.activation(V[:, k % VRING, :, :].rearrange("p c d -> p (c d)"),
                                             pv[:, 0:256], ACT.Copy).then_inc(s_v, 1)
                    if k >= 1:
                        t = k - 1
                        act.wait_ge(s_tr, at(j, NSLOT, t + 1))
                        act.wait_ge(s_o, at(j, NSLOT, t - QRING + 1))
                        nc.scalar.activation(QKT[:, t % QRING, :, :, :].rearrange("p c a l -> p (c a l)"),
                                             pt[:, :], ACT.Copy).then_inc(s_qkt, 1)
                    if k >= 8 and k % 4 == 0:
                        square(j, 1, k // 4 - 2)
                if is_last(j):
                    square(j, 1, 3)

            def ffn(j, more):
                if not more:
                    for n in range(NFILL):
                        read_fill(j, 1, n, None)
                for k in range(NQ + 1):
                    if more and 4 <= k < 4 + LQ:
                        square((j[0], j[1] + 1), 0, k - 4)
                    if k < NQ:
                        for m in range(NB):
                            act.wait_ge(s_hid, at(j, NB * NQ, NB * k + (m | 1) + 1))
                            act.wait_ge(s_y, at(j, NQ, k - 1))
                            nc.scalar.activation(hid[:, k % 2, m, :],
                                                 ps[:, 2 * (k % 2) + m // 2, 256 * (m % 2):256 * (m % 2) + 256],
                                                 ACT.Gelu_apprx_tanh, bias=b1t[:, m:m + 1]).then_inc(s_gelu, 1)
                    if more and k >= NQ - NFILL and k < NQ:
                        read_fill((j[0], j[1] + 1), 0, k - NQ + NFILL, pv[:, :])
                    if k >= 1:
                        q = k - 1
                        act.wait_ge(s_y, at(j, NQ, q + 1))
                        act.wait_ge(s_out, at(j, NSTORED, 0))
                        act.wait_ge(s_w, at(j, LQ, LQ))
                        nc.scalar.activation(yraw[:, :, 2 * q:2 * q + 2, :],
                                             pa[:, q % 2, 0:256].rearrange("p (c u d) -> p u c d", c=2, u=2),
                                             ACT.Copy).then_inc(s_yev, 1)
                act.wait_ge(s_cls, at(j, 1, 1))
                for u in range(2):
                    act.dma_start(out[bass.ds(pair(j) * 2 + u, 1), 0, :], czz[:, D * u:D * u + D]).then_inc(s_out, 16)

            act.dma_start(cst[:, :], consts).then_inc(s_cload, 16)
            for n, a in enumerate((conv1_b, bn_mean, bn_gamma, bn_beta, bn_var)):
                act.dma_start(bn5[:, n:n + 1], a.rearrange("(p a) -> p a", a=1)).then_inc(s_cload, 16)
            act.dma_start(c1w[:, :], conv1_w).then_inc(s_cload, 16)
            act.dma_start(c2t[:, 0:CR], conv2_w).then_inc(s_cload, 16)
            act.dma_start(c2t[:, CR:YROW], conv2_b.rearrange("(p a) -> p a", a=1)).then_inc(s_cload, 16)
            act.wait_ge(s_pad, 1)
            for n in range(2):
                for b in range(WB):
                    cut_image((0, 0), n, b)
            def first():
                involution((0, 0), norm2=False)
                act.wait_ge(s_setup, 35)
                for m in range(NB):
                    last = nc.scalar.activation(ccol[:, 2 + m:3 + m], pa[:, 0, 4 + m:5 + m],
                                                ACT.Gelu_apprx_tanh, bias=b1t[:, m:m + 1])
                last.then_inc(s_setup, 1)
                for q in range(LQ):
                    square((0, 0), 0, q)
                    if q:
                        read_fill((0, 0), 0, 2 * q - 2, None)
                        read_fill((0, 0), 0, 2 * q - 1, None)
                for n in (NFILL - 2, NFILL - 1):
                    read_fill((0, 0), 0, n, None)

            walk(act, first, retention, involution, ffn)

        @block.vector
        def _(dve):
            def ln_sum(j, kind, q):
                m = LQ * kind + q
                if kind == 0:
                    dve.wait_ge(s_xl[q], at(j, 32, 32))
                else:
                    dve.wait_ge(s_h2, at(j, NSLOT, NSLOT // LQ * (q + 1)))
                dve.wait_ge(s_norm, at(j, NORMS, m + 1 - LQ))
                nc.vector.tensor_reduce(stat(q, 0), quarter(X, q), AX.X, ALU.add).then_inc(s_sum, 1)
                dve.wait_ge(s_sum, at(j, NORMS, m + 1))
                nc.vector.tensor_scalar(st[:, q, 1, :], st[:, q, 0, :], 1.0 / D, None, ALU.mult).then_inc(s_mean, 1)

            def ln_var(j, kind, q):
                m = LQ * kind + q
                dve.wait_ge(s_sq, at(j, NORMS, m + 1))
                nc.vector.tensor_reduce(stat(q, 2), squares(kind, q), AX.X, ALU.add).then_inc(s_ss, 1)
                dve.wait_ge(s_ss, at(j, NORMS, m + 1))
                nc.vector.tensor_scalar(st[:, q, 3, :], st[:, q, 2, :], 1.0 / D, EPS, ALU.mult, ALU.add).then_inc(s_var, 1)

            def centre(j, kind, q):
                m = LQ * kind + q
                dve.wait_ge(s_mean, at(j, NORMS, m + 1))
                dve.wait_ge(s_cent, at(j, NORMS, m))
                dve.wait_ge(s_xt, at(j, 2 * NFILL, NFILL * (kind - 1) + NFILL // LQ * (q + 1)))
                nc.vector.tensor_tensor(quarter(xn, q), quarter(X, q), each_feature(stat(q, 1)),
                                        ALU.subtract).then_inc(s_cent, 1)

            def normalise(j, kind, q):
                m = LQ * kind + q
                dve.wait_ge(s_rstd, at(j, NORMS, m + 1))
                dve.wait_ge(s_norm, at(j, NORMS, m))
                nc.vector.tensor_tensor(quarter(xn, q), quarter(xn, q), each_feature(stat(q, 4)),
                                        ALU.mult).then_inc(s_norm, 1)

            def y3_mask(j, n):
                dve.wait_ge(s_yraw, at(j, NCONV, n + 1))
                r0 = n * ROWS_PER_CONV
                nc.vector.tensor_tensor(
                    y3[:, r0:r0 + ROWS_PER_CONV, :],
                    y_raw[:, n % 2, :].rearrange("p (h w) -> p h w", w=W),
                    const("ymask").unsqueeze(1).broadcast_to([128, ROWS_PER_CONV, W]),
                    ALU.mult).then_inc(s_y3, 1)

            def mask_taps(j, g, u):
                nh = rows(g)
                K = (nh + 2) * PC
                dve.wait_ge(s_gen, at(j, 2 * NG, 2 * g + u + 1))
                dve.wait_ge(s_app, at(j, NG, g - 1))
                shape = [K, nh, WB, WS]
                nc.vector.tensor_tensor(
                    taps[0:K, g % 2, u, 0:nh, :].rearrange("p h (b w) -> p h b w", w=WS),
                    ps[0:K, u, 0:nh * W].rearrange("p (h b w) -> p h b w", b=WB, w=WS),
                    const("tmask", K).rearrange("p (h w) -> p h w", w=WS)[:, 0:nh, :].unsqueeze(2).broadcast_to(shape),
                    ALU.mult).then_inc(s_taps, 1)

            def involution(j):
                for n in range(NCONV):
                    y3_mask(j, n)
                for g in range(NG):
                    for u in range(2):
                        mask_taps(j, g, u)

            def after(n):
                dve.wait_ge(s_setup, n)

            zeroed = (w1_conv[:, :], wqk_bd[:, :, :, :, :], wv_bd[:, :, :], wt[:, :, :],
                      P[:, :, :, :], gen_w[:, :, :, :], ccol[:, :])
            for a in zeroed:
                last = nc.vector.memset(a, 0.0)
            last.then_inc(s_zero, 1)
            dve.wait_ge(s_zero, 1)
            dve.wait_ge(s_cload, N_CONV_LOADS)
            dve.wait_ge(s_memz, 4)
            nc.vector.tensor_copy(c2rep[:, :].rearrange("p (u n) -> p u n", u=2)[:, :, 0:3 * YROW]
                                  .rearrange("p u (r k) -> p u r k", k=YROW),
                                  c2t[:, :].unsqueeze(1).unsqueeze(1).broadcast_to([TAPS, 2, 3, YROW]))
            nc.vector.tensor_copy(ones_b[:, :], const("ones"))
            nc.vector.tensor_copy(tri_b[:, :], const("tri")).then_inc(s_setup, 1)
            after(2)
            nc.vector.tensor_tensor(c2bd[:, :], pa[0:27, 0, 0:128], const("blocks", 27), ALU.mult).then_inc(s_setup, 1)
            after(4)
            nc.vector.tensor_copy(bnp[:, :], pa[:, 0, 0:5])
            nc.vector.tensor_scalar(bns[:, 0:1], pa[:, 0, 4:5], EPS, None, ALU.add)
            for u in range(2):
                hs = slice(64 * u, 64 * u + 64)
                nc.vector.tensor_copy(w1_conv[hs, 64 * u:64 * u + 64], pa[hs, 1, 64 * u:64 * u + 64])
                last = nc.vector.tensor_copy(gen_w[hs, u, :, :].rearrange("p r n -> p (r n)"), pv[hs, 0:3 * PR * PC])
            last.then_inc(s_setup, 1)
            chain = [(bns[:, 2:3], bnp[:, 2:3], bns[:, 1:2], ALU.mult),
                     (bns[:, 0:1], bnp[:, 0:1], bnp[:, 1:2], ALU.subtract),
                     (bns[:, 0:1], bns[:, 0:1], bns[:, 2:3], ALU.mult),
                     (bns[:, 0:1], bns[:, 0:1], bnp[:, 3:4], ALU.add),
                     (bns[:, 3:4], bns[:, 0:1], const("onerow"), ALU.add)]
            for n, (o, a, b, op) in enumerate(chain):
                after(6 + n)
                nc.vector.tensor_tensor(o, a, b, op).then_inc(s_setup, 1)

            def block_diagonals():
                for u in range(2):
                    hs = slice(64 * u, 64 * u + 64)
                    for a in range(2):
                        nc.vector.tensor_copy(wqk_bd[hs, a, u, :, :],
                                              wqkv[hs, a, :].rearrange("p (j e) -> p e j", e=2))
                    last = nc.vector.tensor_copy(wv_bd[hs, u, :], wqkv[hs, 2, :])
                last.then_inc(s_zero, 1)

            def cls_norm(n, src, dst):
                after(n)
                nc.vector.tensor_reduce(cst1[:, 0:1], src, AX.X, ALU.add).then_inc(s_setup, 1)
                after(n + 1)
                nc.vector.tensor_scalar(cst1[:, 1:2], cst1[:, 0:1], 1.0 / D, None, ALU.mult).then_inc(s_setup, 1)
                after(n + 2)
                nc.vector.tensor_scalar(dst, src, cst1[:, 1:2], None, ALU.subtract).then_inc(s_setup, 1)
                after(n + 3)
                nc.vector.scalar_tensor_tensor(ctmp, dst, 1.0, dst, ALU.mult, ALU.mult,
                                               accum_out=cst1[:, 0:1]).then_inc(s_setup, 1)
                after(n + 4)
                nc.vector.tensor_scalar(cst1[:, 2:3], cst1[:, 0:1], 1.0 / D, EPS, ALU.mult, ALU.add).then_inc(s_setup, 1)
                after(n + 6)
                nc.vector.tensor_scalar(dst, dst, cst1[:, 3:4], None, ALU.mult).then_inc(s_setup, 1)

            def class_token():
                cls_norm(11, crow, cxn)
                after(19)
                nc.vector.tensor_copy(ccol[0:64, 0:1], pa[0:64, 0, 0:1]).then_inc(s_setup, 1)
                after(21)
                nc.vector.tensor_copy(cqkv, pa[0:1, 0, 0:192])
                nc.vector.tensor_copy(ck.rearrange("p (e j) -> p e j", e=2),
                                      pa[0:1, 0, 64:128].rearrange("p (j e) -> p e j", e=2)).then_inc(s_setup, 1)
                after(22)
                nc.vector.scalar_tensor_tensor(ctmp, cqkv[:, 0:64], 1.0, cqkv[:, 64:128], ALU.mult, ALU.mult,
                                               accum_out=cst1[:, 4:5]).then_inc(s_setup, 1)
                after(24)
                nc.vector.tensor_scalar(P0[:, :], pa[:, 1, 0:64], GAMMA ** -128.0, None, ALU.mult)
                nc.vector.scalar_tensor_tensor(ch2, cqkv[:, 128:192], cst1[:, 4:5], crow,
                                               ALU.mult, ALU.add).then_inc(s_setup, 1)
                cls_norm(25, ch2, cxn2)
                after(33)
                nc.vector.tensor_copy(ccol[0:64, 1:2], pa[0:64, 0, 0:1])
                nc.vector.tensor_tensor(cbase, ch2, cxn2, ALU.add).then_inc(s_setup, 1)
                after(37)
                nc.vector.tensor_tensor(cy, pa[0:1, 0, 64:128], b2t[0:1, :], ALU.add)
                nc.vector.tensor_tensor(w_cls[:, :], pa[0:1, 1, 64:65], brt[0:1, :], ALU.add).then_inc(s_setup, 1)
                after(38)
                nc.vector.tensor_copy(wt[0:1, :, 0:1].rearrange("p u c -> p (u c)"),
                                      w_cls[:, :].broadcast_to([1, 2])).then_inc(s_setup, 1)
                after(39)

            def first():
                involution((0, 0))
                dve.wait_ge(s_load, N_SETUP_LOADS)
                block_diagonals()
                class_token()
                for q in (0, 1, 2):
                    ln_sum((0, 0), 0, q)
                ln_var((0, 0), 0, 0)
                centre((0, 0), 0, 2)
                ln_var((0, 0), 0, 1)
                ln_sum((0, 0), 0, 3)
                centre((0, 0), 0, 3)
                normalise((0, 0), 0, 0)
                ln_var((0, 0), 0, 2)
                normalise((0, 0), 0, 1)
                ln_var((0, 0), 0, 3)
                normalise((0, 0), 0, 2)
                normalise((0, 0), 0, 3)

            def rotate(j, t):
                ring = t % 2
                dve.wait_ge(s_qkv, at(j, NSLOT, t + 1))
                dve.wait_ge(s_qk, at(j, NSLOT, t - 1))
                ch = slice(2 * t, 2 * t + 2)

                def halves(a, e):
                    return a.rearrange("p (f u e n) -> p f u e n", f=4, u=2, e=2)[:, :, :, e, :]

                def table(a, n):
                    return a[:, ch, :].rearrange("p c (f n) -> p (c f) n", f=2).unsqueeze(2).broadcast_to([128, 4, n, 32])

                nc.vector.tensor_tensor(t1[:, ring, :].rearrange("p (f g n) -> p f g n", f=4, g=4),
                                        pa[:, ring, :].rearrange("p (f g n) -> p f g n", f=4, g=4),
                                        table(cos_t, 4), ALU.mult)
                nc.vector.tensor_tensor(halves(t2[:, ring, :], 0), halves(pa[:, ring, :], 1),
                                        table(sin_t, 2), ALU.mult)
                nc.vector.tensor_tensor(halves(t2[:, ring, :], 1), halves(pa[:, ring, :], 0),
                                        table(sin_t, 2), ALU.mult).then_inc(s_rot, 1)

            def states(j, t):
                dve.wait_ge(s_u, at(j, NSLOT, t + 1))
                dve.wait_ge(s_o, at(j, NSLOT, t - 3))
                for c in range(2):
                    ch = 2 * t + c
                    dve.wait_ge(s_state, at(j, CH + 1, ch + 1))
                    for u in range(2):
                        r = slice(64 * u, 64 * u + 64)
                        last = nc.vector.scalar_tensor_tensor(P[r, ch % PRING, u, :], P[r, (ch - 1) % PRING, u, :],
                                                              GAMMA ** 128.0, ps[r, 3, 64 * c:64 * c + 64],
                                                              ALU.mult, ALU.add)
                    last.then_inc(s_state, 1)

            def mask_scores(j, t):
                dve.wait_ge(s_sc, at(j, NSLOT, t + 1))
                dve.wait_ge(s_o, at(j, NSLOT, t - 1))
                nc.vector.tensor_tensor(RT[:, t % 2, :, :, :],
                                        ps[:, 0:2, 0:256].rearrange("p u (c n) -> p u c n", c=2),
                                        const("cmask").unsqueeze(1).unsqueeze(1).broadcast_to([128, 2, 2, 128]),
                                        ALU.mult).then_inc(s_ret, 1)

            def add_residual(j, t):
                dve.wait_ge(s_o, at(j, NSLOT, t + 1))
                xs = X[:, :, 2 * t:2 * t + 2, :]
                nc.vector.tensor_tensor(xs, ps[:, 2, 0:256].rearrange("p (c u d) -> p u c d", u=2, c=2), xs,
                                        ALU.add).then_inc(s_h2, 1)

            def retention(j):
                dve.wait_ge(s_o, at(j, NSLOT, 0))
                for u in range(2):
                    r = slice(64 * u, 64 * u + 64)
                    last = nc.vector.tensor_copy(P[r, PRING - 1, u, :], P0[r, :])
                last.then_inc(s_state, 1)
                for k in range(NSLOT + 3):
                    if k < NSLOT:
                        rotate(j, k)
                    if 0 <= k - 1 < NSLOT:
                        states(j, k - 1)
                    if 0 <= k - 2 < NSLOT:
                        mask_scores(j, k - 2)
                    if 0 <= k - 3 < NSLOT:
                        add_residual(j, k - 3)
                    if k >= 6 and k % 4 == 2:
                        ln_sum(j, 1, k // 4 - 1)
                    if k >= 9 and k % 4 == 1:
                        ln_var(j, 1, k // 4 - 2)
                    if is_last(j) and k >= 12 and k % 4 == 0:
                        router_sums(j, k // 4 - 3)
                if is_last(j):
                    centre(j, 1, 3)
                    router_sums(j, 2)
                    ln_var(j, 1, 3)
                    normalise(j, 1, 3)
                    router_sums(j, 3)

            def router_sums(j, q):
                dve.wait_ge(s_norm, at(j, NORMS, LQ + q + 1))
                nc.vector.tensor_tensor(quarter(yraw, q), quarter(xn, q),
                                        wr_b[:, :].unsqueeze(1).unsqueeze(1).broadcast_to([128, 2, CQ, D]),
                                        ALU.mult).then_inc(s_prod, 1)
                dve.wait_ge(s_prod, at(j, LQ, q + 1))
                nc.vector.tensor_reduce(wt[:, :, 1 + CQ * q:1 + CQ * q + CQ], quarter(yraw, q),
                                        AX.X, ALU.add).then_inc(s_w, 1)

            chained = [0]

            def link(j, ins):
                chained[0] += 1
                ins.then_inc(s_chain, 1)
                dve.wait_ge(s_chain, at(j, NCHAIN, chained[0]))

            def router_keys(j):
                chained[0] = 0
                dve.wait_ge(s_w, at(j, LQ, LQ))
                link(j, nc.vector.tensor_scalar(wt[:, :, 1:COLS], wt[:, :, 1:COLS], brt[:, 0:1], None, ALU.add))
                bits = wt[:, :, :].bitcast(i32)
                k0, k1 = key[:, 0, :, :], key[:, 1, :, :]
                link(j, nc.vector.tensor_scalar(k0, bits, 31, -2 ** 31, ALU.arith_shift_right, ALU.bitwise_or))
                link(j, nc.vector.tensor_tensor(k1, k0, bits, ALU.bitwise_xor))
                link(j, nc.vector.tensor_scalar(k0.bitcast(u32), k1.bitcast(u32), 16, None, ALU.logical_shift_right))
                link(j, nc.vector.tensor_scalar(k1, k1, 65535, None, ALU.bitwise_and))
                valid = const("valid").rearrange("p (u c) -> p u c", u=2)
                link(j, nc.vector.scalar_tensor_tensor(hi[:, :, :], k0, 1.0, valid, ALU.add, ALU.mult))

            def bc():
                return cand[:, :].unsqueeze(2).broadcast_to([128, 2, COLS])

            def low_halves(j):
                link(j, nc.vector.tensor_tensor(cmp[:, :, :], hi[:, :, :], bc(), ALU.is_equal))
                link(j, nc.vector.tensor_tensor(cmp2[:, :, :], hi[:, :, :], bc(), ALU.is_gt))
                link(j, nc.vector.scalar_tensor_tensor(lo[:, :, :], key[:, 1, :, :], 1.0, cmp[:, :, :], ALU.add, ALU.mult))
                link(j, nc.vector.scalar_tensor_tensor(lo[:, :, :], cmp2[:, :, :], 70000.0, lo[:, :, :], ALU.mult, ALU.add))

            def ask(j, op, vals):
                link(j, nc.vector.tensor_tensor(cmp[:, :, :], vals[:, :, :], bc(), op))
                with nc.allow_low_precision("counts up to COLS are exact in bfloat16"):
                    nc.vector.tensor_reduce(part[:, :], cmp[:, :, :], AX.X, ALU.add).then_inc(s_cmp, 1)

            def router_step(j, n):
                if n >= 1:
                    dve.wait_ge(s_cnt, at(j, NREQ, n))
                    got = counts(j, n - 1)
                if 1 <= n <= 32:
                    bit = 15 - (n - 1) % 16
                    link(j, nc.vector.tensor_scalar(dlt[:, :], got, float(TOPK), float(2 ** bit), ALU.is_ge, ALU.mult))
                    link(j, nc.vector.scalar_tensor_tensor(cand[:, :], dlt[:, :], -float(2 ** (bit - 1)) if bit else -1.0,
                                                           cand[:, :], ALU.add, ALU.add))
                if n == 16:
                    low_halves(j)
                if n in (0, 16):
                    link(j, nc.vector.memset(cand[:, :], 32769.0))
                if n < 32:
                    ask(j, ALU.is_ge, hi if n < 16 else lo)
                elif n == 32:
                    ask(j, ALU.is_gt, lo)
                else:
                    link(j, nc.vector.tensor_scalar(need[:, :], got, -1.0, float(TOPK), ALU.mult, ALU.add))
                    nc.vector.tensor_tensor(tie[:, :, :], lo[:, :, :], bc(), ALU.is_equal).then_inc(s_cmp, 1)

            def router_select(j):
                dve.wait_ge(s_cnt, at(j, NREQ, NREQ))
                inside, totals = pt[:, 64:64 + 2 * COLS], pt[:, 192:192 + 2 * COLS]
                for u in range(2):
                    link(j, nc.vector.tensor_tensor_scan(rank[:, u, :], const("ones")[:, 0:COLS],
                                                         totals[:, u * COLS:(u + 1) * COLS], 0.0, ALU.mult, ALU.add))
                flat = rank[:, :, :].rearrange("p u c -> p (u c)")
                link(j, nc.vector.tensor_tensor(flat, flat, totals, ALU.subtract))
                link(j, nc.vector.tensor_tensor(flat, flat, inside, ALU.add))
                link(j, nc.vector.tensor_tensor(rank[:, :, :], rank[:, :, :],
                                                need[:, :].unsqueeze(2).broadcast_to([128, 2, COLS]), ALU.is_lt))
                link(j, nc.vector.tensor_tensor(rank[:, :, :], rank[:, :, :], tie[:, :, :], ALU.mult))
                link(j, nc.vector.tensor_tensor(rank[:, :, :], rank[:, :, :], cmp[:, :, :], ALU.add))
                dve.wait_ge(s_out, at(j, NSTORED, 0))
                link(j, nc.vector.tensor_tensor(wsel[:, :, :], rank[:, :, :], wt[:, :, :], ALU.mult))
                cz = czz.rearrange("p (u d) -> p u d", u=2)
                link(j, nc.vector.tensor_tensor(cz, cy.unsqueeze(1).broadcast_to([1, 2, D]),
                                                wsel[0:1, :, 0:1].broadcast_to([1, 2, D]), ALU.mult))
                nc.vector.tensor_tensor(cz, cz, cbase.unsqueeze(1).broadcast_to([1, 2, D]), ALU.add).then_inc(s_cls, 1)
                assert chained[0] == NCHAIN, chained[0]

            def involution_and_router(j):
                jn = (j[0], j[1] - 1)
                for n in range(NCONV):
                    y3_mask(j, n)
                for g in range(NG):
                    for u in range(2):
                        mask_taps(j, g, u)
                    if g == 0:
                        ln_var(jn, 1, 3)
                    elif g <= LQ:
                        router_sums(jn, g - 1)
                    if g == LQ:
                        router_keys(jn)
                    if g >= FIRST_ASKING:
                        router_step(jn, g - FIRST_ASKING)
                router_step(jn, NEARLY)

            def ffn(j, more):
                nx = (j[0], j[1] + 1)
                sums = {NEARLY + 4 + 2 * q: q for q in range(LQ)}
                variances = {NEARLY + 9 + 2 * q: q for q in range(LQ)}
                if not more:
                    router_keys(j)
                for n in range(NEARLY + 1 if more else 0, NREQ):
                    router_step(j, n)
                    if more and n in sums:
                        ln_sum(nx, 0, sums[n])
                    if more and n in variances:
                        ln_var(nx, 0, variances[n])
                router_select(j)
                for r in range(LR):
                    dve.wait_ge(s_yb, at(j, LR, r + 1))
                    nc.vector.tensor_tensor(piece(yraw, r), piece(yraw, r),
                                            wsel[:, :, 1 + CP * r:1 + CP * r + CP].unsqueeze(3).broadcast_to([128, 2, CP, D]),
                                            ALU.mult).then_inc(s_mul, 1)
                    dve.wait_ge(s_mul, at(j, LR, r + 1))
                    dve.wait_ge(s_base, at(j, LQ, r * LQ // LR + 1))
                    nc.vector.tensor_tensor(piece(yraw, r), piece(yraw, r), piece(base, r),
                                            ALU.add).then_inc(s_fin, 1)

            walk(dve, first, retention, involution_and_router, ffn)


        @block.tensor
        def _(pe):
            mm = nc.tensor.matmul

            def conv(j, n):
                pe.wait_ge(s_yraw, at(j, NCONV, n - 1))
                pe.wait_ge(s_rot, at(j, NSLOT, 0))
                pe.wait_ge(s_blk, at(j, 2, 2))
                r0 = 1 + n * ROWS_PER_CONV
                mm(pa[:, n % 2, :].rearrange("p (h b w) -> p b h w", b=WB, w=WS), w1_conv[:, :],
                   xblk[:, :, r0:r0 + ROWS_PER_CONV, 1:WS + 1], start=True, stop=True).then_inc(s_conv, 1)

            def count(j, n):
                pe.wait_ge(s_cmp, at(j, NREQ, n + 1))
                if n < NREQ - 1:
                    mm(counts(j, n), ones_b[:, :], part[:, :], start=True, stop=True).then_inc(s_cnt, 1)
                else:
                    ties = tie[:, :, :].rearrange("p u c -> p (u c)")
                    mm(pt[:, 64:64 + 2 * COLS], tri_b[:, :], ties, start=True, stop=True)
                    mm(pt[:, 192:192 + 2 * COLS], ones_b[:, :], ties, start=True, stop=True).then_inc(s_cnt, 1)

            def fill(j, kind, n, bank):
                pe.wait_ge(s_norm, at(j, NORMS, LQ * kind + n // (NFILL // LQ) + 1))
                pe.wait_ge(s_xte, at(j, 2 * NFILL, NFILL * kind + n - (n >= 1 and bank is None)))
                dst = pa[:, n % 2, :] if bank is None else bank
                for c in range(4):
                    last = nc.tensor.transpose(dst[:, 128 * c:128 * c + 128],
                                               xn[:, 4 * n + c, :, :].rearrange("p u d -> p (u d)"), const("ident"))
                last.then_inc(s_xt, 1)

            def involution(j):
                looped = not isinstance(j[0], int)
                jn = (j[0], j[1] - 1)
                for n in range(2 if looped else 0, NCONV):
                    conv(j, n)
                pe.wait_ge(s_yraw, at(j, NCONV, NCONV))
                pe.wait_ge(s_h2, at(j, NSLOT, 0))
                pe.wait_ge(s_qkt, at(j, NSLOT, 0))
                pe.wait_ge(s_v, at(j, NSLOT, 0))
                pe.wait_ge(s_state, at(j, CH + 1, 0))
                for k in range(NG + 1):
                    if k < NG:
                        g, nh = k, rows(k)
                        K = (nh + 2) * PC
                        pe.wait_ge(s_patch, at(j, NG, g - 1))
                        for b in range(WB):
                            last = nc.tensor.transpose(p_patch[g % 2][0:K, 128 * b:128 * b + 128],
                                                       xblk[:, b, HS * g:HS * g + nh + 2, :].rearrange("p r s -> p (r s)"),
                                                       const("ident"))
                        last.then_inc(s_pt, 1)
                        pe.wait_ge(s_y3, at(j, NCONV, (HS * g + nh - 1) // ROWS_PER_CONV + 1))
                        for u in range(2):
                            pe.wait_ge(s_taps, at(j, 2 * NG, 2 * (g - 1) + u + 1))
                            dst = ps[0:K, u, 0:nh * W].rearrange("p (h w) -> p h w", w=W)
                            for rh in range(3):
                                last = mm(dst[:, rh:nh:3, :], gen_w[:, u, rh, 0:K],
                                          y3[:, HS * g + rh:HS * g + nh:3, :], start=True, stop=True)
                            last.then_inc(s_gen, 1)
                        if looped and k > FIRST_ASKING:
                            count(jn, k - 1 - FIRST_ASKING)
                        if looped and k >= NG - NFILL:
                            fill(jn, 1, k - NG + NFILL, pa[:, 1, :])
                    if k >= 1:
                        g, nh = k - 1, rows(k - 1)
                        K = (nh + 2) * PC
                        pe.wait_ge(s_patch, at(j, NG, g + 1))
                        pe.wait_ge(s_taps, at(j, 2 * NG, 2 * g + 2))
                        pe.wait_ge(s_strd, at(j, NG, g - 1))
                        for b in range(WB):
                            for u in range(2):
                                dst = ps[64 * u:64 * u + 64, 2 + g % 2, 0:nh * W].rearrange("p (h w) -> p h w", w=W)
                                last = mm(dst[:, :, WS * b:WS * b + WS], patch[0:K, g % 2, b, 64 * u:64 * u + 64],
                                          taps[0:K, g % 2, u, 0:nh, WS * b:WS * b + WS], start=True, stop=True)
                        last.then_inc(s_app, 1)
                if looped:
                    count(jn, NEARLY - 1)

            def retention(j):
                pe.wait_ge(s_gelu, at(j, NB * NQ, 0))
                pe.wait_ge(s_yev, at(j, NQ, 0))
                pe.wait_ge(s_cls, at(j, 1, 0))
                pe.wait_ge(s_strd, at(j, NG, NG))
                pe.wait_ge(s_taps, at(j, 2 * NG, 2 * NG))
                pe.wait_ge(s_patch, at(j, NG, NG))
                pe.wait_ge(s_yraw, at(j, NCONV, NCONV))
                pe.wait_ge(s_xte, at(j, 2 * NFILL, NFILL))
                for k in range(NSLOT + 3):
                    if k < NSLOT:
                        t = k
                        pe.wait_ge(s_rot, at(j, NSLOT, t - 1))
                        pe.wait_ge(s_v, at(j, NSLOT, t))
                        for c in range(2):
                            lhsT = xT[:, 2 * t + c, :]
                            mm(pa[:, t % 2, 256 * c:256 * c + 256], lhsT,
                               wqk_bd[:, :, :, :, :].rearrange("p a u e j -> p (a u e j)"), start=True, stop=True)
                            last = mm(pv[:, 128 * c:128 * c + 128], lhsT,
                                      wv_bd[:, :, :].rearrange("p u d -> p (u d)"), start=True, stop=True)
                        last.then_inc(s_qkv, 1)
                    if 0 <= k - 1 < NSLOT:
                        t = k - 1
                        pe.wait_ge(s_qk, at(j, NSLOT, t + 1))
                        pe.wait_ge(s_qkt, at(j, NSLOT, t))
                        src = qk[:, t % 2, :].rearrange("p (c a n) -> p c a n", c=2, a=2)
                        for c in range(2):
                            for a in range(2):
                                last = nc.tensor.transpose(pt[:, 128 * (2 * c + a):128 * (2 * c + a) + 128],
                                                           src[:, c, a, :], const("ident"))
                        last.then_inc(s_tr, 1)
                        pe.wait_ge(s_v, at(j, NSLOT, t + 1))
                        pe.wait_ge(s_state, at(j, CH + 1, 2 * t + 1))
                        for c in range(2):
                            for u in range(2):
                                last = mm(ps[64 * u:64 * u + 64, 3, 64 * c:64 * c + 64],
                                          src[:, c, 1, 64 * u:64 * u + 64],
                                          V[:, t % VRING, c, 64 * u:64 * u + 64], start=True, stop=True)
                        last.then_inc(s_u, 1)
                    if 0 <= k - 2 < NSLOT:
                        t = k - 2
                        pe.wait_ge(s_qkt, at(j, NSLOT, t + 1))
                        pe.wait_ge(s_ret, at(j, NSLOT, t))
                        for c in range(2):
                            for u in range(2):
                                r = slice(64 * u, 64 * u + 64)
                                last = mm(ps[:, u, 128 * c:128 * c + 128], QKT[r, t % QRING, c, 1, :],
                                          QKT[r, t % QRING, c, 0, :], start=True, stop=True)
                        last.then_inc(s_sc, 1)
                    if 0 <= k - 3 < NSLOT:
                        t = k - 3
                        pe.wait_ge(s_ret, at(j, NSLOT, t + 1))
                        pe.wait_ge(s_state, at(j, CH + 1, 2 * t + 2))
                        pe.wait_ge(s_h2, at(j, NSLOT, t))
                        for c in range(2):
                            mm(ps[:, 2, 128 * c:128 * c + 128], QKT[:, t % QRING, c, 0, :],
                               P[:, (2 * t + c - 1) % PRING, :, :].rearrange("p u d -> p (u d)"),
                               start=True, stop=False)
                            for u in range(2):
                                last = mm(ps[:, 2, 128 * c + 64 * u:128 * c + 64 * u + 64], RT[:, t % 2, u, c, :],
                                          V[:, t % VRING, c, 64 * u:64 * u + 64], start=False, stop=(u == 1))
                        last.then_inc(s_o, 1)
                    if not is_last(j) and k > NSLOT:
                        conv((j[0], j[1] + 1), k - NSLOT - 1)

            def ffn(j, more):
                pe.wait_ge(s_h2, at(j, NSLOT, NSLOT))
                pe.wait_ge(s_state, at(j, CH + 1, CH + 1))
                pe.wait_ge(s_qkt, at(j, NSLOT, NSLOT))
                if more:
                    nx = (j[0], j[1] + 1)
                    pe.wait_ge(s_strd, at(nx, NG, NG))
                    pe.wait_ge(s_taps, at(nx, 2 * NG, 2 * NG))
                    pe.wait_ge(s_yraw, at(nx, NCONV, NCONV))
                    pe.wait_ge(s_patch, at(nx, NG, NG))
                if more:
                    pe.wait_ge(s_cmp, at(j, NREQ, NEARLY + 1))
                else:
                    for n in range(NFILL):
                        fill(j, 1, n, None)
                pe.wait_ge(s_xte, at(j, 2 * NFILL, 2 * NFILL))
                asked = NEARLY if more else 0
                for k in range(NQ + 1):
                    if k < NQ:
                        for m in range(NB):
                            pe.wait_ge(s_gelu, at(j, NB * NQ, NB * (k - 2) + (m | 1) + 1))
                            mm(ps[:, 2 * (k % 2) + m // 2, 256 * (m % 2):256 * (m % 2) + 256],
                               w1_bd[:, m, :, :].rearrange("p u h -> p (u h)"),
                               xT[:, 2 * k:2 * k + 2, :].rearrange("p c l -> p (c l)"),
                               start=True, stop=True).then_inc(s_hid, 1)
                            if m % 2 and asked < NREQ:
                                count(j, asked)
                                asked += 1
                    if more and k >= NQ - NFILL and k < NQ:
                        fill(nx, 0, k - NQ + NFILL, pv[:, :])
                    if k >= 1:
                        q = k - 1
                        pe.wait_ge(s_gelu, at(j, NB * NQ, NB * q + NB))
                        pe.wait_ge(s_yev, at(j, NQ, q - 1))
                        for c in range(2):
                            if c and not more and asked < NREQ:
                                count(j, asked)
                                asked += 1
                            for m in range(NB):
                                last = mm(pa[:, q % 2, 128 * c:128 * c + 128], hid[:, q % 2, m, 128 * c:128 * c + 128],
                                          w2_bd[:, m, :, :].rearrange("p u d -> p (u d)"),
                                          start=(m == 0), stop=(m == NB - 1))
                        last.then_inc(s_y, 1)
                for n in range(asked, NREQ):
                    count(j, n)

            pe.wait_ge(s_cload, N_CONV_LOADS)
            pe.wait_ge(s_setup, 1)
            mm(pa[0:27, 0, 0:128], const("rep", TAPS), c2rep[:, :], start=True, stop=True).then_inc(s_setup, 1)
            pe.wait_ge(s_setup, 3)
            mm(pa[:, 0, 0:5], const("spread", CR), bn5[:, :], start=True, stop=True)
            for u in range(2):
                mm(pa[64 * u:64 * u + 64, 1, 64 * u:64 * u + 64], c1w[:, :], const("spread", CR)[:, 0:64],
                   start=True, stop=True)
            n = PR * PC
            for rh in range(3):
                last = mm(pv[:, n * rh:n * rh + n], c2bd[:, :], const("sel", 27)[:, n * rh:n * rh + n],
                          start=True, stop=True)
            last.then_inc(s_setup, 1)
            pe.wait_ge(s_setup, 11)

            def class_token():
                pe.wait_ge(s_yraw, at((0, 0), NCONV, NCONV))
                pe.wait_ge(s_load, N_SETUP_LOADS)
                pe.wait_ge(s_setup, 18)
                nc.tensor.transpose(pa[0:64, 0, 0:1], cxn, const("ident", 1)[:, 0:1]).then_inc(s_setup, 1)
                pe.wait_ge(s_setup, 20)
                mm(pa[0:1, 0, 0:192], ccol[0:64, 0:1], wqkv[0:64, :, :].rearrange("p a d -> p (a d)"),
                   start=True, stop=True).then_inc(s_setup, 1)
                pe.wait_ge(s_setup, 23)
                for u in range(2):
                    last = mm(pa[64 * u:64 * u + 64, 1, 0:64], ck, cqkv[:, 128:192], start=True, stop=True)
                last.then_inc(s_setup, 1)
                pe.wait_ge(s_setup, 32)
                nc.tensor.transpose(pa[0:64, 0, 0:1], cxn2, const("ident", 1)[:, 0:1]).then_inc(s_setup, 1)
                pe.wait_ge(s_setup, 34)
                for m in range(NB):
                    mm(pa[:, 0, 4 + m:5 + m], w1_bd[:, m, :, :].rearrange("p u h -> p (u h)"), ccol[:, 1:2],
                       start=True, stop=True)
                mm(pa[0:1, 1, 64:65], ccol[0:64, 1:2], wrt[:, :], start=True, stop=True).then_inc(s_setup, 1)
                pe.wait_ge(s_setup, 36)
                for m in range(NB):
                    last = mm(pa[0:1, 0, 64:128], ccol[0:64, 2 + m:3 + m], w2_bd[0:64, m, 0, :],
                              start=(m == 0), stop=(m == NB - 1))
                last.then_inc(s_setup, 1)
                pe.wait_ge(s_setup, 39)
                pe.wait_ge(s_zero, 2)
                pe.wait_ge(s_tab, 32)

            def first():
                involution((0, 0))
                class_token()
                for n in range(NFILL):
                    fill((0, 0), 0, n, None)

            walk(pe, first, retention, involution, ffn)


_INS = ['x', 'cls_tok', 'L0_tok_conv1_w', 'L0_tok_conv1_b', 'L0_tok_bn_gamma', 'L0_tok_bn_beta', 'L0_tok_bn_mean',
        'L0_tok_bn_var', 'L0_tok_conv2_w', 'L0_tok_conv2_b', 'L0_attn_W_Q', 'L0_attn_W_K', 'L0_attn_W_V',
        'L0_ffn_wr', 'L0_ffn_br', 'L0_ffn_w1', 'L0_ffn_b1', 'L0_ffn_w2', 'L0_ffn_b2']


def kernel(**inputs):
    import numpy as _np
    import concourse.bacc as _bacc
    from concourse import mybir as _mybir
    from concourse.bass_utils import run_bass_kernel_spmd as _run

    nc = _bacc.Bacc("TRN2", target_bir_lowering=False, num_devices=1)
    arrays, args = {}, []
    feeds = [(name, _np.ascontiguousarray(inputs[name])) for name in _INS]
    feeds += [("small_constants", small_constants()), ("position_tables", position_tables())]
    for name, a in feeds:
        arrays[f"in_{name}_dram"] = a
        args.append(nc.dram_tensor(f"in_{name}_dram", a.shape, _mybir.dt.from_np(a.dtype), kind="ExternalInput").ap())
    args.append(nc.dram_tensor("out_0_dram", (B, SEQ, D), _mybir.dt.float32, kind="ExternalOutput").ap())
    vit_tower(nc, *args)
    r = _run(nc, [arrays], core_ids=[0])
    return r.results[0]["out_0_dram"]
```

```python
from contextlib import ExitStack

import concourse.bass as bass
import numpy as np
from concourse import mybir

B, C, H, W = 8, 64, 64, 64
NPAIR = B // 2
CR = C // 4
TAPS = 9
SEQ = C * H + 1
D = W
CH = C * H // 128
HID = 4 * D
GAMMA = 0.96875
SCALE_BASE = 512.0
EPS = 1e-5
TOPK = max(1, int(0.5 * SEQ)) - 1

HS, WS = 5, 16
WB = W // WS
NG = -(-H // HS)
PR, PC = HS + 2, WS + 2
YROW = CR + 1
ROWS_PER_CONV = 512 // W
NCONV = H // ROWS_PER_CONV
NSLOT = CH // 2
NFILL = CH // 4
NQ = CH // 2
NB = HID // 64
LQ, CQ = 4, CH // 4
LR, CP = 8, CH // 8
COLS = CH + 1
VRING, QRING, PRING = 4, 3, 8

CONST = {}


def _layout():
    at = 0
    for name, n in (("ident", 128), ("cmask", 128), ("tri", 128), ("ones", 128), ("ymask", 64),
                    ("tmask", HS * WS), ("sel", 3 * PR * PC), ("blocks", 128),
                    ("rep", 27), ("spread", 128), ("valid", 2 * COLS), ("digits", 6),
                    ("onerow", 1)):
        CONST[name] = (at, at + n)
        at += n
    return at


NCONST = _layout()


def small_constants():
    c = np.zeros((128, NCONST), np.float32)

    def put(name, rows, a):
        s, e = CONST[name]
        c[:rows, s:e] = a.reshape(rows, e - s)

    i = np.arange(128)
    put("ident", 128, np.eye(128))
    put("cmask", 128, (i[:, None] <= i[None, :]) * GAMMA ** -128.0)
    put("tri", 128, (i[:, None] < i[None, :]) * 1.0)
    put("ones", 128, np.ones((128, 128)))
    ym = np.zeros((128, W))
    for u in range(2):
        for rw in range(3):
            r0 = 64 * u + rw * YROW
            ym[r0:r0 + YROW] = (np.arange(W) % WS % 3 == rw)
    put("ymask", 128, ym)
    tm = np.zeros((PR * PC, HS, WS))
    sel = np.zeros((27, 3, PR * PC))
    for r in range(PR):
        for s in range(PC):
            for h in range(HS):
                for w in range(WS):
                    tm[r * PC + s, h, w] = 0 <= r - h <= 2 and 0 <= s - w <= 2
            for rh in range(3):
                for rw in range(3):
                    sel[rw * TAPS + (r - rh) % 3 * 3 + (s - rw) % 3, rh, r * PC + s] = 1
    put("tmask", PR * PC, tm)
    put("sel", 27, sel)
    bl = np.zeros((27, 128))
    for rw in range(3):
        for u in range(2):
            bl[rw * TAPS:(rw + 1) * TAPS, 64 * u + rw * YROW:64 * u + (rw + 1) * YROW] = 1
    put("blocks", 27, bl)
    put("rep", TAPS, np.tile(np.eye(TAPS), 3))
    sp = np.zeros((CR, 128))
    one = np.zeros((128, 1))
    for u in range(2):
        for rw in range(3):
            for k in range(CR):
                sp[k, 64 * u + rw * YROW + k] = 1
            one[64 * u + rw * YROW + CR] = 1
    put("spread", CR, sp)
    put("onerow", 128, one)
    v = np.ones((128, 2, COLS))
    v[1:, :, 0] = 0
    put("valid", 128, v)
    put("digits", 128, np.tile(np.arange(1.0, 4.0), (128, 2)))
    return c


def position_tables():
    f = np.float32
    inv_freq = (f(1.0) / np.power(f(10000.0), np.arange(0, D, 2, dtype=f) / f(D))).astype(f)
    pos = (1 + np.arange(CH * 128)).astype(f)
    ang = (pos[:, None] * inv_freq[None, :]).astype(f).astype(np.float64)
    base = ((np.arange(0, D, 2, dtype=f) + f(0.4 * D)) / f(1.4 * D)).astype(np.float64)
    scale = base[None, :] ** (pos[:, None].astype(np.float64) / SCALE_BASE)
    step = (np.arange(CH * 128) % 128 + 1.0)[:, None]
    q = scale * GAMMA ** (step + 128)
    k = 1.0 / scale * GAMMA ** -step
    out = []
    for trig in (np.cos(ang), np.sin(ang)):
        t = np.stack([trig * q, trig * k], axis=1)
        out.append(t.reshape(CH, 128, 64).transpose(1, 0, 2))
    return np.ascontiguousarray(np.stack(out), dtype=np.float32)


def vit_tower(nc, x, cls_tok, conv1_w, conv1_b, bn_gamma, bn_beta, bn_mean, bn_var, conv2_w, conv2_b,
              W_Q, W_K, W_V, wr, br, w1, b1, w2, b2, consts, tables, out):
    bf16 = mybir.dt.bfloat16
    fp32, i32, u32 = mybir.dt.float32, mybir.dt.int32, mybir.dt.uint32
    ALU, ACT, AX = mybir.AluOpType, mybir.ActivationFunctionType, mybir.AxisListType

    with ExitStack() as ctx:
        def sb(name, shape, dt=fp32):
            return ctx.enter_context(nc.sbuf_tensor(name, shape, dt))

        def sem(name):
            return ctx.enter_context(nc.semaphore(name))

        h_dram = nc.dram_tensor("h_scratch", [B, C * H * W], fp32, kind="Internal").ap()

        cst = sb("cst", [128, NCONST])

        def const(name, rows=128):
            s, e = CONST[name]
            return cst[0:rows, s:e]

        cos_t = sb("cos_t", [128, CH, 64])
        sin_t = sb("sin_t", [128, CH, 64])
        wqkv = sb("wqkv", [128, 3, D])
        wqk_bd = sb("wqk_bd", [128, 2, 2, 2, 32])
        wv_bd = sb("wv_bd", [128, 2, D])
        wrt = sb("wrt", [D, 1])
        wr_b = sb("wr_b", [128, D])
        w1_bd = sb("w1_bd", [128, NB, 2, 64])
        w2_bd = sb("w2_bd", [128, NB, 2, D])
        b1t = sb("b1t", [128, NB])
        b2t = sb("b2t", [128, D])
        brt = sb("brt", [128, 1])
        bn5 = sb("bn5", [CR, 5])
        c1w = sb("c1w", [CR, C])
        c2t = sb("c2t", [TAPS, YROW])
        c2rep = sb("c2rep", [TAPS, 128])
        c2bd = sb("c2bd", [27, 128])
        bnp = sb("bnp", [128, 5])
        bns = sb("bns", [128, 4])
        w1_conv = sb("w1_conv", [128, 128])
        gen_w = sb("gen_w", [128, 2, 3, PR * PC])
        ones_b = sb("ones_b", [128, 128], bf16)
        tri_b = sb("tri_b", [128, 128], bf16)
        half = sb("half", [128, 2 * CQ])

        xblk = sb("xblk", [128, WB, H + 2, PC])
        scores = sb("scores", [128, 2, 512])
        y3 = sb("y3", [128, H, W])
        patch = sb("patch", [128, 2, WB, 128])
        taps = sb("taps", [128, 2, 2, HS, W])
        y_raw = taps[:, :, :, :, :].rearrange("p r u h w -> p (r u h w)")[:, 0:1024].rearrange("p (r n) -> p r n", r=2)
        strip = sb("strip", [128, 4, HS, W])

        X = sb("X", [128, 2, CH, D])
        xn = sb("xn", [128, CH, 2, D])
        base = sb("base", [128, 2, CH, D])
        yraw = sb("yraw", [128, 2, CH, D])
        xT = sb("xT", [128, CH, 128])
        sq = sb("sq", [128, CH, D])
        st = sb("st", [128, LQ, 5, 2 * CQ])

        def quarter(a, q):
            return a[:, CQ * q:CQ * q + CQ, :, :].rearrange("p c u d -> p u c d") if a is xn \
                else a[:, :, CQ * q:CQ * q + CQ, :]

        def piece(a, r):
            return a[:, :, CP * r:CP * r + CP, :]

        def squares(kind, q):
            if kind:
                return quarter(yraw, q)
            return sq[:, 2 * CQ * (q % 2):2 * CQ * (q % 2) + 2 * CQ, :].rearrange("p (u c) d -> p u c d", u=2)

        def stat(q, n):
            return st[:, q, n, :].rearrange("p (u c) -> p u c", u=2)

        def each_feature(a):
            return a.unsqueeze(3).broadcast_to([128, 2, CQ, D])
        terms = sb("terms", [128, 4, 512])
        t1, t2 = (terms[:, :, :].rearrange("p (r t) n -> p r t n", t=2)[:, :, n, :] for n in range(2))
        qk = sb("qk", [128, 2, 512])
        cmp3 = qk[:, 0, 0:6 * COLS].rearrange("p (u k c) -> p u k c", u=2, k=3)
        V = sb("V", [128, VRING, 2, 128])
        QKT = sb("QKT", [128, QRING, 2, 2, 128])
        RT = scores[:, :, :].rearrange("p r (u c n) -> p r u c n", u=2, c=2)
        P = sb("P", [128, PRING, 2, D])
        P0 = sb("P0", [128, D])
        hid = terms[:, :, :].rearrange("p (k m) (b n) -> p k (m b) n", m=2, b=2)

        cl = sb("cl", [1, 832])
        crow, cxn, ctmp, cqkv, ck, ch2, cxn2, cy, cbase, czz = (cl[:, a:b] for a, b in (
            (0, 64), (64, 128), (128, 192), (192, 384), (384, 448), (448, 512), (512, 576), (576, 640),
            (640, 704), (704, 832)))
        cst1 = sb("cst1", [1, 8])
        ccol = sb("ccol", [128, 2 + NB])
        w_cls = sb("w_cls", [1, 1])

        wt = sb("wt", [128, 2, COLS])
        key = sb("key", [128, 2, 2, COLS], i32)
        hi = sb("hi", [128, 2, COLS])
        lo = sb("lo", [128, 2, COLS])
        cmp = sb("cmp", [128, 2, COLS])
        tie = sb("tie", [128, 2, COLS], bf16)
        part = sb("part", [128, 2, 3], bf16)
        cand = sb("cand", [128, 2])
        thr = sb("thr", [128, 2, 3])
        dlt = sb("dlt", [128, 2, 3])
        digit = sb("digit", [128, 2])
        need = sb("need", [128, 2])
        wsel = sb("wsel", [128, 2, COLS])
        rank = sb("rank", [128, 2, COLS])
        cmp2 = rank

        pa = ctx.enter_context(nc.psum_tensor("pa", [128, 2, 512], fp32))
        pv = ctx.enter_context(nc.psum_tensor("pv", [128, 512], fp32))
        pt = ctx.enter_context(nc.psum_tensor("pt", [128, 512], fp32))
        ps = ctx.enter_context(nc.psum_tensor("ps", [128, 4, 512], fp32))
        p_patch = (pv, pt)

        s_load, s_cload, s_tab = sem("weights_loaded"), sem("conv_weights_loaded"), sem("tables_loaded")
        s_x, s_out = sem("image_loaded"), sem("stored")
        s_x_first = sem("first_half_image_loaded")
        s_xl = [sem(f"tokens_loaded{q}") for q in range(LQ)]
        s_strip = [sem(f"strip_stored{n}") for n in range(4)]
        s_setup, s_gen_w = sem("setup_step"), sem("tap_weights_ready")
        s_pad, s_blk = sem("image_padding_zero"), sem("image_cut")
        s_memz, s_zero = sem("weights_zeroed"), sem("tiles_zeroed")
        s_conv, s_yraw = sem("conv1_done"), sem("relu_done")
        s_y3 = sem("y3_ready")
        s_pt, s_patch = sem("patch_transposed"), sem("patch_ready")
        s_gen, s_taps = sem("taps_made"), sem("taps_masked")
        s_app, s_strd = sem("involution_done"), sem("strip_ready")
        s_sum, s_mean, s_cent, s_sq, s_ss, s_var, s_rstd, s_norm = (sem("ln_" + n) for n in (
            "sum", "mean", "centred", "squared", "square_sum", "variance", "rstd", "normed"))
        s_base = sem("base_ready")
        s_xt, s_xte = sem("tokens_transposed"), sem("xT_ready")
        s_qkv, s_rot, s_qk, s_v = sem("qkv_done"), sem("rotated"), sem("qk_ready"), sem("v_ready")
        s_tr, s_qkt, s_u, s_state = sem("qk_transposed"), sem("qkt_ready"), sem("kv_done"), sem("state_ready")
        s_sc, s_ret, s_o, s_h2 = sem("scores_done"), sem("ret_ready"), sem("retention_done"), sem("h2_ready")
        s_prod, s_w = sem("router_products"), sem("router_sums")
        s_cmp, s_cnt, s_chain = sem("count_asked"), sem("count_done"), sem("router_step")
        s_hid, s_gelu, s_y, s_yev = sem("hidden_done"), sem("gelu_done"), sem("ffn_done"), sem("ffn_read")
        s_yb, s_mul, s_fin, s_cls = sem("ffn_biased"), sem("ffn_weighted"), sem("result_ready"), sem("cls_result_ready")

        counting = [s_x, *s_xl, s_out, *s_strip, s_blk, s_conv, s_yraw, s_y3, s_pt, s_patch, s_gen, s_taps, s_app,
                    s_strd, s_sum, s_mean, s_cent, s_sq, s_ss, s_var, s_rstd, s_norm, s_base, s_xt, s_xte, s_qkv,
                    s_rot, s_qk, s_v, s_tr, s_qkt, s_u, s_state, s_sc, s_ret, s_o, s_h2, s_prod, s_w, s_cmp, s_cnt,
                    s_chain, s_hid, s_gelu, s_y, s_yev, s_yb, s_mul, s_fin, s_cls]

        def at(j, per_pair, n):
            reg, add = j
            return reg * per_pair + (1 + max(n + add * per_pair, 0)) if not isinstance(reg, int) \
                else 1 + max((reg + add) * per_pair + n, 0)

        def is_last(j):
            return isinstance(j[0], int) and j[0] == NPAIR - 1

        def counts(j, n):
            bank = pa[:, 0, :] if n < NEARLY and not isinstance(j[0], int) else pt
            return bank[:, 6 * (n % 2):6 * (n % 2) + 6].rearrange("p (u k) -> p u k", k=3)

        def pair(j):
            return j[0] + j[1]

        def rows(g):
            return min(HS, H - HS * g)

        N_SETUP_LOADS = 16 * 17
        N_CONV_LOADS = 16 * 9
        NORMS = 2 * LQ
        NSTORED = 16 * (2 * LQ + 2)
        NDIG = 8
        NREQ = 2 * NDIG + 2
        NCHAIN = 103
        NEARLY = 5
        FIRST_ASKING = NG - NEARLY
        SUM_STRIPS = (1, 2, 4, 7)
        TWICE, LATE = 9, 4
        LATE_FILLS = {1: 4, 2: 5, 5: 6, 6: 7}
        block = ctx.enter_context(nc.Block())

        def walk(eng, first, retention, involution, ffn):
            first()
            with eng.Fori(0, NPAIR - 1) as i:
                retention((i, 0))
                involution((i, 1))
                ffn((i, 0), True)
            retention((NPAIR - 1, 0))
            ffn((NPAIR - 1, 0), False)

        @block.sync
        def _(sp):
            loads = [0]

            def load(dst, src):
                loads[0] += 1
                sp.dma_start(dst, src).then_inc(s_load, 16)

            def load_image(j, buffers=(sq, sq)):
                sp.wait_ge(s_ss, at((j[0], j[1] - 1), NORMS, LQ))
                for n, dst in enumerate(buffers):
                    if dst is sq:
                        sp.wait_ge(s_blk, at(j, 2, n))
                    src = x[bass.ds(pair(j) * 2, 2), :, H // 2 * n:H // 2 * (n + 1), :]
                    signal = s_x_first if n == 0 and isinstance(j[0], int) else s_x
                    sp.dma_start(dst[:, :, :], src.rearrange("b c h w -> (b c) h w")).then_inc(signal, 16)
                    if signal is s_x_first:
                        for i, a in enumerate((conv1_b, bn_mean, bn_gamma, bn_beta)):
                            sp.dma_start(bn5[:, i:i + 1], a.rearrange("(p a) -> p a", a=1)).then_inc(s_cload, 16)

            def store_strips(j):
                for g in range(NG):
                    nh = rows(g)
                    sp.wait_ge(s_strd, at(j, NG, g + 1))
                    dst = h_dram[bass.ds(pair(j) * 2, 2), :].rearrange("b (c n) -> (b c) n", c=C)
                    sp.dma_start(dst[:, g * HS * W:(g * HS + nh) * W],
                                 strip[:, g % 4, 0:nh, :].rearrange("p h w -> p (h w)")).then_inc(s_strip[g % 4], 16)

            def load_tokens(j):
                for n in range(4):
                    per = 16 * len(range(n, NG, 4))
                    sp.wait_ge(s_strip[n], at(j, per, per))
                sp.wait_ge(s_base, at(j, LQ, 0))
                for q in range(LQ):
                    cs = slice(CQ * q, CQ * q + CQ)
                    for u in range(2):
                        src = h_dram[bass.ds(pair(j) * 2 + u, 1), :].rearrange("a (c l d) -> l (a c) d", l=128, d=D)
                        sp.dma_start(X[:, u, cs, :], src[:, cs, :]).then_inc(s_xl[q], 16)

            def store_result(j):
                for q in range(LQ):
                    sp.wait_ge(s_fin, at(j, LR, LR // LQ * (q + 1)))
                    cs = slice(CQ * q, CQ * q + CQ)
                    for u in range(2):
                        dst = out[bass.ds(pair(j) * 2 + u, 1), 1:SEQ, :].rearrange("a (c l) d -> l (a c) d", l=128)
                        sp.dma_start(dst[:, cs, :], yraw[:, u, cs, :]).then_inc(s_out, 16)

            load_image((0, 0), (sq, yraw[:, 0, :, :]))
            sp.wait_ge(s_memz, 4)
            for u in range(2):
                hs = slice(64 * u, 64 * u + 64)
                for n, a in enumerate((W_Q, W_K, W_V)):
                    load(wqkv[hs, n, :], a)
                load(w1_bd[hs, :, u, :], w1.rearrange("d (b h) -> d b h", h=64))
                load(w2_bd[hs, :, u, :], w2.rearrange("(b h) d -> h b d", h=64))
                with nc.allow_non_contiguous_dma("256 biases, once"):
                    load(b1t[hs, :], b1.rearrange("(b h) -> h b", h=64))
            load(wrt[:, :], wr)
            load(wr_b[:, :], wr.rearrange("d a -> (a d)").partition_broadcast(128))
            load(b2t[:, :], b2.partition_broadcast(128))
            load(brt[:, :], br.partition_broadcast(128))
            load(crow, cls_tok[0, :, :])
            assert 16 * loads[0] == N_SETUP_LOADS
            for n, tab in enumerate((cos_t, sin_t)):
                sp.dma_start(tab[:, :, :], tables[n, :, :, :]).then_inc(s_tab, 16)

            def first():
                store_strips((0, 0))
                load_tokens((0, 0))

            def ffn(j, more):
                if more:
                    load_tokens((j[0], j[1] + 1))
                store_result(j)

            def retention(j):
                if not isinstance(j[0], int):
                    load_image((j[0], j[1] + 1))

            walk(sp, first, retention, store_strips, ffn)
            sp.wait_ge(s_out, at((0, NPAIR), NSTORED, 0))

        @block.gpsimd
        def _(pool):
            def centre(j, kind, q):
                m = LQ * kind + q
                pool.wait_ge(s_mean, at(j, NORMS, m + 1))
                pool.wait_ge(s_xt, at(j, 2 * NFILL, NFILL * (kind - 1) + NFILL // LQ * (q + 1)))
                if kind == 0:
                    pool.wait_ge(s_w, at(j, LQ, 0))
                nc.gpsimd.tensor_tensor(quarter(xn, q), quarter(X, q), each_feature(stat(q, 1)),
                                        ALU.subtract).then_inc(s_cent, 1)

            def root(j, kind, q):
                pool.wait_ge(s_var, at(j, NORMS, LQ * kind + q + 1))
                nc.gpsimd.tensor_tensor(st[:, q, 4, :], st[:, q, 3, :], half[:, 0:2 * CQ], ALU.pow).then_inc(s_rstd, 1)

            def normalise(j, kind, q):
                pool.wait_ge(s_rstd, at(j, NORMS, LQ * kind + q + 1))
                nc.gpsimd.tensor_tensor(quarter(xn, q), quarter(xn, q), each_feature(stat(q, 4)),
                                        ALU.mult).then_inc(s_norm, 1)

            def router_product(j, q):
                pool.wait_ge(s_norm, at(j, NORMS, LQ + q + 1))
                pool.wait_ge(s_ss, at(j, NORMS, LQ + q + 1))
                nc.gpsimd.tensor_tensor(quarter(yraw, q), quarter(xn, q),
                                        wr_b[:, :].unsqueeze(1).unsqueeze(1).broadcast_to([128, 2, CQ, D]),
                                        ALU.mult).then_inc(s_prod, 1)

            def base_quarter(j, q):
                pool.wait_ge(s_norm, at(j, NORMS, LQ + q + 1))
                pool.wait_ge(s_fin, at(j, LR, 0))
                nc.gpsimd.tensor_tensor(quarter(base, q), quarter(X, q), quarter(xn, q), ALU.add).then_inc(s_base, 1)

            def add_terms(j, t):
                pool.wait_ge(s_rot, at(j, NSLOT, t + 1))
                pool.wait_ge(s_u, at(j, NSLOT, t - 1))
                o, a, b = (v.rearrange("p (f e n) -> p f e n", e=2, n=32)
                           for v in (qk[:, t % 2, :], t1[:, t % 2, :], t2[:, t % 2, :]))
                nc.gpsimd.tensor_tensor(o[:, :, 0, :], a[:, :, 0, :], b[:, :, 0, :], ALU.subtract)
                nc.gpsimd.tensor_tensor(o[:, :, 1, :], a[:, :, 1, :], b[:, :, 1, :], ALU.add).then_inc(s_qk, 1)

            def bias(j, r):
                pool.wait_ge(s_yev, at(j, NQ, NQ // LR * (r + 1)))
                nc.gpsimd.tensor_tensor(piece(yraw, r), piece(yraw, r),
                                        b2t[:, :].unsqueeze(1).unsqueeze(1).broadcast_to([128, 2, CP, D]),
                                        ALU.add).then_inc(s_yb, 1)

            for s in counting:
                pool.sem_inc(s, 1)
            pool.sem_inc(s_x, 16)
            for border in (xblk[:, :, 0, :], xblk[:, :, H + 1, :],
                           xblk[:, 0, 1:H + 1, 0:1], xblk[:, WB - 1, 1:H + 1, PC - 1:PC]):
                nc.gpsimd.memset(border, 0.0).then_inc(s_pad, 1)
            nc.gpsimd.memset(w1_bd[:, :, :, :], 0.0).then_inc(s_memz, 1)
            nc.gpsimd.memset(w2_bd[:, :, :, :], 0.0).then_inc(s_memz, 1)
            nc.gpsimd.memset(half[:, :], -0.5).then_inc(s_memz, 1)
            nc.gpsimd.memset(c2rep[:, :], 0.0).then_inc(s_memz, 1)
            pool.wait_ge(s_memz, 4)
            pool.wait_ge(s_setup, 5)
            nc.gpsimd.tensor_tensor(bns[:, 1:2], bns[:, 0:1], half[:, 0:1], ALU.pow).then_inc(s_setup, 1)

            def first():
                for n in (16, 30):
                    pool.wait_ge(s_setup, n)
                    nc.gpsimd.tensor_tensor(cst1[:, 3:4], cst1[:, 2:3], half[0:1, 0:1], ALU.pow).then_inc(s_setup, 1)
                centre((0, 0), 0, 0)
                centre((0, 0), 0, 1)
                for q in range(LQ):
                    root((0, 0), 0, q)
                add_terms((0, 0), 0)

            def retention(j):
                for t in range(NSLOT):
                    if t:
                        add_terms(j, t)
                    if t >= 7 and t % 4 == 3:
                        centre(j, 1, t // 4 - 1)
                    if t == 10 or t == 14:
                        root(j, 1, t // 4 - 2)
                    if t == 12:
                        normalise(j, 1, 0)
                normalise(j, 1, 1)
                if is_last(j):
                    root(j, 1, 2)
                    normalise(j, 1, 2)
                    root(j, 1, 3)
                    for q in range(LQ):
                        router_product(j, q)
                    for q in range(LQ):
                        base_quarter(j, q)

            def involution(j):
                jn = (j[0], j[1] - 1)
                router_product(jn, 0)
                router_product(jn, 1)
                root(jn, 1, 2)
                normalise(jn, 1, 2)
                router_product(jn, 2)
                base_quarter(jn, 0)
                base_quarter(jn, 1)
                root(jn, 1, 3)
                normalise(jn, 1, 3)
                router_product(jn, 3)
                base_quarter(jn, 2)
                base_quarter(jn, 3)

            def ffn(j, more):
                nx = (j[0], j[1] + 1)
                if more:
                    for q in (0, 1, 2):
                        centre(nx, 0, q)
                    root(nx, 0, 0)
                    normalise(nx, 0, 0)
                    for q in (1, 2, 3):
                        root(nx, 0, q)
                        normalise(nx, 0, q)
                for r in range(LR):
                    if more and r == LR - 1:
                        add_terms(nx, 0)
                    bias(j, r)

            walk(pool, first, retention, involution, ffn)

        @block.scalar
        def _(act):
            def cut_image(j, n, b):
                if b == 0:
                    act.wait_ge(s_app, at(j, NG, 0))
                    if n == 0 and isinstance(j[0], int):
                        act.wait_ge(s_x_first, 16)
                    else:
                        act.wait_ge(s_x, at(j, 32, 16 * (n + 1)))
                r0 = 1 + H // 2 * n
                first_col, last_col = max(WS * b - 1, 0), min(WS * b + WS + 1, W)
                d0 = first_col - (WS * b - 1)
                src = yraw[:, 0, :, :] if n == 1 and isinstance(j[0], int) else sq
                last = nc.scalar.activation(xblk[:, b, r0:r0 + H // 2, d0:d0 + last_col - first_col],
                                            src[:, :, first_col:last_col], ACT.Copy)
                if b == WB - 1:
                    last.then_inc(s_blk, 1)

            def relus(j, ns=range(NCONV)):
                for n in ns:
                    act.wait_ge(s_conv, at(j, NCONV, n + 1))
                    act.wait_ge(s_y3, at(j, NCONV, n - 1))
                    if n == 0:
                        act.wait_ge(s_app, at(j, NG, 0))
                    nc.scalar.activation(y_raw[:, n % 2, :], pa[:, n % 2, :], ACT.Relu,
                                         bias=bns[:, 3:4], scale=bns[:, 2:3]).then_inc(s_yraw, 1)

            def involution(j, norm2=True):
                if norm2:
                    relus(j)
                for g in range(NG + 1):
                    if norm2 and g == 2:
                        square((j[0], j[1] - 1), 1, 3)
                    if g < NG:
                        K = (rows(g) + 2) * PC
                        act.wait_ge(s_pt, at(j, NG, g + 1))
                        act.wait_ge(s_app, at(j, NG, g - 1))
                        nc.scalar.activation(patch[0:K, g % 2, :, :].rearrange("p b c -> p (b c)"),
                                             p_patch[g % 2][0:K, :], ACT.Copy).then_inc(s_patch, 1)
                        if norm2 and g >= NG - NFILL:
                            read_fill((j[0], j[1] - 1), 1, g - NG + NFILL, pa[:, 1, :])
                    if g >= 1:
                        q = g - 1
                        nh = rows(q)
                        act.wait_ge(s_app, at(j, NG, q + 1))
                        act.wait_ge(s_strip[q % 4], at(j, 16 * len(range(q % 4, NG, 4)), 16 * (q // 4)))
                        nc.scalar.activation(strip[:, q % 4, 0:nh, :].rearrange("p h w -> p (h w)"),
                                             ps[:, 2 + q % 2, 0:nh * W], ACT.Copy).then_inc(s_strd, 1)

            def square(j, kind, q):
                m = LQ * kind + q
                act.wait_ge(s_cent, at(j, NORMS, m + 1))
                if kind:
                    act.wait_ge(s_out, at(j, NSTORED, 0))
                else:
                    act.wait_ge(s_blk, at(j, 2, 2))
                    act.wait_ge(s_ss, at(j, NORMS, m - 1))
                nc.scalar.activation(squares(kind, q), quarter(xn, q), ACT.Square).then_inc(s_sq, 1)

            def read_v(j, t):
                act.wait_ge(s_qkv, at(j, NSLOT, t + 1))
                act.wait_ge(s_o, at(j, NSLOT, t - VRING + 1))
                nc.scalar.activation(V[:, t % VRING, :, :].rearrange("p c d -> p (c d)"),
                                     pv[:, 0:256], ACT.Copy).then_inc(s_v, 1)

            def read_fill(j, kind, n, bank):
                act.wait_ge(s_xt, at(j, 2 * NFILL, NFILL * kind + n + 1))
                if kind:
                    act.wait_ge(s_qkv, at(j, NSLOT, NSLOT))
                else:
                    act.wait_ge(s_hid, at((j[0], j[1] - 1), NB * NQ, NB * (2 * n + 2)))
                nc.scalar.activation(xT[:, 4 * n:4 * n + 4, :].rearrange("p c l -> p (c l)"),
                                     bank, ACT.Copy).then_inc(s_xte, 1)

            def retention(j):
                for k in range(NSLOT + 1):
                    for n, first_slot in enumerate((5, 11)):
                        if not isinstance(j[0], int) and 0 <= k - first_slot < WB:
                            cut_image((j[0], j[1] + 1), n, k - first_slot)
                    if 1 <= k < NSLOT:
                        read_v(j, k)
                    if k >= 1:
                        t = k - 1
                        act.wait_ge(s_tr, at(j, NSLOT, t + 1))
                        act.wait_ge(s_o, at(j, NSLOT, t - QRING + 1))
                        nc.scalar.activation(QKT[:, t % QRING, :, :, :].rearrange("p c a l -> p (c a l)"),
                                             pt[:, :], ACT.Copy).then_inc(s_qkt, 1)
                    if k >= 8 and k % 4 == 0:
                        square(j, 1, k // 4 - 2)
                if is_last(j):
                    square(j, 1, 3)

            def ffn(j, more):
                if not more:
                    for n in range(NFILL // 2):
                        read_fill(j, 1, n, pa[:, n % 2, :])
                for k in range(NQ + 1):
                    if more and 4 <= k < 4 + LQ:
                        square((j[0], j[1] + 1), 0, k - 4)
                    if k < NQ:
                        for m in range(NB):
                            act.wait_ge(s_hid, at(j, NB * NQ, NB * k + (m | 1) + 1))
                            act.wait_ge(s_y, at(j, NQ, k - 1))
                            nc.scalar.activation(hid[:, k % 2, m, :],
                                                 ps[:, 2 * (k % 2) + m // 2, 256 * (m % 2):256 * (m % 2) + 256],
                                                 ACT.Gelu_apprx_tanh, bias=b1t[:, m:m + 1]).then_inc(s_gelu, 1)
                    if more and k >= NQ - NFILL and k < NQ:
                        read_fill((j[0], j[1] + 1), 0, k - NQ + NFILL, pv[:, :])
                    if not more and k in LATE_FILLS:
                        read_fill(j, 1, LATE_FILLS[k], pv[:, :])
                    if k >= 1:
                        q = k - 1
                        act.wait_ge(s_y, at(j, NQ, q + 1))
                        act.wait_ge(s_out, at(j, NSTORED, 0))
                        act.wait_ge(s_w, at(j, LQ, LQ))
                        nc.scalar.activation(yraw[:, :, 2 * q:2 * q + 2, :],
                                             pa[:, q % 2, 0:256].rearrange("p (c u d) -> p u c d", c=2, u=2),
                                             ACT.Copy).then_inc(s_yev, 1)
                    if more and k == NQ - 1:
                        read_v((j[0], j[1] + 1), 0)
                act.wait_ge(s_cls, at(j, 1, 1))
                for u in range(2):
                    act.dma_start(out[bass.ds(pair(j) * 2 + u, 1), 0, :], czz[:, D * u:D * u + D]).then_inc(s_out, 16)

            act.dma_start(cst[:, :], consts).then_inc(s_cload, 16)
            act.dma_start(bn5[:, 4:5], bn_var.rearrange("(p a) -> p a", a=1)).then_inc(s_cload, 16)
            act.dma_start(c1w[:, :], conv1_w).then_inc(s_cload, 16)
            act.dma_start(c2t[:, 0:CR], conv2_w).then_inc(s_cload, 16)
            act.dma_start(c2t[:, CR:YROW], conv2_b.rearrange("(p a) -> p a", a=1)).then_inc(s_cload, 16)
            act.wait_ge(s_pad, 4)
            for b in range(WB):
                cut_image((0, 0), 0, b)
            def first():
                for b in range(WB):
                    cut_image((0, 0), 1, b)
                act.wait_ge(s_setup, 11)
                relus((0, 0))
                involution((0, 0), norm2=False)
                act.wait_ge(s_setup, 35)
                for m in range(NB):
                    last = nc.scalar.activation(ccol[:, 2 + m:3 + m], pa[:, 0, 4 + m:5 + m],
                                                ACT.Gelu_apprx_tanh, bias=b1t[:, m:m + 1])
                last.then_inc(s_setup, 1)
                for q in range(LQ):
                    square((0, 0), 0, q)
                for n in range(NFILL):
                    read_fill((0, 0), 0, n, ps[:, n % 4, :])
                    if n == NFILL - 3:
                        read_v((0, 0), 0)

            walk(act, first, retention, involution, ffn)

        @block.vector
        def _(dve):
            def ln_sum(j, kind, q):
                m = LQ * kind + q
                if kind == 0:
                    dve.wait_ge(s_xl[q], at(j, 32, 32))
                else:
                    dve.wait_ge(s_h2, at(j, NSLOT, NSLOT // LQ * (q + 1)))
                dve.wait_ge(s_norm, at(j, NORMS, m + 1 - LQ))
                nc.vector.tensor_reduce(stat(q, 0), quarter(X, q), AX.X, ALU.add).then_inc(s_sum, 1)
                dve.wait_ge(s_sum, at(j, NORMS, m + 1))
                nc.vector.tensor_scalar(st[:, q, 1, :], st[:, q, 0, :], 1.0 / D, None, ALU.mult).then_inc(s_mean, 1)

            def ln_var(j, kind, q):
                m = LQ * kind + q
                dve.wait_ge(s_sq, at(j, NORMS, m + 1))
                nc.vector.tensor_reduce(stat(q, 2), squares(kind, q), AX.X, ALU.add).then_inc(s_ss, 1)
                dve.wait_ge(s_ss, at(j, NORMS, m + 1))
                nc.vector.tensor_scalar(st[:, q, 3, :], st[:, q, 2, :], 1.0 / D, EPS, ALU.mult, ALU.add).then_inc(s_var, 1)

            def centre(j, kind, q):
                m = LQ * kind + q
                dve.wait_ge(s_mean, at(j, NORMS, m + 1))
                dve.wait_ge(s_cent, at(j, NORMS, m))
                dve.wait_ge(s_xt, at(j, 2 * NFILL, NFILL * (kind - 1) + NFILL // LQ * (q + 1)))
                if kind == 0:
                    dve.wait_ge(s_base, at(j, LQ, 0))
                nc.vector.tensor_tensor(quarter(xn, q), quarter(X, q), each_feature(stat(q, 1)),
                                        ALU.subtract).then_inc(s_cent, 1)

            def normalise(j, kind, q):
                m = LQ * kind + q
                dve.wait_ge(s_rstd, at(j, NORMS, m + 1))
                dve.wait_ge(s_norm, at(j, NORMS, m))
                nc.vector.tensor_tensor(quarter(xn, q), quarter(xn, q), each_feature(stat(q, 4)),
                                        ALU.mult).then_inc(s_norm, 1)

            def y3_mask(j, n):
                dve.wait_ge(s_yraw, at(j, NCONV, n + 1))
                r0 = n * ROWS_PER_CONV
                nc.vector.tensor_tensor(
                    y3[:, r0:r0 + ROWS_PER_CONV, :],
                    y_raw[:, n % 2, :].rearrange("p (h w) -> p h w", w=W),
                    const("ymask").unsqueeze(1).broadcast_to([128, ROWS_PER_CONV, W]),
                    ALU.mult).then_inc(s_y3, 1)

            def mask_taps(j, g, u):
                nh = rows(g)
                K = (nh + 2) * PC
                dve.wait_ge(s_gen, at(j, 2 * NG, 2 * g + u + 1))
                if g == 0:
                    dve.wait_ge(s_y3, at(j, NCONV, NCONV))
                dve.wait_ge(s_app, at(j, NG, g - 1))
                shape = [K, nh, WB, WS]
                nc.vector.tensor_tensor(
                    taps[0:K, g % 2, u, 0:nh, :].rearrange("p h (b w) -> p h b w", w=WS),
                    ps[0:K, u, 0:nh * W].rearrange("p (h b w) -> p h b w", b=WB, w=WS),
                    const("tmask", K).rearrange("p (h w) -> p h w", w=WS)[:, 0:nh, :].unsqueeze(2).broadcast_to(shape),
                    ALU.mult).then_inc(s_taps, 1)

            def involution(j):
                for n in range(NCONV):
                    y3_mask(j, n)
                for g in range(NG):
                    for u in range(2):
                        mask_taps(j, g, u)

            def after(n):
                dve.wait_ge(s_setup, n)

            zeroed = (w1_conv[:, :], wqk_bd[:, :, :, :, :], wv_bd[:, :, :], wt[:, :, :],
                      P[:, :, :, :], gen_w[:, :, :, :], ccol[:, :])
            for a in zeroed:
                last = nc.vector.memset(a, 0.0)
            last.then_inc(s_zero, 1)
            dve.wait_ge(s_zero, 1)
            dve.wait_ge(s_cload, N_CONV_LOADS)
            dve.wait_ge(s_memz, 4)
            nc.vector.tensor_copy(c2rep[:, :].rearrange("p (u n) -> p u n", u=2)[:, :, 0:3 * YROW]
                                  .rearrange("p u (r k) -> p u r k", k=YROW),
                                  c2t[:, :].unsqueeze(1).unsqueeze(1).broadcast_to([TAPS, 2, 3, YROW]))
            nc.vector.tensor_copy(ones_b[:, :], const("ones"))
            nc.vector.tensor_copy(tri_b[:, :], const("tri")).then_inc(s_setup, 1)
            after(2)
            nc.vector.tensor_tensor(c2bd[:, :], pa[0:27, 0, 0:128], const("blocks", 27), ALU.mult).then_inc(s_setup, 1)
            after(4)
            nc.vector.tensor_copy(bnp[:, :], pa[:, 0, 0:5])
            nc.vector.tensor_scalar(bns[:, 0:1], pa[:, 0, 4:5], EPS, None, ALU.add)
            for u in range(2):
                hs = slice(64 * u, 64 * u + 64)
                last = nc.vector.tensor_copy(w1_conv[hs, 64 * u:64 * u + 64], pa[hs, 1, 64 * u:64 * u + 64])
            last.then_inc(s_setup, 1)
            chain = [(bns[:, 2:3], bnp[:, 2:3], bns[:, 1:2], ALU.mult),
                     (bns[:, 0:1], bnp[:, 0:1], bnp[:, 1:2], ALU.subtract),
                     (bns[:, 0:1], bns[:, 0:1], bns[:, 2:3], ALU.mult),
                     (bns[:, 0:1], bns[:, 0:1], bnp[:, 3:4], ALU.add),
                     (bns[:, 3:4], bns[:, 0:1], const("onerow"), ALU.add)]
            for n, (o, a, b, op) in enumerate(chain):
                after(6 + n)
                nc.vector.tensor_tensor(o, a, b, op).then_inc(s_setup, 1)
            for u in range(2):
                hs = slice(64 * u, 64 * u + 64)
                last = nc.vector.tensor_copy(gen_w[hs, u, :, :].rearrange("p r n -> p (r n)"), pv[hs, 0:3 * PR * PC])
            last.then_inc(s_gen_w, 1)

            def block_diagonals():
                for u in range(2):
                    hs = slice(64 * u, 64 * u + 64)
                    for a in range(2):
                        nc.vector.tensor_copy(wqk_bd[hs, a, u, :, :],
                                              wqkv[hs, a, :].rearrange("p (j e) -> p e j", e=2))
                    last = nc.vector.tensor_copy(wv_bd[hs, u, :], wqkv[hs, 2, :])
                last.then_inc(s_zero, 1)

            def cls_norm(n, src, dst):
                after(n)
                nc.vector.tensor_reduce(cst1[:, 0:1], src, AX.X, ALU.add).then_inc(s_setup, 1)
                after(n + 1)
                nc.vector.tensor_scalar(cst1[:, 1:2], cst1[:, 0:1], 1.0 / D, None, ALU.mult).then_inc(s_setup, 1)
                after(n + 2)
                nc.vector.tensor_scalar(dst, src, cst1[:, 1:2], None, ALU.subtract).then_inc(s_setup, 1)
                after(n + 3)
                nc.vector.scalar_tensor_tensor(ctmp, dst, 1.0, dst, ALU.mult, ALU.mult,
                                               accum_out=cst1[:, 0:1]).then_inc(s_setup, 1)
                after(n + 4)
                nc.vector.tensor_scalar(cst1[:, 2:3], cst1[:, 0:1], 1.0 / D, EPS, ALU.mult, ALU.add).then_inc(s_setup, 1)
                after(n + 6)
                nc.vector.tensor_scalar(dst, dst, cst1[:, 3:4], None, ALU.mult).then_inc(s_setup, 1)

            def class_token():
                cls_norm(11, crow, cxn)
                after(19)
                nc.vector.tensor_copy(ccol[0:64, 0:1], pa[0:64, 0, 0:1]).then_inc(s_setup, 1)
                after(21)
                nc.vector.tensor_copy(cqkv, pa[0:1, 0, 0:192])
                nc.vector.tensor_copy(ck.rearrange("p (e j) -> p e j", e=2),
                                      pa[0:1, 0, 64:128].rearrange("p (j e) -> p e j", e=2)).then_inc(s_setup, 1)
                after(22)
                nc.vector.scalar_tensor_tensor(ctmp, cqkv[:, 0:64], 1.0, cqkv[:, 64:128], ALU.mult, ALU.mult,
                                               accum_out=cst1[:, 4:5]).then_inc(s_setup, 1)
                after(24)
                nc.vector.tensor_scalar(P0[:, :], pa[:, 1, 0:64], GAMMA ** -128.0, None, ALU.mult)
                nc.vector.scalar_tensor_tensor(ch2, cqkv[:, 128:192], cst1[:, 4:5], crow,
                                               ALU.mult, ALU.add).then_inc(s_setup, 1)
                cls_norm(25, ch2, cxn2)
                after(33)
                nc.vector.tensor_copy(ccol[0:64, 1:2], pa[0:64, 0, 0:1])
                nc.vector.tensor_tensor(cbase, ch2, cxn2, ALU.add).then_inc(s_setup, 1)
                after(37)
                nc.vector.tensor_tensor(cy, pa[0:1, 0, 64:128], b2t[0:1, :], ALU.add)
                nc.vector.tensor_tensor(w_cls[:, :], pa[0:1, 1, 64:65], brt[0:1, :], ALU.add).then_inc(s_setup, 1)
                after(38)
                nc.vector.tensor_copy(wt[0:1, :, 0:1].rearrange("p u c -> p (u c)"),
                                      w_cls[:, :].broadcast_to([1, 2])).then_inc(s_setup, 1)
                after(39)

            def first_state(j):
                dve.wait_ge(s_o, at(j, NSLOT, 0))
                for u in range(2):
                    r = slice(64 * u, 64 * u + 64)
                    last = nc.vector.tensor_copy(P[r, PRING - 1, u, :], P0[r, :])
                last.then_inc(s_state, 1)

            def rotate(j, t):
                ring = t % 2
                dve.wait_ge(s_qkv, at(j, NSLOT, t + 1))
                dve.wait_ge(s_qk, at(j, NSLOT, t - 1))
                dve.wait_ge(s_y, at((j[0], j[1] - 1), NQ, NQ - 1 + t % 2))
                ch = slice(2 * t, 2 * t + 2)

                def halves(a, e):
                    return a.rearrange("p (f u e n) -> p f u e n", f=4, u=2, e=2)[:, :, :, e, :]

                def table(a, n):
                    return a[:, ch, :].rearrange("p c (f n) -> p (c f) n", f=2).unsqueeze(2).broadcast_to([128, 4, n, 32])

                nc.vector.tensor_tensor(t1[:, ring, :].rearrange("p (f g n) -> p f g n", f=4, g=4),
                                        pa[:, ring, :].rearrange("p (f g n) -> p f g n", f=4, g=4),
                                        table(cos_t, 4), ALU.mult)
                nc.vector.tensor_tensor(halves(t2[:, ring, :], 0), halves(pa[:, ring, :], 1),
                                        table(sin_t, 2), ALU.mult)
                nc.vector.tensor_tensor(halves(t2[:, ring, :], 1), halves(pa[:, ring, :], 0),
                                        table(sin_t, 2), ALU.mult).then_inc(s_rot, 1)

            def first():
                involution((0, 0))
                dve.wait_ge(s_load, N_SETUP_LOADS)
                block_diagonals()
                class_token()
                for q in (0, 1, 2):
                    ln_sum((0, 0), 0, q)
                ln_var((0, 0), 0, 0)
                centre((0, 0), 0, 2)
                ln_var((0, 0), 0, 1)
                ln_sum((0, 0), 0, 3)
                centre((0, 0), 0, 3)
                normalise((0, 0), 0, 0)
                ln_var((0, 0), 0, 2)
                normalise((0, 0), 0, 1)
                ln_var((0, 0), 0, 3)
                normalise((0, 0), 0, 2)
                normalise((0, 0), 0, 3)
                rotate((0, 0), 0)
                first_state((0, 0))
                rotate((0, 0), 1)

            def states(j, t):
                dve.wait_ge(s_u, at(j, NSLOT, t + 1))
                dve.wait_ge(s_o, at(j, NSLOT, t - 3))
                for c in range(2):
                    ch = 2 * t + c
                    dve.wait_ge(s_state, at(j, CH + 1, ch + 1))
                    for u in range(2):
                        r = slice(64 * u, 64 * u + 64)
                        last = nc.vector.scalar_tensor_tensor(P[r, ch % PRING, u, :], P[r, (ch - 1) % PRING, u, :],
                                                              GAMMA ** 128.0, ps[r, 3, 64 * c:64 * c + 64],
                                                              ALU.mult, ALU.add)
                    last.then_inc(s_state, 1)

            def mask_scores(j, t):
                dve.wait_ge(s_sc, at(j, NSLOT, t + 1))
                dve.wait_ge(s_o, at(j, NSLOT, t - 1))
                nc.vector.tensor_tensor(RT[:, t % 2, :, :, :],
                                        ps[:, 0:2, 0:256].rearrange("p u (c n) -> p u c n", c=2),
                                        const("cmask").unsqueeze(1).unsqueeze(1).broadcast_to([128, 2, 2, 128]),
                                        ALU.mult).then_inc(s_ret, 1)

            def add_residual(j, t):
                dve.wait_ge(s_o, at(j, NSLOT, t + 1))
                xs = X[:, :, 2 * t:2 * t + 2, :]
                nc.vector.tensor_tensor(xs, ps[:, 2, 0:256].rearrange("p (c u d) -> p u c d", u=2, c=2), xs,
                                        ALU.add).then_inc(s_h2, 1)

            def retention(j):
                for k in range(NSLOT + 3):
                    if 2 <= k < NSLOT:
                        rotate(j, k)
                    if 0 <= k - 1 < NSLOT:
                        states(j, k - 1)
                    if not is_last(j) and k == NSLOT + 1:
                        y3_mask((j[0], j[1] + 1), 1)
                    if 0 <= k - 2 < NSLOT:
                        mask_scores(j, k - 2)
                    if not is_last(j) and k >= NSLOT:
                        y3_mask((j[0], j[1] + 1), (0, 2, 3)[k - NSLOT])
                    if 0 <= k - 3 < NSLOT:
                        add_residual(j, k - 3)
                    if k >= 6 and k % 4 == 2 and (k < NSLOT or is_last(j)):
                        ln_sum(j, 1, k // 4 - 1)
                    if k >= 9 and k % 4 == 1 and (k < NSLOT or is_last(j)):
                        ln_var(j, 1, k // 4 - 2)
                if is_last(j):
                    centre(j, 1, 3)
                    ln_var(j, 1, 3)
                    normalise(j, 1, 3)
                    for q in range(LQ):
                        router_sum(j, q)

            def router_sum(j, q):
                dve.wait_ge(s_prod, at(j, LQ, q + 1))
                nc.vector.tensor_reduce(wt[:, :, 1 + CQ * q:1 + CQ * q + CQ], quarter(yraw, q),
                                        AX.X, ALU.add).then_inc(s_w, 1)

            chained = [0]

            def link(j, ins):
                chained[0] += 1
                ins.then_inc(s_chain, 1)
                dve.wait_ge(s_chain, at(j, NCHAIN, chained[0]))

            def router_keys(j):
                chained[0] = 0
                dve.wait_ge(s_w, at(j, LQ, LQ))
                link(j, nc.vector.tensor_scalar(wt[:, :, 1:COLS], wt[:, :, 1:COLS], brt[:, 0:1], None, ALU.add))
                bits = wt[:, :, :].bitcast(i32)
                k0, k1 = key[:, 0, :, :], key[:, 1, :, :]
                link(j, nc.vector.tensor_scalar(k0, bits, 31, -2 ** 31, ALU.arith_shift_right, ALU.bitwise_or))
                link(j, nc.vector.tensor_tensor(k1, k0, bits, ALU.bitwise_xor))
                link(j, nc.vector.tensor_scalar(k0.bitcast(u32), k1.bitcast(u32), 16, None, ALU.logical_shift_right))
                link(j, nc.vector.tensor_scalar(k1, k1, 65535, None, ALU.bitwise_and))
                valid = const("valid").rearrange("p (u c) -> p u c", u=2)
                link(j, nc.vector.scalar_tensor_tensor(hi[:, :, :], k0, 1.0, valid, ALU.add, ALU.mult))

            def bc():
                return cand[:, :].unsqueeze(2).broadcast_to([128, 2, COLS])

            def low_halves(j):
                link(j, nc.vector.tensor_tensor(cmp[:, :, :], hi[:, :, :], bc(), ALU.is_equal))
                link(j, nc.vector.tensor_tensor(cmp2[:, :, :], hi[:, :, :], bc(), ALU.is_gt))
                link(j, nc.vector.scalar_tensor_tensor(lo[:, :, :], key[:, 1, :, :], 1.0, cmp[:, :, :], ALU.add, ALU.mult))
                link(j, nc.vector.scalar_tensor_tensor(lo[:, :, :], cmp2[:, :, :], 70000.0, lo[:, :, :], ALU.mult, ALU.add))

            def next_thresholds(j, n):
                link(j, nc.vector.scalar_tensor_tensor(
                    thr[:, :, :], const("digits").rearrange("p (u k) -> p u k", k=3), float(4 ** (NDIG - 1 - n % NDIG)),
                    cand[:, :].unsqueeze(2).broadcast_to([128, 2, 3]), ALU.mult, ALU.add))

            def ask_digit(j, vals):
                shape = [128, 2, 3, COLS]
                link(j, nc.vector.tensor_tensor(cmp3, vals[:, :, :].unsqueeze(2).broadcast_to(shape),
                                                thr[:, :, :].unsqueeze(3).broadcast_to(shape), ALU.is_ge))
                with nc.allow_low_precision("counts up to COLS are exact in bfloat16"):
                    nc.vector.tensor_reduce(part[:, :, :], cmp3, AX.X, ALU.add).then_inc(s_cmp, 1)

            def take_digit(j, n):
                dve.wait_ge(s_cnt, at(j, NREQ, n + 1))
                link(j, nc.vector.tensor_scalar(dlt[:, :, :], counts(j, n), float(TOPK), None, ALU.is_ge))
                link(j, nc.vector.tensor_reduce(digit[:, :], dlt[:, :, :], AX.X, ALU.add))
                link(j, nc.vector.scalar_tensor_tensor(cand[:, :], digit[:, :], float(4 ** (NDIG - 1 - n % NDIG)),
                                                       cand[:, :], ALU.mult, ALU.add))

            def router_step(j, n):
                if 1 <= n <= 2 * NDIG:
                    take_digit(j, n - 1)
                if n == NDIG:
                    low_halves(j)
                if n in (0, NDIG):
                    link(j, nc.vector.memset(cand[:, :], 1.0))
                if n < 2 * NDIG:
                    next_thresholds(j, n)
                    ask_digit(j, hi if n < NDIG else lo)
                elif n == 2 * NDIG:
                    link(j, nc.vector.tensor_tensor(cmp[:, :, :], lo[:, :, :], bc(), ALU.is_gt))
                    with nc.allow_low_precision("counts up to COLS are exact in bfloat16"):
                        nc.vector.tensor_reduce(part[:, :, 0:1].rearrange("p u k -> p (u k)"), cmp[:, :, :],
                                                AX.X, ALU.add).then_inc(s_cmp, 1)
                else:
                    dve.wait_ge(s_cnt, at(j, NREQ, n))
                    above = counts(j, n - 1)[:, :, 0:1].rearrange("p u k -> p (u k)")
                    link(j, nc.vector.tensor_scalar(need[:, :], above, -1.0, float(TOPK), ALU.mult, ALU.add))
                    nc.vector.tensor_tensor(tie[:, :, :], lo[:, :, :], bc(), ALU.is_equal).then_inc(s_cmp, 1)

            def router_select(j):
                dve.wait_ge(s_cnt, at(j, NREQ, NREQ))
                inside, totals = pt[:, 64:64 + 2 * COLS], pt[:, 192:192 + 2 * COLS]
                for u in range(2):
                    link(j, nc.vector.tensor_tensor_scan(rank[:, u, :], const("ones")[:, 0:COLS],
                                                         totals[:, u * COLS:(u + 1) * COLS], 0.0, ALU.mult, ALU.add))
                flat = rank[:, :, :].rearrange("p u c -> p (u c)")
                link(j, nc.vector.tensor_tensor(flat, flat, totals, ALU.subtract))
                link(j, nc.vector.tensor_tensor(flat, flat, inside, ALU.add))
                link(j, nc.vector.tensor_tensor(rank[:, :, :], rank[:, :, :],
                                                need[:, :].unsqueeze(2).broadcast_to([128, 2, COLS]), ALU.is_lt))
                link(j, nc.vector.tensor_tensor(rank[:, :, :], rank[:, :, :], tie[:, :, :], ALU.mult))
                link(j, nc.vector.tensor_tensor(rank[:, :, :], rank[:, :, :], cmp[:, :, :], ALU.add))
                dve.wait_ge(s_out, at(j, NSTORED, 0))
                link(j, nc.vector.tensor_tensor(wsel[:, :, :], rank[:, :, :], wt[:, :, :], ALU.mult))
                cz = czz.rearrange("p (u d) -> p u d", u=2)
                link(j, nc.vector.tensor_tensor(cz, cy.unsqueeze(1).broadcast_to([1, 2, D]),
                                                wsel[0:1, :, 0:1].broadcast_to([1, 2, D]), ALU.mult))
                nc.vector.tensor_tensor(cz, cz, cbase.unsqueeze(1).broadcast_to([1, 2, D]), ALU.add).then_inc(s_cls, 1)
                assert chained[0] == NCHAIN, chained[0]

            def involution_and_router(j):
                jn = (j[0], j[1] - 1)
                for n in range(4, NCONV):
                    y3_mask(j, n)
                    if n == 4:
                        ln_var(jn, 1, 2)
                ln_sum(jn, 1, 3)
                for g in range(NG):
                    for u in range(2):
                        mask_taps(j, g, u)
                    if g == 0:
                        centre(jn, 1, 3)
                    if g == 3:
                        ln_var(jn, 1, 3)
                    if g in SUM_STRIPS:
                        router_sum(jn, SUM_STRIPS.index(g))
                    if g == FIRST_ASKING:
                        router_keys(jn)
                    if g >= FIRST_ASKING:
                        router_step(jn, g - FIRST_ASKING)
                router_step(jn, NEARLY)

            def ffn(j, more):
                nx = (j[0], j[1] + 1)
                sums = {NEARLY + 2 + q: q for q in range(LQ)}
                variances = {NEARLY + 5 + q: q for q in range(LQ)}
                if not more:
                    router_keys(j)
                for n in range(NEARLY + 1 if more else 0, NREQ):
                    router_step(j, n)
                    if more and n in sums:
                        ln_sum(nx, 0, sums[n])
                    if more and sums.get(n) == 3:
                        centre(nx, 0, 3)
                    if more and n in variances:
                        ln_var(nx, 0, variances[n])
                router_select(j)
                if more:
                    first_state(nx)
                for r in range(LR):
                    if more and r >= LR - 2:
                        rotate(nx, r - (LR - 2))
                    dve.wait_ge(s_yb, at(j, LR, r + 1))
                    nc.vector.tensor_tensor(piece(yraw, r), piece(yraw, r),
                                            wsel[:, :, 1 + CP * r:1 + CP * r + CP].unsqueeze(3).broadcast_to([128, 2, CP, D]),
                                            ALU.mult).then_inc(s_mul, 1)
                    dve.wait_ge(s_mul, at(j, LR, r + 1))
                    dve.wait_ge(s_base, at(j, LQ, r * LQ // LR + 1))
                    nc.vector.tensor_tensor(piece(yraw, r), piece(yraw, r), piece(base, r),
                                            ALU.add).then_inc(s_fin, 1)

            walk(dve, first, retention, involution_and_router, ffn)


        @block.tensor
        def _(pe):
            mm = nc.tensor.matmul

            def conv(j, n):
                pe.wait_ge(s_yraw, at(j, NCONV, n - 1))
                pe.wait_ge(s_rot, at(j, NSLOT, min(n, 1) - 1))
                pe.wait_ge(s_blk, at(j, 2, 1 + 2 * n // NCONV))
                r0 = 1 + n * ROWS_PER_CONV
                mm(pa[:, n % 2, :].rearrange("p (h b w) -> p b h w", b=WB, w=WS), w1_conv[:, :],
                   xblk[:, :, r0:r0 + ROWS_PER_CONV, 1:WS + 1], start=True, stop=True).then_inc(s_conv, 1)

            def count(j, n):
                pe.wait_ge(s_cmp, at(j, NREQ, n + 1))
                if n < NREQ - 1:
                    mm(counts(j, n), ones_b[:, :], part[:, :, :], start=True, stop=True).then_inc(s_cnt, 1)
                else:
                    ties = tie[:, :, :].rearrange("p u c -> p (u c)")
                    mm(pt[:, 64:64 + 2 * COLS], tri_b[:, :], ties, start=True, stop=True)
                    mm(pt[:, 192:192 + 2 * COLS], ones_b[:, :], ties, start=True, stop=True).then_inc(s_cnt, 1)

            def fill(j, kind, n, bank, ahead=0):
                pe.wait_ge(s_norm, at(j, NORMS, LQ * kind + n // (NFILL // LQ) + 1))
                pe.wait_ge(s_xte, at(j, 2 * NFILL, NFILL * kind + n - min(n, ahead)))
                for c in range(4):
                    last = nc.tensor.transpose(bank[:, 128 * c:128 * c + 128],
                                               xn[:, 4 * n + c, :, :].rearrange("p u d -> p (u d)"), const("ident"))
                last.then_inc(s_xt, 1)

            def involution(j):
                looped = not isinstance(j[0], int)
                jn = (j[0], j[1] - 1)
                for n in range(5 if looped else 0, NCONV):
                    conv(j, n)
                pe.wait_ge(s_gen_w, 1)
                pe.wait_ge(s_yraw, at(j, NCONV, NCONV))
                pe.wait_ge(s_h2, at(j, NSLOT, 0))
                pe.wait_ge(s_qkt, at(j, NSLOT, 0))
                pe.wait_ge(s_v, at(j, NSLOT, 0))
                pe.wait_ge(s_state, at(j, CH + 1, 0))
                for k in range(NG + 1):
                    if k < NG:
                        g, nh = k, rows(k)
                        K = (nh + 2) * PC
                        pe.wait_ge(s_patch, at(j, NG, g - 1))
                        for b in range(WB):
                            last = nc.tensor.transpose(p_patch[g % 2][0:K, 128 * b:128 * b + 128],
                                                       xblk[:, b, HS * g:HS * g + nh + 2, :].rearrange("p r s -> p (r s)"),
                                                       const("ident"))
                        last.then_inc(s_pt, 1)
                        pe.wait_ge(s_y3, at(j, NCONV, (HS * g + nh - 1) // ROWS_PER_CONV + 1))
                        for u in range(2):
                            pe.wait_ge(s_taps, at(j, 2 * NG, 2 * (g - 1) + u + 1))
                            dst = ps[0:K, u, 0:nh * W].rearrange("p (h w) -> p h w", w=W)
                            for rh in range(3):
                                last = mm(dst[:, rh:nh:3, :], gen_w[:, u, rh, 0:K],
                                          y3[:, HS * g + rh:HS * g + nh:3, :], start=True, stop=True)
                            last.then_inc(s_gen, 1)
                        if looped and k > FIRST_ASKING:
                            count(jn, k - 1 - FIRST_ASKING)
                        if looped and k >= NG - NFILL:
                            fill(jn, 1, k - NG + NFILL, pa[:, 1, :])
                    if k >= 1:
                        g, nh = k - 1, rows(k - 1)
                        K = (nh + 2) * PC
                        pe.wait_ge(s_patch, at(j, NG, g + 1))
                        pe.wait_ge(s_taps, at(j, 2 * NG, 2 * g + 2))
                        pe.wait_ge(s_strd, at(j, NG, g - 1))
                        for b in range(WB):
                            for u in range(2):
                                dst = ps[64 * u:64 * u + 64, 2 + g % 2, 0:nh * W].rearrange("p (h w) -> p h w", w=W)
                                last = mm(dst[:, :, WS * b:WS * b + WS], patch[0:K, g % 2, b, 64 * u:64 * u + 64],
                                          taps[0:K, g % 2, u, 0:nh, WS * b:WS * b + WS], start=True, stop=True)
                        last.then_inc(s_app, 1)

            def project(j, t, fills=NFILL):
                pe.wait_ge(s_yev, at((j[0], j[1] - 1), NQ, NQ - 1 + min(t, 1)))
                pe.wait_ge(s_xte, at(j, 2 * NFILL, fills))
                pe.wait_ge(s_rot, at(j, NSLOT, t - 1))
                pe.wait_ge(s_v, at(j, NSLOT, t))
                for c in range(2):
                    lhsT = xT[:, 2 * t + c, :]
                    mm(pa[:, t % 2, 256 * c:256 * c + 256], lhsT,
                       wqk_bd[:, :, :, :, :].rearrange("p a u e j -> p (a u e j)"), start=True, stop=True)
                    last = mm(pv[:, 128 * c:128 * c + 128], lhsT,
                              wv_bd[:, :, :].rearrange("p u d -> p (u d)"), start=True, stop=True)
                last.then_inc(s_qkv, 1)

            def retention(j):
                pe.wait_ge(s_gelu, at(j, NB * NQ, 0))
                pe.wait_ge(s_cls, at(j, 1, 0))
                pe.wait_ge(s_strd, at(j, NG, NG))
                pe.wait_ge(s_taps, at(j, 2 * NG, 2 * NG))
                pe.wait_ge(s_patch, at(j, NG, NG))
                pe.wait_ge(s_yraw, at(j, NCONV, NCONV))
                pe.wait_ge(s_xte, at(j, 2 * NFILL, NFILL))
                for k in range(NSLOT + 3):
                    if 2 <= k < NSLOT:
                        project(j, k)
                    if not is_last(j) and k >= NSLOT:
                        conv((j[0], j[1] + 1), 2 * (k - NSLOT))
                    if 0 <= k - 1 < NSLOT:
                        t = k - 1
                        pe.wait_ge(s_qk, at(j, NSLOT, t + 1))
                        pe.wait_ge(s_qkt, at(j, NSLOT, t))
                        src = qk[:, t % 2, :].rearrange("p (c a n) -> p c a n", c=2, a=2)
                        for c in range(2):
                            for a in range(2):
                                last = nc.tensor.transpose(pt[:, 128 * (2 * c + a):128 * (2 * c + a) + 128],
                                                           src[:, c, a, :], const("ident"))
                        last.then_inc(s_tr, 1)
                        pe.wait_ge(s_v, at(j, NSLOT, t + 1))
                        pe.wait_ge(s_state, at(j, CH + 1, 2 * t + 1))
                        for c in range(2):
                            for u in range(2):
                                last = mm(ps[64 * u:64 * u + 64, 3, 64 * c:64 * c + 64],
                                          src[:, c, 1, 64 * u:64 * u + 64],
                                          V[:, t % VRING, c, 64 * u:64 * u + 64], start=True, stop=True)
                        last.then_inc(s_u, 1)
                    if 0 <= k - 2 < NSLOT:
                        t = k - 2
                        pe.wait_ge(s_qkt, at(j, NSLOT, t + 1))
                        pe.wait_ge(s_ret, at(j, NSLOT, t))
                        for c in range(2):
                            for u in range(2):
                                r = slice(64 * u, 64 * u + 64)
                                last = mm(ps[:, u, 128 * c:128 * c + 128], QKT[r, t % QRING, c, 1, :],
                                          QKT[r, t % QRING, c, 0, :], start=True, stop=True)
                        last.then_inc(s_sc, 1)
                    if not is_last(j) and NSLOT <= k < NSLOT + 2:
                        conv((j[0], j[1] + 1), 2 * (k - NSLOT) + 1)
                    if 0 <= k - 3 < NSLOT:
                        t = k - 3
                        pe.wait_ge(s_ret, at(j, NSLOT, t + 1))
                        pe.wait_ge(s_state, at(j, CH + 1, 2 * t + 2))
                        pe.wait_ge(s_h2, at(j, NSLOT, t))
                        for c in range(2):
                            mm(ps[:, 2, 128 * c:128 * c + 128], QKT[:, t % QRING, c, 0, :],
                               P[:, (2 * t + c - 1) % PRING, :, :].rearrange("p u d -> p (u d)"),
                               start=True, stop=False)
                            for u in range(2):
                                last = mm(ps[:, 2, 128 * c + 64 * u:128 * c + 64 * u + 64], RT[:, t % 2, u, c, :],
                                          V[:, t % VRING, c, 64 * u:64 * u + 64], start=False, stop=(u == 1))
                        last.then_inc(s_o, 1)

            def ffn(j, more):
                pe.wait_ge(s_h2, at(j, NSLOT, NSLOT))
                pe.wait_ge(s_state, at(j, CH + 1, CH + 1))
                pe.wait_ge(s_qkt, at(j, NSLOT, NSLOT))
                if more:
                    nx = (j[0], j[1] + 1)
                    pe.wait_ge(s_taps, at(nx, 2 * NG, 2 * NG))
                    pe.wait_ge(s_yraw, at(nx, NCONV, NCONV))
                    pe.wait_ge(s_patch, at(nx, NG, NG))
                if not more:
                    for n in range(NFILL // 2):
                        fill(j, 1, n, pa[:, n % 2, :], ahead=1)
                asked = NEARLY - 1 if more else 0
                for k in range(NQ + 1):
                    if k < NQ:
                        pe.wait_ge(s_xte, at(j, 2 * NFILL, NFILL + k // 2 + 1))
                        if more and k == 1:
                            pe.wait_ge(s_strd, at(nx, NG, NG))
                        for m in range(NB):
                            pe.wait_ge(s_gelu, at(j, NB * NQ, NB * (k - 2) + (m | 1) + 1))
                            mm(ps[:, 2 * (k % 2) + m // 2, 256 * (m % 2):256 * (m % 2) + 256],
                               w1_bd[:, m, :, :].rearrange("p u h -> p (u h)"),
                               xT[:, 2 * k:2 * k + 2, :].rearrange("p c l -> p (c l)"),
                               start=True, stop=True).then_inc(s_hid, 1)
                            if m == 1 and (more or k >= LATE) and asked < NREQ:
                                count(j, asked)
                                asked += 1
                    if more and k >= NQ - NFILL and k < NQ:
                        fill(nx, 0, k - NQ + NFILL, pv[:, :])
                    if not more and k in LATE_FILLS:
                        fill(j, 1, LATE_FILLS[k], pv[:, :])
                    if more and k == NQ:
                        project(nx, 0)
                    if k == 1 and more:
                        pe.wait_ge(s_cmp, at(j, NREQ, NEARLY + 1))
                    if k == 1 and not more:
                        pe.wait_ge(s_xte, at(j, 2 * NFILL, NFILL + NFILL // 2))
                    if k >= 1:
                        q = k - 1
                        pe.wait_ge(s_gelu, at(j, NB * NQ, NB * q + NB))
                        pe.wait_ge(s_yev, at(j, NQ, q - 1))
                        for c in range(2):
                            if c and k >= (TWICE if more else LATE) and asked < NREQ:
                                count(j, asked)
                                asked += 1
                            for m in range(NB):
                                last = mm(pa[:, q % 2, 128 * c:128 * c + 128], hid[:, q % 2, m, 128 * c:128 * c + 128],
                                          w2_bd[:, m, :, :].rearrange("p u d -> p (u d)"),
                                          start=(m == 0), stop=(m == NB - 1))
                        last.then_inc(s_y, 1)
                if more:
                    project(nx, 1)
                for n in range(asked, NREQ):
                    count(j, n)

            pe.wait_ge(s_cload, N_CONV_LOADS)
            pe.wait_ge(s_setup, 1)
            mm(pa[0:27, 0, 0:128], const("rep", TAPS), c2rep[:, :], start=True, stop=True).then_inc(s_setup, 1)
            pe.wait_ge(s_setup, 3)
            mm(pa[:, 0, 0:5], const("spread", CR), bn5[:, :], start=True, stop=True)
            for u in range(2):
                mm(pa[64 * u:64 * u + 64, 1, 64 * u:64 * u + 64], c1w[:, :], const("spread", CR)[:, 0:64],
                   start=True, stop=True)
            n = PR * PC
            for rh in range(3):
                last = mm(pv[:, n * rh:n * rh + n], c2bd[:, :], const("sel", 27)[:, n * rh:n * rh + n],
                          start=True, stop=True)
            last.then_inc(s_setup, 1)
            pe.wait_ge(s_setup, 5)

            def class_token():
                pe.wait_ge(s_yraw, at((0, 0), NCONV, NCONV))
                pe.wait_ge(s_load, N_SETUP_LOADS)
                pe.wait_ge(s_setup, 18)
                nc.tensor.transpose(pa[0:64, 0, 0:1], cxn, const("ident", 1)[:, 0:1]).then_inc(s_setup, 1)
                pe.wait_ge(s_setup, 20)
                mm(pa[0:1, 0, 0:192], ccol[0:64, 0:1], wqkv[0:64, :, :].rearrange("p a d -> p (a d)"),
                   start=True, stop=True).then_inc(s_setup, 1)
                pe.wait_ge(s_setup, 23)
                for u in range(2):
                    last = mm(pa[64 * u:64 * u + 64, 1, 0:64], ck, cqkv[:, 128:192], start=True, stop=True)
                last.then_inc(s_setup, 1)
                pe.wait_ge(s_setup, 32)
                nc.tensor.transpose(pa[0:64, 0, 0:1], cxn2, const("ident", 1)[:, 0:1]).then_inc(s_setup, 1)
                pe.wait_ge(s_setup, 34)
                for m in range(NB):
                    mm(pa[:, 0, 4 + m:5 + m], w1_bd[:, m, :, :].rearrange("p u h -> p (u h)"), ccol[:, 1:2],
                       start=True, stop=True)
                mm(pa[0:1, 1, 64:65], ccol[0:64, 1:2], wrt[:, :], start=True, stop=True).then_inc(s_setup, 1)
                pe.wait_ge(s_setup, 36)
                for m in range(NB):
                    last = mm(pa[0:1, 0, 64:128], ccol[0:64, 2 + m:3 + m], w2_bd[0:64, m, 0, :],
                              start=(m == 0), stop=(m == NB - 1))
                last.then_inc(s_setup, 1)
                pe.wait_ge(s_setup, 39)
                pe.wait_ge(s_zero, 2)
                pe.wait_ge(s_tab, 32)

            def first():
                involution((0, 0))
                class_token()
                pe.wait_ge(s_strd, at((0, 0), NG, NG))
                for n in range(NFILL):
                    if n >= NFILL - 2:
                        project((0, 0), n - (NFILL - 2), fills=1)
                    fill((0, 0), 0, n, ps[:, n % 4, :], ahead=3)

            walk(pe, first, retention, involution, ffn)


_INS = ['x', 'cls_tok', 'L0_tok_conv1_w', 'L0_tok_conv1_b', 'L0_tok_bn_gamma', 'L0_tok_bn_beta', 'L0_tok_bn_mean',
        'L0_tok_bn_var', 'L0_tok_conv2_w', 'L0_tok_conv2_b', 'L0_attn_W_Q', 'L0_attn_W_K', 'L0_attn_W_V',
        'L0_ffn_wr', 'L0_ffn_br', 'L0_ffn_w1', 'L0_ffn_b1', 'L0_ffn_w2', 'L0_ffn_b2']


def kernel(**inputs):
    import numpy as _np
    import concourse.bacc as _bacc
    from concourse import mybir as _mybir
    from concourse.bass_utils import run_bass_kernel_spmd as _run

    nc = _bacc.Bacc("TRN2", target_bir_lowering=False, num_devices=1)
    arrays, args = {}, []
    feeds = [(name, _np.ascontiguousarray(inputs[name])) for name in _INS]
    feeds += [("small_constants", small_constants()), ("position_tables", position_tables())]
    for name, a in feeds:
        arrays[f"in_{name}_dram"] = a
        args.append(nc.dram_tensor(f"in_{name}_dram", a.shape, _mybir.dt.from_np(a.dtype), kind="ExternalInput").ap())
    args.append(nc.dram_tensor("out_0_dram", (B, SEQ, D), _mybir.dt.float32, kind="ExternalOutput").ap())
    vit_tower(nc, *args)
    r = _run(nc, [arrays], core_ids=[0])
    return r.results[0]["out_0_dram"]
```
